# Optimizing a Trainium2 kernel written in Bass

```python
import numpy as np
import jax
import jax.numpy as jnp

def _softmax(x, axis=-1):
    return jax.nn.softmax(x, axis=axis)

def _gelu(x):
    return jax.nn.gelu(x, approximate=True)

def _silu(x):
    return jax.nn.silu(x)

def _sigmoid(x):
    return jax.nn.sigmoid(x)

def _layernorm(x, axis=-1, eps=1e-05):
    m = jnp.mean(x, axis=axis, keepdims=True)
    v = jnp.var(x, axis=axis, keepdims=True)
    return (x - m) / jnp.sqrt(v + eps)

def _scatter_add(tgt, idx, src, axis=0):
    return tgt.at[idx].add(src)

def _segment_sum(src, seg, n):
    return jax.ops.segment_sum(src, seg, n)
kernel_name = 'mk_lm_tower_d1_tok_ids256_r4_2d59cb'

def setup_inputs(seed: int=0):
    np.random.seed(seed)
    _w = jnp.asarray

    def _rec_inputs():
        import jax
        import jax.numpy as jnp
        _rk = jax.random.key(seed)
        x = jax.random.randint(jax.random.fold_in(_rk, 1), (8, 1024), 0, 12564, jnp.int32)
        return x
    x = _rec_inputs()

    def _L0_tok_setup():
        import jax, jax.numpy as jnp
        import numpy as np
        VOCAB, N_TURNS, OUT_DIM, POLY_DEG = (50257, 4, 64, 4)
        key = jax.random.key(seed)
        k1, k2, k3 = jax.random.split(key, 3)
        token_ids = jax.random.randint(k1, (16, 1024), 0, VOCAB)
        turns = jax.random.normal(k2, (VOCAB, N_TURNS), dtype=jnp.float32) * 3.0
        poly_coeffs = jax.random.normal(k3, (N_TURNS, POLY_DEG + 1, OUT_DIM), dtype=jnp.float32) * 0.01
        return {'token_ids': token_ids, 'turns': turns, 'poly_coeffs': poly_coeffs}
    _L0_tok_all = _L0_tok_setup()
    _L0_tok_in = {k: v for k, v in _L0_tok_all.items() if k in ('turns', 'poly_coeffs')}
    del _L0_tok_all

    def _L0_attn_setup():
        import jax, jax.numpy as jnp
        import numpy as np
        import math
        D_MODEL = 64
        NHEAD = 8
        D_LATTICE = 512
        D_K = D_LATTICE // NHEAD
        PHI = (1.0 + math.sqrt(5.0)) / 2.0
        PHI_INV = 1.0 / PHI
        PHI_INT = 1618.0
        C1 = PHI * math.sqrt(2.0) * 51.85
        C2 = math.pi / PHI

        def qrt_damping(x):
            return jnp.sin(C1 * x) * jnp.exp(-(x * x) / PHI) + jnp.cos(C2 * x)

        def ttt_filter(scores):
            int_scores = (jnp.abs(scores) * PHI_INT).astype(jnp.int32)
            mod9 = int_scores % 9
            chaos = (mod9 == 0) | (mod9 == 3) | (mod9 == 6)
            penalty = jnp.where(chaos, jnp.float32(PHI_INV), jnp.float32(1.0))
            return scores * penalty
        key = jax.random.key(seed)
        ks = jax.random.split(key, 9)
        B, S = (2, 512)
        s_in = 1.0 / math.sqrt(D_MODEL)
        s_lat = 1.0 / math.sqrt(D_LATTICE)
        return {'x': jax.random.normal(ks[0], (B, S, D_MODEL), dtype=jnp.float32), 'Wq': jax.random.normal(ks[1], (D_MODEL, D_LATTICE), dtype=jnp.float32) * s_in, 'bq': jax.random.normal(ks[2], (D_LATTICE,), dtype=jnp.float32) * 0.01, 'Wk': jax.random.normal(ks[3], (D_MODEL, D_LATTICE), dtype=jnp.float32) * s_in, 'bk': jax.random.normal(ks[4], (D_LATTICE,), dtype=jnp.float32) * 0.01, 'Wv': jax.random.normal(ks[5], (D_MODEL, D_LATTICE), dtype=jnp.float32) * s_in, 'bv': jax.random.normal(ks[6], (D_LATTICE,), dtype=jnp.float32) * 0.01, 'Wo': jax.random.normal(ks[7], (D_LATTICE, D_MODEL), dtype=jnp.float32) * s_lat, 'bo': jax.random.normal(ks[8], (D_MODEL,), dtype=jnp.float32) * 0.01}
    _L0_attn_all = _L0_attn_setup()
    _L0_attn_in = {k: v for k, v in _L0_attn_all.items() if k in ('Wq', 'bq', 'Wk', 'bk', 'Wv', 'bv', 'Wo', 'bo')}
    del _L0_attn_all

    def _L0_ffn_setup():
        import jax, jax.numpy as jnp
        import numpy as np
        B, T, C = (64, 96, 64)
        NH, NKV = (4, 2)
        HD = C // NH
        NREP = NH // NKV
        NE, TOPK = (8, 2)
        HID = int(8 / 3 * C)
        EPS_RMS = 1e-06

        def _rope_tables(t_len):
            inv_freq = 1.0 / 10000.0 ** (np.arange(0, HD, 2, dtype=np.float32) / HD)
            t = np.arange(t_len, dtype=np.float32)
            freqs = np.outer(t, inv_freq)
            emb = np.concatenate([freqs, freqs], axis=-1)
            return (jnp.asarray(np.cos(emb)), jnp.asarray(np.sin(emb)))

        def _rotate_half(x):
            h = x.shape[-1] // 2
            return jnp.concatenate([-x[..., h:], x[..., :h]], axis=-1)

        def _rmsnorm(v, w):
            return v * jax.lax.rsqrt(jnp.mean(v * v, axis=-1, keepdims=True) + EPS_RMS) * w
        key = jax.random.key(seed)
        ks = jax.random.split(key, 10)
        s = lambda k, shape: jax.random.normal(k, shape, jnp.float32) * 0.02
        return {'x': jax.random.normal(ks[0], (B, T, C), jnp.float32), 'ln1_w': jnp.ones((C,), jnp.float32), 'ln2_w': jnp.ones((C,), jnp.float32), 'wq': s(ks[1], (NH * HD, C)), 'wk': s(ks[2], (NKV * HD, C)), 'wv': s(ks[3], (NKV * HD, C)), 'wo': s(ks[4], (C, C)), 'router_w': s(ks[5], (NE, C)), 'w1': s(ks[6], (NE, HID, C)), 'w2': s(ks[7], (NE, C, HID)), 'w3': s(ks[8], (NE, HID, C))}
    _L0_ffn_all = _L0_ffn_setup()
    _L0_ffn_in = {k: v for k, v in _L0_ffn_all.items() if k in ('ln1_w', 'ln2_w', 'wq', 'wk', 'wv', 'wo', 'router_w', 'w1', 'w2', 'w3')}
    del _L0_ffn_all
    return {'x': x, 'L0_tok_turns': _L0_tok_in['turns'], 'L0_tok_poly_coeffs': _L0_tok_in['poly_coeffs'], 'L0_attn_Wq': _L0_attn_in['Wq'], 'L0_attn_bq': _L0_attn_in['bq'], 'L0_attn_Wk': _L0_attn_in['Wk'], 'L0_attn_bk': _L0_attn_in['bk'], 'L0_attn_Wv': _L0_attn_in['Wv'], 'L0_attn_bv': _L0_attn_in['bv'], 'L0_attn_Wo': _L0_attn_in['Wo'], 'L0_attn_bo': _L0_attn_in['bo'], 'L0_ffn_ln1_w': _L0_ffn_in['ln1_w'], 'L0_ffn_ln2_w': _L0_ffn_in['ln2_w'], 'L0_ffn_wq': _L0_ffn_in['wq'], 'L0_ffn_wk': _L0_ffn_in['wk'], 'L0_ffn_wv': _L0_ffn_in['wv'], 'L0_ffn_wo': _L0_ffn_in['wo'], 'L0_ffn_router_w': _L0_ffn_in['router_w'], 'L0_ffn_w1': _L0_ffn_in['w1'], 'L0_ffn_w2': _L0_ffn_in['w2'], 'L0_ffn_w3': _L0_ffn_in['w3']}

def reference(x, L0_tok_turns, L0_tok_poly_coeffs, L0_attn_Wq, L0_attn_bq, L0_attn_Wk, L0_attn_bk, L0_attn_Wv, L0_attn_bv, L0_attn_Wo, L0_attn_bo, L0_ffn_ln1_w, L0_ffn_ln2_w, L0_ffn_wq, L0_ffn_wk, L0_ffn_wv, L0_ffn_wo, L0_ffn_router_w, L0_ffn_w1, L0_ffn_w2, L0_ffn_w3):
    import jax
    import jax.numpy as jnp

    def _L0_tok_ref(token_ids, turns, poly_coeffs):
        import jax, jax.numpy as jnp
        import numpy as np
        VOCAB, N_TURNS, OUT_DIM, POLY_DEG = (50257, 4, 64, 4)
        base_turns = turns[token_ids]
        x = jax.lax.stop_gradient(jnp.trunc(base_turns)).astype(jnp.float32)
        degs = jnp.arange(POLY_DEG + 1, dtype=jnp.float32)
        xp = x[..., None] ** degs
        emb = jnp.einsum('bstd,tdo->bso', xp, poly_coeffs)
        return emb

    def _L0_attn_ref(x, Wq, bq, Wk, bk, Wv, bv, Wo, bo):
        import jax, jax.numpy as jnp
        import numpy as np
        import math
        D_MODEL = 64
        NHEAD = 8
        D_LATTICE = 512
        D_K = D_LATTICE // NHEAD
        PHI = (1.0 + math.sqrt(5.0)) / 2.0
        PHI_INV = 1.0 / PHI
        PHI_INT = 1618.0
        C1 = PHI * math.sqrt(2.0) * 51.85
        C2 = math.pi / PHI

        def qrt_damping(x):
            return jnp.sin(C1 * x) * jnp.exp(-(x * x) / PHI) + jnp.cos(C2 * x)

        def ttt_filter(scores):
            int_scores = (jnp.abs(scores) * PHI_INT).astype(jnp.int32)
            mod9 = int_scores % 9
            chaos = (mod9 == 0) | (mod9 == 3) | (mod9 == 6)
            penalty = jnp.where(chaos, jnp.float32(PHI_INV), jnp.float32(1.0))
            return scores * penalty
        B, S, _ = x.shape

        def split_heads(t):
            return t.reshape(B, S, NHEAD, D_K).transpose(0, 2, 1, 3)
        q = split_heads(x @ Wq + bq)
        k = split_heads(x @ Wk + bk)
        v = split_heads(x @ Wv + bv)
        scores = jnp.einsum('bhqd,bhkd->bhqk', q, k) / jnp.float32(math.sqrt(D_K))
        scores = ttt_filter(scores)
        attn = jax.nn.softmax(scores, axis=-1)
        attn = attn * qrt_damping(attn)
        ctx = jnp.einsum('bhqk,bhkd->bhqd', attn, v)
        ctx = ctx.transpose(0, 2, 1, 3).reshape(B, S, D_LATTICE)
        return ctx @ Wo + bo

    def _L0_ffn_ref(x, ln1_w, ln2_w, wq, wk, wv, wo, router_w, w1, w2, w3):
        import jax, jax.numpy as jnp
        import numpy as np
        B, T, C = (64, 96, 64)
        NH, NKV = (4, 2)
        HD = C // NH
        NREP = NH // NKV
        NE, TOPK = (8, 2)
        HID = int(8 / 3 * C)
        EPS_RMS = 1e-06

        def _rope_tables(t_len):
            inv_freq = 1.0 / 10000.0 ** (np.arange(0, HD, 2, dtype=np.float32) / HD)
            t = np.arange(t_len, dtype=np.float32)
            freqs = np.outer(t, inv_freq)
            emb = np.concatenate([freqs, freqs], axis=-1)
            return (jnp.asarray(np.cos(emb)), jnp.asarray(np.sin(emb)))

        def _rotate_half(x):
            h = x.shape[-1] // 2
            return jnp.concatenate([-x[..., h:], x[..., :h]], axis=-1)

        def _rmsnorm(v, w):
            return v * jax.lax.rsqrt(jnp.mean(v * v, axis=-1, keepdims=True) + EPS_RMS) * w
        Bx, Tx, Cx = x.shape
        h = _rmsnorm(x, ln1_w)
        q = (h @ wq.T).reshape(Bx, Tx, NH, HD).transpose(0, 2, 1, 3)
        k = (h @ wk.T).reshape(Bx, Tx, NKV, HD).transpose(0, 2, 1, 3)
        v = (h @ wv.T).reshape(Bx, Tx, NKV, HD).transpose(0, 2, 1, 3)
        cos, sin = _rope_tables(Tx)
        cos, sin = (cos[None, None], sin[None, None])
        q = q * cos + _rotate_half(q) * sin
        k = k * cos + _rotate_half(k) * sin
        k = jnp.repeat(k, NREP, axis=1)
        v = jnp.repeat(v, NREP, axis=1)
        scores = jnp.einsum('bhtd,bhsd->bhts', q, k) / jnp.sqrt(jnp.float32(HD))
        causal = jnp.tril(jnp.ones((Tx, Tx), dtype=bool))
        scores = jnp.where(causal[None, None], scores, jnp.float32(-1e+30))
        att = jax.nn.softmax(scores, axis=-1)
        y = jnp.einsum('bhts,bhsd->bhtd', att, v).transpose(0, 2, 1, 3).reshape(Bx, Tx, Cx)
        x = x + y @ wo.T
        flat = _rmsnorm(x, ln2_w).reshape(-1, Cx)
        probs = jax.nn.softmax(flat @ router_w.T, axis=-1)
        tp, ti = jax.lax.top_k(probs, TOPK)
        tp = tp / (jnp.sum(tp, axis=-1, keepdims=True) + 1e-09)
        weights = jnp.sum(tp[..., None] * jax.nn.one_hot(ti, NE, dtype=flat.dtype), axis=1)
        out = jnp.zeros_like(flat)
        for e in range(NE):
            hh = jax.nn.silu(flat @ w1[e].T) * (flat @ w3[e].T)
            out = out + weights[:, e:e + 1] * (hh @ w2[e].T)
        return x + out.reshape(Bx, Tx, Cx)
    h = _L0_tok_ref(x, L0_tok_turns, L0_tok_poly_coeffs)
    h = h + _L0_attn_ref(_layernorm(h, axis=-1), L0_attn_Wq, L0_attn_bq, L0_attn_Wk, L0_attn_bk, L0_attn_Wv, L0_attn_bv, L0_attn_Wo, L0_attn_bo)
    h = h + _L0_ffn_ref(_layernorm(h, axis=-1), L0_ffn_ln1_w, L0_ffn_ln2_w, L0_ffn_wq, L0_ffn_wk, L0_ffn_wv, L0_ffn_wo, L0_ffn_router_w, L0_ffn_w1, L0_ffn_w2, L0_ffn_w3)
    return h

_drawn_inputs = setup_inputs


def setup_inputs(seed=0):
    import zlib

    import numpy as np

    out = dict(_drawn_inputs(seed))
    spreads = {'L0_ffn_ln1_w': (1.0, 0.6), 'L0_ffn_ln2_w': (1.0, 0.6)}
    factors = {'L0_attn_bq': 8.0,
     'L0_attn_bk': 123.264,
     'L0_attn_bv': 8.0,
     'L0_attn_bo': 8.0,
     'L0_ffn_wq': 8.0,
     'L0_ffn_wk': 8.0,
     'L0_ffn_wv': 8.0,
     'L0_ffn_wo': 8.0,
     'L0_ffn_router_w': 8.0,
     'L0_ffn_w1': 8.0,
     'L0_ffn_w2': 8.0,
     'L0_ffn_w3': 8.0}
    for name, (base, spread) in spreads.items():
        noise = np.random.default_rng([zlib.crc32(name.encode()), seed]).standard_normal(out[name].shape)
        drawn = base * np.exp(spread * noise) if base else spread * noise
        out[name] = jnp.asarray(drawn.astype(out[name].dtype))
    for name, factor in factors.items():
        out[name] = (out[name] * factor).astype(out[name].dtype)
    return out
```

```python
import math
from contextlib import ExitStack

import concourse.bass as bass
from concourse import mybir

ALU = mybir.AluOpType
ACT = mybir.ActivationFunctionType
AX = mybir.AxisListType.X
F32 = mybir.dt.float32
BF16 = mybir.dt.bfloat16
I32 = mybir.dt.int32

P = 128
B, S, D = 8, 1024, 64
NT = B * S // P
TB = S // P
VOCAB, TURNS, DEGS = 50257, 4, 5
H = 8
NHEADS = B * H
PHI = (1.0 + math.sqrt(5.0)) / 2.0
C1 = PHI * math.sqrt(2.0) * 51.85
C2 = math.pi / PHI
ROUND = 1.5 * 2.0 ** 23
QSCALE = 1618.0 / (8.0 * 3.0)
EXPSCALE = 3.0 / (1618.0 * PHI * PHI)
TURN = C1 / (2.0 * math.pi)
EPS = 1e-5


def embed(nc, ident, hres, xT_dram, wvo, ids, turns, coeffs, Wv, bv, Wo, bo):
    with ExitStack() as ctx:
        def sb(name, shape, dt=F32):
            return ctx.enter_context(nc.sbuf_tensor(name, shape, dt))

        def sem(name):
            return ctx.enter_context(nc.semaphore(name))

        ids_i = sb("ids_i", [NT, P], I32)
        ids_f = sb("ids_f", [NT, P])
        idx = sb("idx", [P, NT], I32)
        base = sb("base", [P, NT, TURNS])
        mag = sb("mag", [P, NT, TURNS])
        sgn = sb("sgn", [P, NT, TURNS])
        rnd = sb("rnd", [P, NT, TURNS])
        over = sb("over", [P, NT, TURNS])
        pw = sb("pw", [P, NT, 32])
        pwT = sb("pwT", [P, 2, P])
        coef4 = sb("coef4", [P, 4 * D])
        wv1 = sb("wv1", [D + 1, H * D])
        wvT = sb("wvT", [D, H, D + 1])
        wo_h = sb("wo_h", [D, H, D])
        bo_all = sb("bo_all", [P, D])
        cen = sb("cen", [P, NT, D])
        sq = sb("sq", [P, NT, D])
        s1 = sb("s1", [P, NT])
        mean = sb("mean", [P, NT])
        s2 = sb("s2", [P, NT])
        var = sb("var", [P, NT])
        std = sb("std", [P, NT])
        rstd = sb("rstd", [P, NT])
        xn = sb("xn", [P, 2, TB, D])
        xT = sb("xT", [D, 2, S])

        ps_a = ctx.enter_context(nc.psum_tensor("ps_a", [P, 2, 512], F32))
        ps_e = ctx.enter_context(nc.psum_tensor("ps_e", [P, 2, 512], F32))
        ps_x = ctx.enter_context(nc.psum_tensor("ps_x", [P, 2, 1024], F32))

        ids_in, w_in, coef_in = sem("ids_in"), sem("w_in"), sem("coef_in")
        zeroed = sem("zeroed")
        idf, idT, idx_ok, got = sem("idf"), sem("idT"), sem("idx_ok"), sem("got")
        magn, trunc, pows = sem("magn"), sem("trunc"), sem("pows")
        pT, pT_sb, emb, emb_sb = sem("pT"), sem("pT_sb"), sem("emb"), sem("emb_sb")
        wT, wT_sb, wm, wm_sb = sem("wT"), sem("wT_sb"), sem("wm"), sem("wm_sb")
        ln, sqd, rooted, normed, nT, nT_sb = (sem(n) for n in
            ("ln", "sqd", "rooted", "normed", "nT", "nT_sb"))
        nT_out = [sem("nT_out0"), sem("nT_out1")]

        block = ctx.enter_context(nc.Block())

        @block.sync
        def _(sp):
            sp.dma_start(ids_i[:], ids.rearrange("b (t p) -> (b t) p", p=P)).then_inc(ids_in, 16)
            sp.dma_start(wv1[0:D, :], Wv).then_inc(w_in, 16)
            sp.dma_start(wv1[D:D + 1, :], bv.rearrange("(a n) -> a n", a=1)).then_inc(w_in, 16)
            sp.dma_start(wo_h[:], Wo.rearrange("(h d) o -> d h o", d=D)).then_inc(w_in, 16)
            sp.dma_start(bo_all[:], bo.partition_broadcast(P)).then_inc(w_in, 16)
            sp.wait_ge(zeroed, 2)
            for j in range(4):
                sp.dma_start(coef4[32 * j:32 * j + TURNS * DEGS, j * D:(j + 1) * D],
                             coeffs.rearrange("t d o -> (t d) o")).then_inc(coef_in, 16)
            for b in range(B):
                sp.wait_ge(nT_sb, b + 1)
                sp.dma_start(xT_dram[:, b * S:(b + 1) * S], xT[:, b % 2, :]).then_inc(nT_out[b % 2], 16)
            for n in nT_out:
                sp.wait_ge(n, 16 * B // 2)

        @block.gpsimd
        def _(pool):
            nc.gpsimd.memset(coef4[:], 0.0).then_inc(zeroed, 1)
            nc.gpsimd.memset(pw[:], 0.0).then_inc(zeroed, 1)
            pool.wait_ge(idx_ok, 1)
            for t in range(NT):
                nc.gpsimd.indirect_dma_start(
                    out=base[:, t, :], out_offset=None, in_=turns[:, :],
                    in_offset=bass.IndirectOffsetOnAxis(ap=idx[:, t:t + 1], axis=0)).then_inc(got, 16)

        @block.scalar
        def _(act):
            act.wait_ge(got, 16 * NT)
            nc.scalar.activation(mag[:], base[:], ACT.Abs).then_inc(magn, 1)
            nc.scalar.activation(sgn[:], base[:], ACT.Sign).then_inc(magn, 1)
            for g in range(NT // 4):
                act.wait_ge(pT, g + 1)
                if g >= 2:
                    act.wait_ge(emb, g - 1)
                nc.scalar.activation(pwT[:, g % 2, :], ps_a[:, g % 2, 0:P], ACT.Copy).then_inc(pT_sb, 1)
            act.wait_ge(wT, 1)
            nc.scalar.activation(wvT[:, 0:4, :], ps_x[0:D, 0, 0:4 * (D + 1)].rearrange("p (h c) -> p h c", h=4),
                                 ACT.Copy).then_inc(wT_sb, 1)
            nc.scalar.activation(wvT[:, 4:8, :], ps_x[0:D, 1, 0:4 * (D + 1)].rearrange("p (h c) -> p h c", h=4),
                                 ACT.Copy).then_inc(wT_sb, 1)
            act.wait_ge(wm, 1)
            nc.scalar.activation(wvo[:], ps_a[0:D + 1, 0, :], ACT.Copy).then_inc(wm_sb, 1)
            act.wait_ge(ln, 3)
            nc.scalar.activation(sq[:], cen[:], ACT.Square).then_inc(sqd, 1)
            act.wait_ge(ln, 5)
            nc.scalar.activation(std[:], var[:], ACT.Sqrt).then_inc(rooted, 1)
            for b in range(B):
                act.wait_ge(nT, b + 1)
                if b >= 2:
                    act.wait_ge(nT_out[b % 2], 16 * (b // 2))
                nc.scalar.activation(xT[:, b % 2, :], ps_x[0:D, b % 2, :], ACT.Copy).then_inc(nT_sb, 1)

        @block.vector
        def _(dve):
            dve.wait_ge(ids_in, 16)
            nc.vector.tensor_copy(ids_f[:], ids_i[:]).then_inc(idf, 1)
            dve.wait_ge(idT, 1)
            nc.vector.tensor_copy(idx[:], ps_a[:, 0, 0:NT]).then_inc(idx_ok, 1)
            dve.wait_ge(magn, 2)
            nc.vector.tensor_scalar(rnd[:], mag[:], ROUND, -ROUND, ALU.add, ALU.add).then_inc(trunc, 1)
            dve.wait_ge(trunc, 1)
            nc.vector.tensor_tensor(over[:], rnd[:], mag[:], ALU.is_gt).then_inc(trunc, 1)
            dve.wait_ge(trunc, 2)
            nc.vector.tensor_tensor(rnd[:], rnd[:], over[:], ALU.subtract).then_inc(trunc, 1)
            dve.wait_ge(trunc, 3)
            dve.wait_ge(zeroed, 2)
            pv = pw[:, :, 0:TURNS * DEGS].rearrange("p n (t d) -> p n t d", d=DEGS)
            nc.vector.memset(pv[:, :, :, 0], 1.0).then_inc(pows, 1)
            nc.vector.tensor_tensor(pv[:, :, :, 1], rnd[:], sgn[:], ALU.mult).then_inc(pows, 1)
            dve.wait_ge(pows, 2)
            for d in range(2, DEGS):
                nc.vector.tensor_tensor(pv[:, :, :, d], pv[:, :, :, d - 1], pv[:, :, :, 1], ALU.mult).then_inc(pows, 1)
                dve.wait_ge(pows, d + 1)
            for e in range(NT // 8):
                dve.wait_ge(emb, 2 * e + 2)
                nc.vector.tensor_copy(hres[:, 8 * e:8 * e + 8, :],
                                      ps_e[:, e % 2, :].rearrange("p (t d) -> p t d", d=D)).then_inc(emb_sb, 1)
            dve.wait_ge(emb_sb, NT // 8)
            nc.vector.tensor_reduce(s1[:], hres[:], AX, ALU.add).then_inc(ln, 1)
            dve.wait_ge(ln, 1)
            nc.vector.tensor_scalar(mean[:], s1[:], 1.0 / D, None, ALU.mult).then_inc(ln, 1)
            dve.wait_ge(ln, 2)
            nc.vector.tensor_tensor(cen[:], hres[:], mean[:].unsqueeze(2).to_broadcast([P, NT, D]),
                                    ALU.subtract).then_inc(ln, 1)
            dve.wait_ge(w_in, 64)
            nc.vector.tensor_tensor(hres[:], hres[:], bo_all[:].unsqueeze(1).to_broadcast([P, NT, D]),
                                    ALU.add)
            dve.wait_ge(sqd, 1)
            nc.vector.tensor_reduce(s2[:], sq[:], AX, ALU.add).then_inc(ln, 1)
            dve.wait_ge(ln, 4)
            nc.vector.tensor_scalar(var[:], s2[:], 1.0 / D, EPS, ALU.mult, ALU.add).then_inc(ln, 1)
            dve.wait_ge(rooted, 1)
            nc.vector.reciprocal(rstd[:], std[:]).then_inc(ln, 1)
            dve.wait_ge(ln, 6)
            for b in range(B):
                if b >= 2:
                    dve.wait_ge(nT, b - 1)
                nc.vector.tensor_tensor(xn[:, b % 2], cen[:, TB * b:TB * b + TB, :],
                                        rstd[:, TB * b:TB * b + TB].unsqueeze(2).to_broadcast([P, TB, D]),
                                        ALU.mult).then_inc(normed, 1)

        @block.tensor
        def _(pe):
            pe.wait_ge(idf, 1)
            nc.tensor.transpose(ps_a[:, 0, 0:NT], ids_f[:], ident[0:NT, 0:NT]).then_inc(idT, 1)
            pe.wait_ge(w_in, 64)
            for h in range(H):
                mm = nc.tensor.transpose(ps_x[0:D, h // 4, (h % 4) * (D + 1):(h % 4 + 1) * (D + 1)],
                                         wv1[:, h * D:(h + 1) * D], ident[0:D + 1, 0:D + 1])
            mm.then_inc(wT, 1)
            pe.wait_ge(coef_in, 64)
            pe.wait_ge(pows, DEGS)
            pe.wait_ge(idx_ok, 1)
            for g in range(NT // 4):
                if g >= 2:
                    pe.wait_ge(pT_sb, g - 1)
                nc.tensor.transpose(ps_a[:, g % 2, 0:P], pw[:, 4 * g:4 * g + 4, :].rearrange("p t c -> p (t c)"),
                                    ident[:]).then_inc(pT, 1)
                pe.wait_ge(pT_sb, g + 1)
                if g >= 4:
                    pe.wait_ge(emb_sb, g // 2 - 1)
                o = (g % 2) * 4 * D
                nc.tensor.matmul(ps_e[:, (g // 2) % 2, o:o + 4 * D], pwT[:, g % 2, :], coef4[:],
                                 start=True, stop=True).then_inc(emb, 1)
            pe.wait_ge(wT_sb, 2)
            for h in range(H):
                mm = nc.tensor.matmul(ps_a[0:D + 1, 0, h * D:(h + 1) * D], wvT[:, h, :], wo_h[:, h, :],
                                      start=True, stop=True)
            mm.then_inc(wm, 1)
            for b in range(B):
                pe.wait_ge(normed, b + 1)
                if b >= 2:
                    pe.wait_ge(nT_sb, b - 1)
                for t in range(TB):
                    mm = nc.tensor.transpose(ps_x[0:D, b % 2, t * P:(t + 1) * P], xn[:, b % 2, t, :], ident[:])
                mm.then_inc(nT, 1)


def lattice(nc, ident, hres, xT_dram, wvo, Wq, bq, Wk, bk):
    with ExitStack() as ctx:
        def sb(name, shape, dt=F32):
            return ctx.enter_context(nc.sbuf_tensor(name, shape, dt))

        def sem(name):
            return ctx.enter_context(nc.semaphore(name))

        xb = sb("xb", [D + 1, S])
        wqk = sb("wqk", [D + 1, P])
        qT = sb("qT", [D, S])
        kT = sb("kT", [D, S])
        vo = sb("vo", [P, 2, TB, D])
        mag = sb("mag2", [P, 2, S])
        wgt = sb("wgt", [P, 2, S])
        att = sb("att", [P, 2, TB, S])
        nturn = sb("nturn", [P, TB, S], BF16)
        ag = sb("ag", [P, TB, S])
        gau = sb("gau", [P, 3, 512])
        cosb = sb("cosb", [P, 4, 512])
        sinb = sb("sinb", [P, 4, 512])
        mx = sb("mx", [P, 2, TB])
        nb = sb("nb", [P, 2, TB])
        ssum = sb("ssum", [P, TB])
        rs = sb("rs", [P, TB])
        negI = sb("negI", [P, P], BF16)
        halfpi = sb("halfpi", [P, 1])

        scr = ctx.enter_context(nc.psum_tensor("scr", [P, 2, S], F32))
        xp = ctx.enter_context(nc.psum_tensor("xp", [P, 3, 512], F32))
        outp = ctx.enter_context(nc.psum_tensor("outp", [P, 512], F32))

        names = ("consts loaded proj qk_sb v_sb qk mags halved rounded rest factor filtered bias expd "
                 "recip weights turned xpose squared gauss agd cosd acd nned sined tmul summed av outd").split()
        (consts, loaded, proj, qk_sb, v_sb, qk, mags, halved, rounded, rest, factor, filtered, bias,
         expd, recip, weights, turned, xpose, squared, gauss, agd, cosd, acd, nned, sined, tmul, summed,
         av, outd) = (sem("l_" + n) for n in names)

        NX = 4 * TB
        NTILE = 2 * TB
        BASE = [0, 5, 9, 14, 18, 23, 28, 32]
        E0, D0, S0, END = 0, 8, 24, 44

        block = ctx.enter_context(nc.Block())

        def w(eng, s, v):
            if not isinstance(v, int) or v > 0:
                eng.wait_ge(s, v)

        def over_heads(eng, iteration):
            iteration(0, 0, True, False)
            iteration(1, 1, True, True)
            with eng.Fori(0, NHEADS // 2 - 1) as i:
                iteration(2 * i + 2, 0, True, True)
                iteration(2 * i + 3, 1, True, True)
            iteration(NHEADS, 0, False, True)

        @block.sync
        def _(sp):
            def load(t):
                w(sp, proj, 2 * t)
                h = t % H
                sp.dma_start(xb[0:D, :], xT_dram[:, bass.ds((t // H) * S, S)]).then_inc(loaded, 16)
                sp.dma_start(wqk[0:D, 0:D], Wq[:, bass.ds(h * D, D)]).then_inc(loaded, 16)
                sp.dma_start(wqk[0:D, D:P], Wk[:, bass.ds(h * D, D)]).then_inc(loaded, 16)
                sp.dma_start(wqk[D:D + 1, 0:D], bq.rearrange("(a n) -> a n", a=1)[:, bass.ds(h * D, D)]).then_inc(loaded, 16)
                sp.dma_start(wqk[D:D + 1, D:P], bk.rearrange("(a n) -> a n", a=1)[:, bass.ds(h * D, D)]).then_inc(loaded, 16)

            load(0)
            with sp.Fori(1, NHEADS) as t:
                load(t)

        @block.gpsimd
        def _(pool):
            nc.gpsimd.memset(xb[D:D + 1, :], 1.0).then_inc(consts, 1)
            pool.wait_ge(consts, 1)
            nc.gpsimd.memset(negI[:], 0.0).then_inc(consts, 1)
            pool.wait_ge(consts, 2)
            nc.gpsimd.affine_select(out=negI[:], in_=negI[:], compare_op=ALU.not_equal, fill=-1.0,
                                    base=0, pattern=[[-1, P]], channel_multiplier=1).then_inc(consts, 1)
            nc.gpsimd.memset(halfpi[:], math.pi / 2).then_inc(consts, 1)

            def iteration(t, par, front, back):
                g = t - 1
                for s in range(END):
                    if back and s < D0:
                        w(pool, recip, TB * g + s + 1)
                        nc.gpsimd.nop(nofuse=True)
                        nc.gpsimd.tensor_scalar(att[:, 1 - par, s], att[:, 1 - par, s], rs[:, s:s + 1], TURN,
                                                ALU.mult, ALU.mult).then_inc(weights, 1)
                    k = s - S0 - 2
                    if back and 0 <= k < NTILE:
                        w(pool, tmul, NTILE * g + k + 1)
                        nc.gpsimd.tensor_tensor(sinb[:, k % 4], sinb[:, k % 4], cosb[:, k % 4],
                                                ALU.add).then_inc(summed, 1)
                    if front:
                        for u in range(TB):
                            if s == BASE[u] + 2:
                                w(pool, mags, TB * t + u + 1)
                                nc.gpsimd.nop(nofuse=True)
                                nc.gpsimd.tensor_scalar(mag[:, u % 2], mag[:, u % 2], 1.0, -0.5,
                                                        ALU.mult, ALU.add).then_inc(halved, 1)
                            if s == BASE[u] + 4:
                                w(pool, rounded, TB * t + u + 1)
                                nc.gpsimd.tensor_tensor(wgt[:, u % 2], mag[:, u % 2], wgt[:, u % 2],
                                                        ALU.subtract).then_inc(rest, 1)

            over_heads(pool, iteration)

        @block.scalar
        def _(act):
            act.wait_ge(consts, 4)

            def iteration(t, par, front, back):
                g = t - 1
                if front:
                    w(act, proj, 2 * t + 1)
                    w(act, qk, TB * t)
                    nc.scalar.activation(qT[:], scr[0:D, 0], ACT.Copy, scale=QSCALE).then_inc(qk_sb, 1)
                    nc.scalar.activation(kT[:], scr[D:P, 0], ACT.Copy).then_inc(qk_sb, 1)
                    w(act, proj, 2 * t + 2)
                    w(act, av, NTILE * (t - 1))
                    nc.scalar.activation(vo[:, par], scr[:, 1, 0:512].rearrange("p (t d) -> p t d", d=D),
                                         ACT.Copy, scale=1.0 / TURN).then_inc(v_sb, 1)

                def gsquare(d):
                    w(act, xpose, NX * g + d + 1)
                    w(act, agd, NTILE * g + d - 2)
                    nc.scalar.activation(gau[:, d % 3], xp[:, d % 3], ACT.Square,
                                         scale=1.0 / TURN).then_inc(squared, 1)

                def cosine(k):
                    w(act, xpose, NX * g + NTILE + k + 1)
                    w(act, summed, NTILE * g + k - 3)
                    nc.scalar.activation(cosb[:, k % 4], xp[:, (NTILE + k) % 3], ACT.Sin,
                                         bias=halfpi[:, 0:1], scale=-C2 / TURN).then_inc(cosd, 1)

                for s in range(END):
                    if back and s < D0:
                        w(act, bias, g + 1)
                        nc.scalar.activation(att[:, 1 - par, s], att[:, 1 - par, s], ACT.Exp,
                                             bias=nb[:, 1 - par, s:s + 1], scale=EXPSCALE,
                                             accum_out=ssum[:, s:s + 1]).then_inc(expd, 1)
                    if front and s in BASE:
                        u = BASE.index(s)
                        w(act, qk, TB * t + u + 1)
                        w(act, rest, TB * t + u - 1)
                        nc.scalar.activation(mag[:, u % 2], scr[:, u % 2], ACT.Abs).then_inc(mags, 1)
                    if back and D0 <= s < S0:
                        d = s - D0
                        if d == 0:
                            gsquare(0)
                        if d + 1 < NTILE:
                            gsquare(d + 1)
                        w(act, squared, NTILE * g + d + 1)
                        nc.scalar.activation(gau[:, d % 3], gau[:, d % 3], ACT.Exp,
                                             scale=-1.0 / PHI).then_inc(gauss, 1)
                    if back and S0 <= s < S0 + NTILE:
                        k = s - S0
                        if k == 0:
                            cosine(0)
                        if k + 1 < NTILE:
                            cosine(k + 1)
                        w(act, nned, NTILE * g + k + 1)
                        w(act, av, NTILE * g + k - 3)
                        nc.scalar.activation(sinb[:, k % 4], xp[:, (NTILE + k) % 3], ACT.Sin,
                                             scale=2.0 * math.pi * (1.0 - 2.0 ** -22)).then_inc(sined, 1)

            over_heads(act, iteration)

        @block.vector
        def _(dve):
            def iteration(t, par, front, back):
                g = t - 1
                b8 = (g // H) * TB
                for s in range(END):
                    if back and s < D0:
                        w(dve, expd, TB * g + s + 1)
                        nc.vector.reciprocal(rs[:, s:s + 1], ssum[:, s:s + 1]).then_inc(recip, 1)
                    j = s - 2
                    if back and 0 <= j < TB:
                        w(dve, weights, TB * g + j + 1)
                        w(dve, nned, NTILE * g)
                        nc.vector.tensor_scalar(nturn[:, j], att[:, 1 - par, j], ROUND, -ROUND,
                                                ALU.add, ALU.add).then_inc(turned, 1)
                    d = s - D0
                    if back and 0 <= d < NTILE:
                        w(dve, gauss, NTILE * g + d + 1)
                        nc.vector.tensor_tensor(ag[:, d // 2, (d % 2) * 512:(d % 2 + 1) * 512], xp[:, d % 3],
                                                gau[:, d % 3], ALU.mult).then_inc(agd, 1)
                    k = s - S0
                    if back and 0 <= k < NTILE:
                        w(dve, cosd, NTILE * g + k + 1)
                        nc.vector.tensor_tensor(cosb[:, k % 4], xp[:, (NTILE + k) % 3], cosb[:, k % 4],
                                                ALU.mult).then_inc(acd, 1)
                    k = s - S0 - 1
                    if back and 0 <= k < NTILE:
                        w(dve, sined, NTILE * g + k + 1)
                        nc.vector.tensor_tensor(sinb[:, k % 4], sinb[:, k % 4],
                                                ag[:, k // 2, (k % 2) * 512:(k % 2 + 1) * 512],
                                                ALU.mult).then_inc(tmul, 1)
                    if front:
                        for u in range(TB):
                            if s == BASE[u] + 3:
                                w(dve, halved, TB * t + u + 1)
                                w(dve, filtered, TB * t + u - 1)
                                nc.vector.tensor_scalar(wgt[:, u % 2], mag[:, u % 2], ROUND, -ROUND,
                                                        ALU.add, ALU.add).then_inc(rounded, 1)
                            if s == BASE[u] + 7:
                                w(dve, rest, TB * t + u + 1)
                                nc.vector.tensor_scalar(wgt[:, u % 2], wgt[:, u % 2], 1.0 / 3.0 - 0.5, PHI,
                                                        ALU.is_ge, ALU.add).then_inc(factor, 1)
                                w(dve, factor, TB * t + u + 1)
                                w(dve, xpose, NX * (t - 1))
                                nc.vector.nop(nofuse=True)
                                nc.vector.tensor_tensor_reduce(
                                    att[:, par, u], wgt[:, u % 2], scr[:, u % 2], 1.0, -3.0e38, ALU.mult, ALU.max,
                                    mx[:, par, u:u + 1]).then_inc(filtered, 1)
                if front:
                    w(dve, filtered, TB * (t + 1))
                    nc.vector.tensor_scalar(nb[:, par], mx[:, par], -EXPSCALE, None, ALU.mult).then_inc(bias, 1)
                if back:
                    w(dve, av, NTILE * (g + 1))
                    hv = hres[:, bass.ds(b8, TB), :]
                    nc.vector.tensor_tensor(hv, outp[:].rearrange("p (t d) -> p t d", d=D), hv,
                                            ALU.add).then_inc(outd, 1)

            over_heads(dve, iteration)

        @block.tensor
        def _(pe):
            pe.wait_ge(consts, 4)

            def iteration(t, par, front, back):
                g = t - 1
                if front:
                    w(pe, loaded, 80 * (t + 1))
                    w(pe, filtered, TB * t - 1)
                    for c in range(2):
                        mm = nc.tensor.matmul(scr[:, 0, c * 512:(c + 1) * 512], wqk[:], xb[:, c * 512:(c + 1) * 512],
                                              start=True, stop=True)
                    mm.then_inc(proj, 1)
                    w(pe, filtered, TB * t)
                    for j in range(TB):
                        mm = nc.tensor.matmul(scr[:, 1, j * D:(j + 1) * D], xb[:, j * P:(j + 1) * P],
                                              wvo[:, bass.ds((t % H) * D, D)], start=True, stop=True)
                    mm.then_inc(proj, 1)

                def fill(x):
                    w(pe, weights, TB * (g + 1))
                    if x < 3:
                        w(pe, sined, NTILE * g - (1, 0, 2)[x])
                    elif x - 3 < NTILE:
                        w(pe, agd, NTILE * g + x - 2)
                    else:
                        w(pe, sined, NTILE * g + x - 2 - NTILE)
                    kt, half = (x // 2) % TB, x % 2
                    for i in range(4):
                        mm = nc.tensor.matmul(xp[:, x % 3, i * P:(i + 1) * P],
                                              att[:, 1 - par, 4 * half + i, kt * P:(kt + 1) * P], ident[:],
                                              is_transpose=True, start=(i == 0), stop=(i == 3),
                                              skip_group_check=True)
                    mm.then_inc(xpose, 1)

                for s in range(END):
                    if front and s in BASE:
                        u = BASE.index(s)
                        if u == 0:
                            w(pe, qk_sb, 2 * t + 2)
                        elif u == 1:
                            w(pe, v_sb, t + 1)
                        else:
                            w(pe, filtered, TB * t + u - 1)
                        for c in range(2):
                            mm = nc.tensor.matmul(scr[:, u % 2, c * 512:(c + 1) * 512], qT[:, u * P:(u + 1) * P],
                                                  kT[:, c * 512:(c + 1) * 512], start=True, stop=True)
                        mm.then_inc(qk, 1)
                    if back:
                        if s == D0:
                            fill(0)
                            fill(1)
                        if D0 <= s < S0:
                            fill(s - D0 + 2)
                        k = s - S0
                        if 0 <= k < NTILE:
                            w(pe, acd, NTILE * g + k + 1)
                            w(pe, turned, TB * (g + 1))
                            kt, half = k // 2, k % 2
                            for i in range(4):
                                mm = nc.tensor.matmul(xp[:, (NTILE + k) % 3, i * P:(i + 1) * P],
                                                      nturn[:, 4 * half + i, kt * P:(kt + 1) * P], negI[:],
                                                      start=False, stop=True, skip_group_check=True)
                            mm.then_inc(nned, 1)
                            if NTILE + k + 2 < NX:
                                fill(NTILE + k + 2)
                        k = s - S0 - 3
                        if 0 <= k < NTILE:
                            w(pe, summed, NTILE * g + k + 1)
                            if k == 0:
                                w(pe, outd, g)
                                w(pe, v_sb, g + 1)
                            kt, half = k // 2, k % 2
                            for i in range(4):
                                o = (4 * half + i) * D
                                mm = nc.tensor.matmul(outp[:, o:o + D], sinb[:, k % 4, i * P:(i + 1) * P],
                                                      vo[:, 1 - par, kt, :], start=(k == 0 and i == 0),
                                                      stop=(k >= NTILE - 2), skip_group_check=True)
                            mm.then_inc(av, 1)

            over_heads(pe, iteration)


NH, NKV, HD = 4, 2, 16
NE, HID = 8, 170
HC = HID // 2
EPS_RMS = 1e-6


def wait(eng, s, v):
    if not isinstance(v, int) or v > 0:
        eng.wait_ge(s, v)


def held(eng, s, v):
    if not isinstance(v, int) or v > 0:
        eng.wait_ge(s, v)
        eng.nop(nofuse=True)


def over_batches(eng, body):
    body(0)
    with eng.Fori(1, B) as b:
        body(b)


def causal(nc, ident, hres, x2, wqk4, wvT, woT, ln1, cosT, sinT):
    with ExitStack() as ctx:
        def sb(name, shape, dt=F32):
            return ctx.enter_context(nc.sbuf_tensor(name, shape, dt))

        sq = sb("c_sq", [P, NT, D])
        s1, mean, s2, var, std, rstd = (sb("c_" + n, [P, NT]) for n in ("s1", "mean", "s2", "var", "std", "rstd"))
        ms, rms, rinv = (sb("c_" + n, [P, NT]) for n in ("ms", "rms", "rinv"))
        lnw = sb("lnw1", [D, 1])
        wqk = sb("c_wqk", [D, 4, P])
        wv = sb("c_wv", [D, NKV * HD])
        wo = sb("c_wo", [D, D])
        cs = sb("c_cs", [P, S])
        sn = sb("c_sn", [P, S])
        mask = sb("c_mask", [P, P])
        xs = sb("c_xs", [P, TB, D])
        xsT = sb("c_xsT", [D, S])
        q_r = sb("c_q", [P, S])
        k_r = sb("c_k", [P, S])
        q_s = sb("c_qs", [P, S])
        k_s = sb("c_ks", [P, S])
        v = sb("c_v", [P, TB, NKV * HD])
        pr = sb("c_pr", [P, 2, S])
        prT = sb("c_prT", [P, 2, S])
        m = sb("c_m", [P, 4 * TB])
        nm = sb("c_nm", [P, 4 * TB])
        sm = sb("c_sm", [P, 4 * TB])
        rs = sb("c_rs", [P, 4 * TB])
        y = sb("c_y", [P, TB, D])
        yT = sb("c_yT", [D, S])

        sc = ctx.enter_context(nc.psum_tensor("c_sc", [P, 2, S], F32))
        pt = ctx.enter_context(nc.psum_tensor("c_pt", [P, 3, 512], F32))
        yp = ctx.enter_context(nc.psum_tensor("c_yp", [P, 512], F32))

        names = ("w_in consts wmul ln sqd rooted scaled xT xT_sb proj cosd sind roped pt_done pt_sb sc_done "
                 "masked maxed negd expd yd recip ynorm wo_add").split()
        (w_in, consts, wmul, ln, sqd, rooted, scaled, xT, xT_sb, proj, cosd, sind, roped, pt_done, pt_sb, sc_done,
         masked, maxed, negd, expd, yd, recip, ynorm, wo_add) = (ctx.enter_context(nc.semaphore("c_" + n)) for n in names)

        UNITS = [(qt, h) for qt in range(TB) for h in range(NH)]
        NU = len(UNITS)
        GROUPS = [(n, g) for n, (qt, h) in enumerate(UNITS) for g in range(qt // 4 + 1)]
        USE_V, USE_G, USE_YT, USE_WO = 0, 1, 1 + len(GROUPS), 3 + len(GROUPS)
        NSB = 3 + len(GROUPS)
        FIRST = {n: GROUPS.index((n, 0)) for n in range(NU)}
        LAST = {n: FIRST[n] + UNITS[n][0] // 4 for n in range(NU)}

        block = ctx.enter_context(nc.Block())

        @block.sync
        def _(sp):
            for dst, src in ((wqk[:], wqk4), (wv[:], wvT), (wo[:], woT), (cs[:], cosT), (sn[:], sinT),
                             (lnw[:], ln1.rearrange("(p a) -> p a", a=1))):
                sp.dma_start(dst, src).then_inc(w_in, 16)
            sp.wait_ge(w_in, 96)

        @block.gpsimd
        def _(pool):
            nc.gpsimd.memset(mask[:], 0.0).then_inc(consts, 1)
            pool.wait_ge(consts, 1)
            nc.gpsimd.affine_select(out=mask[:], in_=mask[:], compare_op=ALU.is_ge, fill=-1e30,
                                    base=0, pattern=[[-1, P]], channel_multiplier=1).then_inc(consts, 1)

            def body(b):
                wait(pool, sind, 2 * b + 1)
                nc.gpsimd.tensor_tensor(q_r[:], q_r[:], q_s[:], ALU.add).then_inc(roped, 1)
                wait(pool, sind, 2 * b + 2)
                nc.gpsimd.tensor_tensor(k_r[:], k_r[:], k_s[:], ALU.add).then_inc(roped, 1)
            over_batches(pool, body)

        @block.scalar
        def _(act):
            act.wait_ge(ln, 3)
            nc.scalar.activation(sq[:], x2[:], ACT.Square).then_inc(sqd, 1)
            act.wait_ge(ln, 5)
            nc.scalar.activation(std[:], var[:], ACT.Sqrt).then_inc(rooted, 1)
            act.wait_ge(ln, 7)
            nc.scalar.activation(sq[:], x2[:], ACT.Square).then_inc(sqd, 1)
            act.wait_ge(ln, 9)
            nc.scalar.activation(rms[:], ms[:], ACT.Sqrt).then_inc(rooted, 1)

            def body(b):
                wait(act, xT, b + 1)
                wait(act, proj, 5 * b)
                nc.scalar.activation(xsT[:], sc[0:D, 0], ACT.Copy).then_inc(xT_sb, 1)
                wait(act, pt_done, 52 * b + USE_V + 1)
                nc.scalar.activation(v[:], pt[:, 0, 0:TB * NKV * HD].rearrange("p (t d) -> p t d", t=TB),
                                     ACT.Copy).then_inc(pt_sb, 1)

                def expo(n):
                    qt = UNITS[n][0]
                    wait(act, negd, NU * b + n + 1)
                    wait(act, pt_done, 52 * b + (USE_G + LAST[n - 2] + 1 if n >= 2 else 0))
                    nc.scalar.activation(pr[:, n % 2, 0:(qt + 1) * P], sc[:, n % 2, 0:(qt + 1) * P], ACT.Exp,
                                         bias=nm[:, n:n + 1], scale=1.0 / math.sqrt(HD),
                                         accum_out=sm[:, n:n + 1]).then_inc(expd, 1)

                expo(0)
                for n in range(NU):
                    if n + 1 < NU:
                        expo(n + 1)
                    qt = UNITS[n][0]
                    for g in range(qt // 4 + 1):
                        use = USE_G + FIRST[n] + g
                        wid = (min(qt, 4 * g + 3) - 4 * g + 1) * P
                        wait(act, pt_done, 52 * b + use + 1)
                        wait(act, yd, NU * b + n - 1)
                        nc.scalar.activation(prT[:, n % 2, g * 512:g * 512 + wid], pt[:, use % 3, 0:wid],
                                             ACT.Copy).then_inc(pt_sb, 1)
                for i in range(2):
                    use = USE_YT + i
                    wait(act, pt_done, 52 * b + use + 1)
                    nc.scalar.activation(yT[:, i * 512:(i + 1) * 512], pt[0:D, use % 3], ACT.Copy).then_inc(pt_sb, 1)
            over_batches(act, body)

        @block.vector
        def _(dve):
            dve.wait_ge(w_in, 96)
            nc.vector.tensor_scalar(wqk[:], wqk[:], lnw[:, 0:1], None, ALU.mult).then_inc(wmul, 1)
            nc.vector.tensor_scalar(wv[:], wv[:], lnw[:, 0:1], None, ALU.mult).then_inc(wmul, 1)
            nc.vector.tensor_reduce(s1[:], hres[:], AX, ALU.add).then_inc(ln, 1)
            dve.wait_ge(ln, 1)
            nc.vector.tensor_scalar(mean[:], s1[:], 1.0 / D, None, ALU.mult).then_inc(ln, 1)
            dve.wait_ge(ln, 2)
            nc.vector.tensor_tensor(x2[:], hres[:], mean[:].unsqueeze(2).to_broadcast([P, NT, D]),
                                    ALU.subtract).then_inc(ln, 1)
            dve.wait_ge(sqd, 1)
            nc.vector.tensor_reduce(s2[:], sq[:], AX, ALU.add).then_inc(ln, 1)
            dve.wait_ge(ln, 4)
            nc.vector.tensor_scalar(var[:], s2[:], 1.0 / D, EPS, ALU.mult, ALU.add).then_inc(ln, 1)
            dve.wait_ge(rooted, 1)
            nc.vector.reciprocal(rstd[:], std[:]).then_inc(ln, 1)
            dve.wait_ge(ln, 6)
            nc.vector.tensor_tensor(x2[:], x2[:], rstd[:].unsqueeze(2).to_broadcast([P, NT, D]),
                                    ALU.mult).then_inc(ln, 1)
            dve.wait_ge(sqd, 2)
            nc.vector.tensor_reduce(s2[:], sq[:], AX, ALU.add).then_inc(ln, 1)
            dve.wait_ge(ln, 8)
            nc.vector.tensor_scalar(ms[:], s2[:], 1.0 / D, EPS_RMS, ALU.mult, ALU.add).then_inc(ln, 1)
            dve.wait_ge(rooted, 2)
            nc.vector.reciprocal(rinv[:], rms[:]).then_inc(ln, 1)
            dve.wait_ge(ln, 10)
            dve.wait_ge(consts, 2)

            def body(b):
                wait(dve, xT, b)
                nc.vector.tensor_tensor(xs[:], x2[:, bass.ds(b * TB, TB), :],
                                        rinv[:, bass.ds(b * TB, TB)].unsqueeze(2).to_broadcast([P, TB, D]),
                                        ALU.mult).then_inc(scaled, 1)
                for i, (dst, tab, done) in enumerate(((q_r, cs, cosd), (q_s, sn, sind), (k_r, cs, cosd), (k_s, sn, sind))):
                    wait(dve, proj, 5 * b + i + 1)
                    wait(dve, sc_done, NU * b)
                    wait(dve, roped, 2 * b)
                    nc.vector.tensor_tensor(dst[:], sc[:, (i + 1) % 2], tab[:], ALU.mult).then_inc(done, 1)

                def top(n):
                    qt = UNITS[n][0]
                    wait(dve, sc_done, NU * b + n + 1)
                    dg = sc[:, n % 2, qt * P:(qt + 1) * P]
                    nc.vector.tensor_tensor(dg, dg, mask[:], ALU.add).then_inc(masked, 1)
                    wait(dve, masked, NU * b + n + 1)
                    nc.vector.tensor_reduce(m[:, n:n + 1], sc[:, n % 2, 0:(qt + 1) * P], AX, ALU.max).then_inc(maxed, 1)
                    wait(dve, maxed, NU * b + n + 1)
                    wait(dve, expd, NU * b)
                    nc.vector.tensor_scalar(nm[:, n:n + 1], m[:, n:n + 1], -1.0 / math.sqrt(HD), None,
                                            ALU.mult).then_inc(negd, 1)

                def norm(n):
                    qt, h = UNITS[n]
                    wait(dve, expd, NU * b + n + 1)
                    nc.vector.reciprocal(rs[:, n:n + 1], sm[:, n:n + 1]).then_inc(recip, 1)
                    wait(dve, recip, NU * b + n + 1)
                    wait(dve, yd, NU * b + n + 1)
                    wait(dve, pt_done, 52 * b)
                    nc.vector.tensor_scalar(y[:, qt, h * HD:(h + 1) * HD], yp[:, 0:HD], rs[:, n:n + 1], None,
                                            ALU.mult).then_inc(ynorm, 1)

                for n in range(NU + 2):
                    if n < NU:
                        top(n)
                    if n >= 2:
                        norm(n - 2)
                wait(dve, pt_done, 52 * (b + 1))
                xv = x2[:, bass.ds(b * TB, TB), :]
                hv = hres[:, bass.ds(b * TB, TB), :]
                nc.vector.tensor_tensor(xv, pt[:, USE_WO % 3].rearrange("p (t d) -> p t d", d=D), xv,
                                        ALU.add).then_inc(wo_add, 1)
                wait(dve, wo_add, 2 * b + 1)
                nc.vector.tensor_tensor(hv, hv, xv, ALU.add).then_inc(wo_add, 1)
            over_batches(dve, body)

        @block.tensor
        def _(pe):
            pe.wait_ge(wmul, 2)

            def body(b):
                wait(pe, expd, NU * b)
                wait(pe, scaled, b + 1)
                pe.nop(nofuse=True)
                for t in range(TB):
                    mm = nc.tensor.transpose(sc[0:D, 0, t * P:(t + 1) * P], xs[:, t, :], ident[:])
                mm.then_inc(xT, 1)
                wait(pe, xT_sb, b + 1)
                for i in range(4):
                    if i >= 2:
                        wait(pe, (cosd, sind)[i - 2], 2 * b + 1)
                    for c in range(2):
                        mm = nc.tensor.matmul(sc[:, (i + 1) % 2, c * 512:(c + 1) * 512], wqk[:, i],
                                              xsT[:, c * 512:(c + 1) * 512], start=True, stop=True)
                    mm.then_inc(proj, 1)
                wait(pe, wo_add, 2 * b)
                for t in range(TB):
                    mm = nc.tensor.matmul(pt[:, 0, t * NKV * HD:(t + 1) * NKV * HD], xsT[:, t * P:(t + 1) * P],
                                          wv[:], start=True, stop=True)
                mm.then_inc(pt_done, 1)
                mm = nc.tensor.matmul(pt[:, 1, 0:NKV * HD], xsT[:, 0:P], wv[:], start=True, stop=True)
                mm.then_inc(proj, 1)
                wait(pe, roped, 2 * b + 2)
                wait(pe, cosd, 2 * b + 2)
                wait(pe, pt_sb, NSB * b + 1)

                def score(n):
                    qt, h = UNITS[n]
                    if n >= 2:
                        wait(pe, expd, NU * b + n - 1)
                    pe.nop(nofuse=True)
                    r = slice(32 * h, 32 * h + HD)
                    for c in range(0, (qt + 1) * P, 512):
                        e = min(c + 512, (qt + 1) * P)
                        mm = nc.tensor.matmul(sc[:, n % 2, c:e], q_r[r, qt * P:(qt + 1) * P], k_r[r, c:e],
                                              start=True, stop=True)
                    mm.then_inc(sc_done, 1)

                def turn(n):
                    qt = UNITS[n][0]
                    wait(pe, expd, NU * b + n + 1)
                    for g in range(qt // 4 + 1):
                        use = USE_G + FIRST[n] + g
                        wait(pe, pt_sb, NSB * b + max(use - 2, 1))
                        for kt in range(4 * g, min(qt, 4 * g + 3) + 1):
                            mm = nc.tensor.transpose(pt[:, use % 3, (kt - 4 * g) * P:(kt - 4 * g + 1) * P],
                                                     pr[:, n % 2, kt * P:(kt + 1) * P], ident[:])
                        mm.then_inc(pt_done, 1)

                def apply(n):
                    qt, h = UNITS[n]
                    wait(pe, pt_sb, NSB * b + USE_G + LAST[n] + 1)
                    wait(pe, ynorm, NU * b + n)
                    pe.nop(nofuse=True)
                    kv = h // (NH // NKV) * HD
                    for kt in range(qt + 1):
                        mm = nc.tensor.matmul(yp[:, 0:HD], prT[:, n % 2, kt * P:(kt + 1) * P],
                                              v[:, kt, kv:kv + HD], start=(kt == 0), stop=(kt == qt))
                    mm.then_inc(yd, 1)

                for n in range(NU + 2):
                    if n < NU:
                        score(n)
                    if 1 <= n <= NU:
                        turn(n - 1)
                    if n >= 2:
                        apply(n - 2)
                wait(pe, ynorm, NU * (b + 1))
                for i in range(2):
                    use = USE_YT + i
                    wait(pe, pt_sb, NSB * b + use - 2)
                    pe.nop(nofuse=True)
                    for t in range(4):
                        mm = nc.tensor.transpose(pt[0:D, use % 3, t * P:(t + 1) * P], y[:, 4 * i + t, :], ident[:])
                    mm.then_inc(pt_done, 1)
                wait(pe, pt_sb, NSB * (b + 1))
                pe.nop(nofuse=True)
                for t in range(TB):
                    mm = nc.tensor.matmul(pt[:, USE_WO % 3, t * D:(t + 1) * D], yT[:, t * P:(t + 1) * P], wo[:],
                                          start=True, stop=True)
                mm.then_inc(pt_done, 1)
            assert USE_WO + 1 == 52 and NSB == 51
            over_batches(pe, body)


def experts(nc, ident, hres, x3, router, w1T, w3T, w2T, ln2, out):
    with ExitStack() as ctx:
        def sb(name, shape, dt=F32):
            return ctx.enter_context(nc.sbuf_tensor(name, shape, dt))

        sq = sb("e_sq", [P, NT, D])
        s2, ms, rms, rinv = (sb("e_" + n, [P, NT]) for n in ("s2", "ms", "rms", "rinv"))
        lnw = sb("lnw2", [D, 1])
        rt = sb("e_rt", [D, NE])
        w1 = sb("e_w1", [D, NE, 2, HC])
        w3 = sb("e_w3", [D, NE, 2, HC])
        w2 = sb("e_w2", [HC, NE, 2, D])
        rank = sb("e_rank", [P, TB, NE])
        rank_i = sb("e_ranki", [P, TB, NE], I32)
        xs = sb("e_xs", [P, TB, D])
        xT = sb("e_xT", [D, S])
        prob = sb("e_prob", [P, TB, NE])
        hot1 = sb("e_hot1", [P, TB, NE])
        hot2 = sb("e_hot2", [P, TB, NE])
        tmp = sb("e_tmp", [P, TB, NE])
        wts = sb("e_wts", [P, TB, NE])
        c1, c2, c3, m1, m2 = (sb("e_" + n, [P, TB]) for n in ("c1", "c2", "c3", "m1", "m2"))
        sl = sb("e_sl", [HC, 3, 512])
        hh = sb("e_hh", [HC, 2, 2, S])
        wout = sb("e_wout", [P, 2, TB, D])

        hp = ctx.enter_context(nc.psum_tensor("e_hp", [P, 3, 2, 512], F32))
        op = ctx.enter_context(nc.psum_tensor("e_op", [P, 2, 512], F32))

        names = ("w_in ranked wmul rm sqd rooted scaled xTd xT_sb logit routed lexp hpd silud hhd opd woutd added out_dma").split()
        (w_in, ranked, wmul, rm, sqd, rooted, scaled, xTd, xT_sb, logit, routed, lexp, hpd, silud, hhd, opd, woutd,
         added, out_dma) = (ctx.enter_context(nc.semaphore("e_" + n)) for n in names)

        UNITS = [(e, c, half) for e in range(NE) for c in range(2) for half in range(2)]
        NU = len(UNITS)
        NR = 20

        block = ctx.enter_context(nc.Block())
        out_v = out.rearrange("b (t p) d -> b p t d", p=P)

        @block.sync
        def _(sp):
            for dst, src in ((rt[:], router), (w1[:], w1T), (w3[:], w3T), (w2[:], w2T),
                             (lnw[:], ln2.rearrange("(p a) -> p a", a=1))):
                sp.dma_start(dst, src).then_inc(w_in, 16)
            sp.wait_ge(w_in, 80)

            def body(b):
                wait(sp, added, NE * (b + 1))
                sp.dma_start(out_v[bass.ds(b, 1)].rearrange("a p t d -> (a p) t d"),
                             hres[:, bass.ds(b * TB, TB), :]).then_inc(out_dma, 16)
            over_batches(sp, body)
            sp.wait_ge(out_dma, 16 * B)

        @block.gpsimd
        def _(pool):
            nc.gpsimd.iota(rank_i[:], pattern=[[0, TB], [-1, NE]], base=NE, channel_multiplier=0).then_inc(ranked, 1)

            def body(b):
                for e in range(NE):
                    wait(pool, woutd, NE * b + e + 1)
                    wait(pool, added, NE * b + e)
                    pool.nop(nofuse=True)
                    hv = hres[:, bass.ds(b * TB, TB), :]
                    nc.gpsimd.tensor_tensor(hv, hv, wout[:, e % 2], ALU.add).then_inc(added, 1)
            over_batches(pool, body)

        @block.scalar
        def _(act):
            nc.scalar.activation(sq[:], x3[:], ACT.Square).then_inc(sqd, 1)
            act.wait_ge(rm, 2)
            nc.scalar.activation(rms[:], ms[:], ACT.Sqrt).then_inc(rooted, 1)

            def body(b):
                wait(act, xTd, b + 1)
                wait(act, hpd, NU * b)
                nc.scalar.activation(xT[:], hp[0:D, 0].rearrange("p a n -> p (a n)"), ACT.Copy).then_inc(xT_sb, 1)
                wait(act, routed, NR * b + 2)
                nc.scalar.activation(prob[:], prob[:], ACT.Exp).then_inc(lexp, 1)
                for n in range(NU):
                    wait(act, hpd, NU * b + n + 1)
                    wait(act, hhd, NU * b + n - 2)
                    nc.scalar.activation(sl[:, n % 3], hp[0:HC, n % 3, 0], ACT.Silu).then_inc(silud, 1)
            over_batches(act, body)

        @block.vector
        def _(dve):
            dve.wait_ge(w_in, 80)
            for t in (rt, w1, w3):
                nc.vector.tensor_scalar(t[:], t[:], lnw[:, 0:1], None, ALU.mult).then_inc(wmul, 1)
            dve.wait_ge(ranked, 1)
            nc.vector.tensor_copy(rank[:], rank_i[:]).then_inc(wmul, 1)
            dve.wait_ge(sqd, 1)
            nc.vector.tensor_reduce(s2[:], sq[:], AX, ALU.add).then_inc(rm, 1)
            dve.wait_ge(rm, 1)
            nc.vector.tensor_scalar(ms[:], s2[:], 1.0 / D, EPS_RMS, ALU.mult, ALU.add).then_inc(rm, 1)
            dve.wait_ge(rooted, 1)
            nc.vector.reciprocal(rinv[:], rms[:]).then_inc(rm, 1)
            dve.wait_ge(rm, 3)
            dve.wait_ge(wmul, 4)

            def body(b):
                wait(dve, xTd, b)
                nc.vector.tensor_tensor(xs[:], x3[:, bass.ds(b * TB, TB), :],
                                        rinv[:, bass.ds(b * TB, TB)].unsqueeze(2).to_broadcast([P, TB, D]),
                                        ALU.mult).then_inc(scaled, 1)
                step = [0]

                def did(ins):
                    step[0] += 1
                    ins.then_inc(routed, 1)
                    wait(dve, routed, NR * b + step[0])

                def wide(x):
                    return x[:].unsqueeze(2).to_broadcast([P, TB, NE])

                V = nc.vector
                lg = op[:, 0, 0:TB * NE].rearrange("p (t e) -> p t e", e=NE)
                wait(dve, logit, b + 1)
                did(V.tensor_reduce(c1[:], lg, AX, ALU.max))
                did(V.tensor_tensor(prob[:], lg, wide(c1), ALU.subtract))
                wait(dve, lexp, b + 1)
                did(V.tensor_reduce(c2[:], prob[:], AX, ALU.add))
                did(V.reciprocal(c3[:], c2[:]))
                did(V.tensor_tensor(prob[:], prob[:], wide(c3), ALU.mult))
                for m, hot, c in ((m1, hot1, c1), (m2, hot2, c2)):
                    did(V.tensor_reduce(m[:], prob[:], AX, ALU.max))
                    did(V.tensor_tensor(tmp[:], prob[:], wide(m), ALU.is_equal))
                    did(V.tensor_tensor(tmp[:], tmp[:], rank[:], ALU.mult))
                    did(V.tensor_reduce(c[:], tmp[:], AX, ALU.max))
                    did(V.tensor_tensor(hot[:], tmp[:], wide(c), ALU.is_equal))
                    if m is m1:
                        did(V.scalar_tensor_tensor(out=prob[:], in0=hot[:], scalar=-4.0, in1=prob[:],
                                                   op0=ALU.mult, op1=ALU.add))
                did(V.scalar_tensor_tensor(out=c3[:], in0=m1[:], scalar=1e-9, in1=m2[:], op0=ALU.add, op1=ALU.add))
                did(V.reciprocal(c1[:], c3[:]))
                V.tensor_tensor(m1[:], m1[:], c1[:], ALU.mult)
                did(V.tensor_tensor(m2[:], m2[:], c1[:], ALU.mult))
                did(V.tensor_tensor(hot1[:], hot1[:], wide(m1), ALU.mult))
                assert step[0] == NR, step[0]
                finish_routing(b)

                for n in range(NU):
                    e, c, half = UNITS[n]
                    wait(dve, silud, NU * b + n + 1)
                    if e >= 2:
                        wait(dve, opd, NE * b + e - 1)
                    else:
                        wait(dve, opd, NE * b)
                    nc.vector.tensor_tensor(hh[:, e % 2, c, half * 512:(half + 1) * 512], hp[0:HC, n % 3, 1],
                                            sl[:, n % 3], ALU.mult).then_inc(hhd, 1)
                    if n % 4 == 1 and e >= 1:
                        weigh(b, e - 1)
                weigh(b, NE - 1)

            def finish_routing(b):
                nc.vector.tensor_tensor(hot2[:], hot2[:], m2[:].unsqueeze(2).to_broadcast([P, TB, NE]),
                                        ALU.mult).then_inc(rm, 1)
                wait(dve, rm, 2 * b + 4)
                nc.vector.tensor_tensor(wts[:], hot1[:], hot2[:], ALU.add).then_inc(rm, 1)
                wait(dve, rm, 2 * b + 5)

            def weigh(b, e):
                wait(dve, opd, NE * b + e + 1)
                wait(dve, added, NE * b + e - 1)
                nc.vector.tensor_tensor(wout[:, e % 2], op[:, e % 2].rearrange("p (t d) -> p t d", d=D),
                                        wts[:, :, e:e + 1].to_broadcast([P, TB, D]), ALU.mult).then_inc(woutd, 1)
            over_batches(dve, body)

        @block.tensor
        def _(pe):
            pe.wait_ge(wmul, 3)

            def body(b):
                wait(pe, hhd, NU * b)
                wait(pe, scaled, b + 1)
                pe.nop(nofuse=True)
                tv = hp[0:D, 0].rearrange("p a n -> p (a n)")
                for t in range(TB):
                    mm = nc.tensor.transpose(tv[:, t * P:(t + 1) * P], xs[:, t, :], ident[:])
                mm.then_inc(xTd, 1)
                wait(pe, xT_sb, b + 1)
                wait(pe, woutd, NE * b)
                pe.nop(nofuse=True)
                for t in range(TB):
                    mm = nc.tensor.matmul(op[:, 0, t * NE:(t + 1) * NE], xT[:, t * P:(t + 1) * P], rt[:],
                                          start=True, stop=True)
                mm.then_inc(logit, 1)

                def up(n):
                    e, c, half = UNITS[n]
                    wait(pe, hhd, NU * b + n - 2)
                    pe.nop(nofuse=True)
                    nc.tensor.matmul(hp[0:HC, n % 3, 0], w1[:, e, c], xT[:, half * 512:(half + 1) * 512],
                                     start=True, stop=True)
                    nc.tensor.matmul(hp[0:HC, n % 3, 1], w3[:, e, c], xT[:, half * 512:(half + 1) * 512],
                                     start=True, stop=True).then_inc(hpd, 1)

                def down(e):
                    wait(pe, hhd, NU * b + 4 * (e + 1))
                    if e == 0:
                        wait(pe, routed, NR * b + 2)
                    wait(pe, woutd, NE * b + max(e - 1, 0))
                    pe.nop(nofuse=True)
                    for t in range(TB):
                        for c in range(2):
                            mm = nc.tensor.matmul(op[:, e % 2, t * D:(t + 1) * D], hh[:, e % 2, c, t * P:(t + 1) * P],
                                                  w2[:, e, c], start=(c == 0), stop=(c == 1))
                    mm.then_inc(opd, 1)

                for n in range(NU):
                    up(n)
                    if n % 4 == 3 and n > 4:
                        down(n // 4 - 1)
                down(NE - 1)
            over_batches(pe, body)


def tower(nc, a, out):
    with ExitStack() as ctx:
        ident = ctx.enter_context(nc.sbuf_tensor("ident", [P, P], F32))
        hres = ctx.enter_context(nc.sbuf_tensor("hres", [P, NT, D], F32))
        wvo = ctx.enter_context(nc.sbuf_tensor("wvo", [D + 1, H * D], F32))
        xT_dram = nc.dram_tensor("xT_dram", (D, B * S), F32, kind="Internal").ap()
        made = ctx.enter_context(nc.semaphore("made"))
        with nc.Block() as block:
            @block.gpsimd
            def _(pool):
                nc.gpsimd.memset(ident[:], 0.0).then_inc(made, 1)
                pool.wait_ge(made, 1)
                nc.gpsimd.affine_select(out=ident[:], in_=ident[:], compare_op=ALU.not_equal, fill=1.0,
                                        base=0, pattern=[[-1, P]], channel_multiplier=1).then_inc(made, 1)
                pool.wait_ge(made, 2)
        embed(nc, ident, hres, xT_dram, wvo, a["x"], a["L0_tok_turns"], a["L0_tok_poly_coeffs"],
              a["L0_attn_Wv"], a["L0_attn_bv"], a["L0_attn_Wo"], a["L0_attn_bo"])
        lattice(nc, ident, hres, xT_dram, wvo, a["L0_attn_Wq"], a["L0_attn_bq"], a["L0_attn_Wk"],
                a["L0_attn_bk"])
        x2 = ctx.enter_context(nc.sbuf_tensor("x2", [P, NT, D], F32))
        causal(nc, ident, hres, x2, a["wqk4"], a["wvT"], a["woT"], a["L0_ffn_ln1_w"], a["cosT"], a["sinT"])
        experts(nc, ident, hres, x2, a["routerT"], a["w1T"], a["w3T"], a["w2T"], a["L0_ffn_ln2_w"], out)


_INS = ["x", "L0_tok_turns", "L0_tok_poly_coeffs", "L0_attn_Wq", "L0_attn_bq", "L0_attn_Wk", "L0_attn_bk",
        "L0_attn_Wv", "L0_attn_bv", "L0_attn_Wo", "L0_attn_bo", "L0_ffn_ln1_w", "L0_ffn_ln2_w"]


def _laid_out(inputs):
    import numpy as _np

    def spread(w, heads, swap):
        o = _np.zeros((D, P), w.dtype)
        for h in range(NH):
            r = w[heads[h] * HD:(heads[h] + 1) * HD]
            if swap:
                r = _np.concatenate([r[HD // 2:], r[:HD // 2]])
            o[:, 32 * h:32 * h + HD] = r.T
        return o

    wq, wk = (_np.asarray(inputs["L0_ffn_" + n]) for n in ("wq", "wk"))
    qh, kh = list(range(NH)), [h // (NH // NKV) for h in range(NH)]
    inv_freq = 1.0 / 10000.0 ** (_np.arange(0, HD, 2, dtype=_np.float32) / HD)
    freqs = _np.outer(_np.arange(S, dtype=_np.float32), inv_freq)
    cos, sin = _np.zeros((P, S), _np.float32), _np.zeros((P, S), _np.float32)
    for h in range(NH):
        cos[32 * h:32 * h + HD] = _np.concatenate([_np.cos(freqs), _np.cos(freqs)], axis=-1).T
        sin[32 * h:32 * h + HD] = _np.concatenate([-_np.sin(freqs), _np.sin(freqs)], axis=-1).T
    hid = lambda n: _np.asarray(inputs["L0_ffn_" + n]).transpose(2, 0, 1).reshape(D, NE, 2, HC)
    return {
        "wqk4": _np.stack([spread(wq, qh, False), spread(wq, qh, True), spread(wk, kh, False),
                           spread(wk, kh, True)], axis=1),
        "wvT": _np.asarray(inputs["L0_ffn_wv"]).T, "woT": _np.asarray(inputs["L0_ffn_wo"]).T,
        "routerT": _np.asarray(inputs["L0_ffn_router_w"]).T, "w1T": hid("w1"), "w3T": hid("w3"),
        "w2T": _np.asarray(inputs["L0_ffn_w2"]).reshape(NE, D, 2, HC).transpose(3, 0, 2, 1),
        "cosT": cos, "sinT": sin,
    }


def kernel(**inputs):
    import numpy as _np
    import concourse.bacc as _bacc
    from concourse import mybir as _mybir
    from concourse.bass_utils import run_bass_kernel_spmd as _run

    nc = _bacc.Bacc("TRN2", target_bir_lowering=False, num_devices=1)
    arrays, aps = {}, {}
    given = {name: inputs[name] for name in _INS} | _laid_out(inputs)
    for name, a in given.items():
        a = _np.ascontiguousarray(a)
        arrays[f"in_{name}"] = a
        aps[name] = nc.dram_tensor(f"in_{name}", a.shape, _mybir.dt.from_np(a.dtype), kind="ExternalInput").ap()
    out = nc.dram_tensor("out", (B, S, D), _mybir.dt.float32, kind="ExternalOutput").ap()
    tower(nc, aps, out)
    r = _run(nc, [arrays], core_ids=[0])
    return r.results[0]["out"]
```

```python
import math
from contextlib import ExitStack

import concourse.bass as bass
from concourse import mybir

ALU = mybir.AluOpType
ACT = mybir.ActivationFunctionType
AX = mybir.AxisListType.X
F32 = mybir.dt.float32
BF16 = mybir.dt.bfloat16
I32 = mybir.dt.int32

P = 128
B, S, D = 8, 1024, 64
NT = B * S // P
TB = S // P
VOCAB, TURNS, DEGS = 50257, 4, 5
H = 8
NHEADS = B * H
PHI = (1.0 + math.sqrt(5.0)) / 2.0
C1 = PHI * math.sqrt(2.0) * 51.85
C2 = math.pi / PHI
ROUND = 1.5 * 2.0 ** 23
QSCALE = 1618.0 / (8.0 * 3.0)
EXPSCALE = 3.0 / (1618.0 * PHI * PHI)
TURN = C1 / (2.0 * math.pi)
EPS = 1e-5


def wait(eng, s, v):
    if not isinstance(v, int) or v > 0:
        eng.wait_ge(s, v)


def held(eng, s, v):
    if not isinstance(v, int) or v > 0:
        eng.wait_ge(s, v)
        eng.nop(nofuse=True)


def embed(nc, ident, hres, xT_dram, wvo, ids, turns, coeffs, Wv, bv, Wo, bo):
    with ExitStack() as ctx:
        def sb(name, shape, dt=F32):
            return ctx.enter_context(nc.sbuf_tensor(name, shape, dt))

        def sem(name):
            return ctx.enter_context(nc.semaphore(name))

        ids_i = sb("ids_i", [NT, P], I32)
        ids_f = sb("ids_f", [NT, P])
        idx = sb("idx", [P, NT], I32)
        base = sb("base", [P, NT, TURNS])
        mag = sb("mag", [P, NT, TURNS])
        sgn = sb("sgn", [P, NT, TURNS])
        rnd = sb("rnd", [P, NT, TURNS])
        over = sb("over", [P, NT, TURNS])
        pw = sb("pw", [P, NT, 32])
        pwT = sb("pwT", [P, 2, P])
        coef4 = sb("coef4", [P, 4 * D])
        wv1 = sb("wv1", [D + 1, H * D])
        wvT = sb("wvT", [D, H, D + 1])
        wo_h = sb("wo_h", [D, H, D])
        bo_all = sb("bo_all", [P, D])
        cen = sb("cen", [P, NT, D])
        sq = sb("sq", [P, NT, D])
        s1 = sb("s1", [P, NT])
        mean = sb("mean", [P, NT])
        s2 = sb("s2", [P, NT])
        var = sb("var", [P, NT])
        std = sb("std", [P, NT])
        rstd = sb("rstd", [P, NT])
        xn = sb("xn", [P, 2, TB, D])
        xT = sb("xT", [D, 2, S])

        ps_a = ctx.enter_context(nc.psum_tensor("ps_a", [P, 2, 512], F32))
        ps_e = ctx.enter_context(nc.psum_tensor("ps_e", [P, 2, 512], F32))
        ps_x = ctx.enter_context(nc.psum_tensor("ps_x", [P, 2, 1024], F32))

        ids_in, w_in, coef_in = sem("ids_in"), sem("w_in"), sem("coef_in")
        zeroed = sem("zeroed")
        idf, idT, idx_ok, got = sem("idf"), sem("idT"), sem("idx_ok"), sem("got")
        magn, trunc, pows = sem("magn"), sem("trunc"), sem("pows")
        pT, pT_sb, emb, emb_sb = sem("pT"), sem("pT_sb"), sem("emb"), sem("emb_sb")
        wT, wT_sb, wm, wm_sb = sem("wT"), sem("wT_sb"), sem("wm"), sem("wm_sb")
        ln, sqd, rooted, normed, nT, nT_sb = (sem(n) for n in
            ("ln", "sqd", "rooted", "normed", "nT", "nT_sb"))
        nT_out = [sem("nT_out0"), sem("nT_out1")]

        block = ctx.enter_context(nc.Block())

        @block.sync
        def _(sp):
            sp.dma_start(ids_i[:], ids.rearrange("b (t p) -> (b t) p", p=P)).then_inc(ids_in, 16)
            sp.dma_start(wv1[0:D, :], Wv).then_inc(w_in, 16)
            sp.dma_start(wv1[D:D + 1, :], bv.rearrange("(a n) -> a n", a=1)).then_inc(w_in, 16)
            sp.dma_start(wo_h[:], Wo.rearrange("(h d) o -> d h o", d=D)).then_inc(w_in, 16)
            sp.dma_start(bo_all[:], bo.partition_broadcast(P)).then_inc(w_in, 16)
            sp.wait_ge(zeroed, 2)
            for j in range(4):
                sp.dma_start(coef4[32 * j:32 * j + TURNS * DEGS, j * D:(j + 1) * D],
                             coeffs.rearrange("t d o -> (t d) o")).then_inc(coef_in, 16)
            for b in range(B):
                sp.wait_ge(nT_sb, b + 1)
                sp.dma_start(xT_dram[:, b * S:(b + 1) * S], xT[:, b % 2, :]).then_inc(nT_out[b % 2], 16)
            for n in nT_out:
                sp.wait_ge(n, 16 * B // 2)

        @block.gpsimd
        def _(pool):
            nc.gpsimd.memset(coef4[:], 0.0).then_inc(zeroed, 1)
            nc.gpsimd.memset(pw[:], 0.0).then_inc(zeroed, 1)
            pool.wait_ge(idx_ok, 1)
            for t in range(NT):
                nc.gpsimd.indirect_dma_start(
                    out=base[:, t, :], out_offset=None, in_=turns[:, :],
                    in_offset=bass.IndirectOffsetOnAxis(ap=idx[:, t:t + 1], axis=0)).then_inc(got, 16)

        @block.scalar
        def _(act):
            act.wait_ge(got, 16 * NT)
            nc.scalar.activation(mag[:], base[:], ACT.Abs).then_inc(magn, 1)
            nc.scalar.activation(sgn[:], base[:], ACT.Sign).then_inc(magn, 1)
            for g in range(NT // 4):
                act.wait_ge(pT, g + 1)
                if g >= 2:
                    act.wait_ge(emb, g - 1)
                nc.scalar.activation(pwT[:, g % 2, :], ps_a[:, g % 2, 0:P], ACT.Copy).then_inc(pT_sb, 1)
            act.wait_ge(wT, 1)
            nc.scalar.activation(wvT[:, 0:4, :], ps_x[0:D, 0, 0:4 * (D + 1)].rearrange("p (h c) -> p h c", h=4),
                                 ACT.Copy).then_inc(wT_sb, 1)
            nc.scalar.activation(wvT[:, 4:8, :], ps_x[0:D, 1, 0:4 * (D + 1)].rearrange("p (h c) -> p h c", h=4),
                                 ACT.Copy).then_inc(wT_sb, 1)
            act.wait_ge(wm, 1)
            nc.scalar.activation(wvo[:], ps_a[0:D + 1, 0, :], ACT.Copy).then_inc(wm_sb, 1)
            act.wait_ge(ln, 3)
            nc.scalar.activation(sq[:], cen[:], ACT.Square).then_inc(sqd, 1)
            act.wait_ge(ln, 5)
            nc.scalar.activation(std[:], var[:], ACT.Sqrt).then_inc(rooted, 1)
            for b in range(B):
                act.wait_ge(nT, b + 1)
                if b >= 2:
                    act.wait_ge(nT_out[b % 2], 16 * (b // 2))
                nc.scalar.activation(xT[:, b % 2, :], ps_x[0:D, b % 2, :], ACT.Copy).then_inc(nT_sb, 1)

        @block.vector
        def _(dve):
            dve.wait_ge(ids_in, 16)
            nc.vector.tensor_copy(ids_f[:], ids_i[:]).then_inc(idf, 1)
            dve.wait_ge(idT, 1)
            nc.vector.tensor_copy(idx[:], ps_a[:, 0, 0:NT]).then_inc(idx_ok, 1)
            dve.wait_ge(magn, 2)
            nc.vector.tensor_scalar(rnd[:], mag[:], ROUND, -ROUND, ALU.add, ALU.add).then_inc(trunc, 1)
            dve.wait_ge(trunc, 1)
            nc.vector.tensor_tensor(over[:], rnd[:], mag[:], ALU.is_gt).then_inc(trunc, 1)
            dve.wait_ge(trunc, 2)
            nc.vector.tensor_tensor(rnd[:], rnd[:], over[:], ALU.subtract).then_inc(trunc, 1)
            dve.wait_ge(trunc, 3)
            dve.wait_ge(zeroed, 2)
            pv = pw[:, :, 0:TURNS * DEGS].rearrange("p n (t d) -> p n t d", d=DEGS)
            nc.vector.memset(pv[:, :, :, 0], 1.0).then_inc(pows, 1)
            nc.vector.tensor_tensor(pv[:, :, :, 1], rnd[:], sgn[:], ALU.mult).then_inc(pows, 1)
            dve.wait_ge(pows, 2)
            for d in range(2, DEGS):
                nc.vector.tensor_tensor(pv[:, :, :, d], pv[:, :, :, d - 1], pv[:, :, :, 1], ALU.mult).then_inc(pows, 1)
                dve.wait_ge(pows, d + 1)
            for e in range(NT // 8):
                dve.wait_ge(emb, 2 * e + 2)
                nc.vector.tensor_copy(hres[:, 8 * e:8 * e + 8, :],
                                      ps_e[:, e % 2, :].rearrange("p (t d) -> p t d", d=D)).then_inc(emb_sb, 1)
            dve.wait_ge(emb_sb, NT // 8)
            nc.vector.tensor_reduce(s1[:], hres[:], AX, ALU.add).then_inc(ln, 1)
            dve.wait_ge(ln, 1)
            nc.vector.tensor_scalar(mean[:], s1[:], 1.0 / D, None, ALU.mult).then_inc(ln, 1)
            dve.wait_ge(ln, 2)
            nc.vector.tensor_tensor(cen[:], hres[:], mean[:].unsqueeze(2).to_broadcast([P, NT, D]),
                                    ALU.subtract).then_inc(ln, 1)
            dve.wait_ge(w_in, 64)
            nc.vector.tensor_tensor(hres[:], hres[:], bo_all[:].unsqueeze(1).to_broadcast([P, NT, D]),
                                    ALU.add)
            dve.wait_ge(sqd, 1)
            nc.vector.tensor_reduce(s2[:], sq[:], AX, ALU.add).then_inc(ln, 1)
            dve.wait_ge(ln, 4)
            nc.vector.tensor_scalar(var[:], s2[:], 1.0 / D, EPS, ALU.mult, ALU.add).then_inc(ln, 1)
            dve.wait_ge(rooted, 1)
            nc.vector.reciprocal(rstd[:], std[:]).then_inc(ln, 1)
            dve.wait_ge(ln, 6)
            for b in range(B):
                if b >= 2:
                    dve.wait_ge(nT, b - 1)
                nc.vector.tensor_tensor(xn[:, b % 2], cen[:, TB * b:TB * b + TB, :],
                                        rstd[:, TB * b:TB * b + TB].unsqueeze(2).to_broadcast([P, TB, D]),
                                        ALU.mult).then_inc(normed, 1)

        @block.tensor
        def _(pe):
            pe.wait_ge(idf, 1)
            nc.tensor.transpose(ps_a[:, 0, 0:NT], ids_f[:], ident[0:NT, 0:NT]).then_inc(idT, 1)
            pe.wait_ge(w_in, 64)
            for h in range(H):
                mm = nc.tensor.transpose(ps_x[0:D, h // 4, (h % 4) * (D + 1):(h % 4 + 1) * (D + 1)],
                                         wv1[:, h * D:(h + 1) * D], ident[0:D + 1, 0:D + 1])
            mm.then_inc(wT, 1)
            pe.wait_ge(coef_in, 64)
            pe.wait_ge(pows, DEGS)
            pe.wait_ge(idx_ok, 1)
            for g in range(NT // 4):
                if g >= 2:
                    pe.wait_ge(pT_sb, g - 1)
                nc.tensor.transpose(ps_a[:, g % 2, 0:P], pw[:, 4 * g:4 * g + 4, :].rearrange("p t c -> p (t c)"),
                                    ident[:]).then_inc(pT, 1)
                pe.wait_ge(pT_sb, g + 1)
                if g >= 4:
                    pe.wait_ge(emb_sb, g // 2 - 1)
                o = (g % 2) * 4 * D
                nc.tensor.matmul(ps_e[:, (g // 2) % 2, o:o + 4 * D], pwT[:, g % 2, :], coef4[:],
                                 start=True, stop=True).then_inc(emb, 1)
            pe.wait_ge(wT_sb, 2)
            for h in range(H):
                mm = nc.tensor.matmul(ps_a[0:D + 1, 0, h * D:(h + 1) * D], wvT[:, h, :], wo_h[:, h, :],
                                      start=True, stop=True)
            mm.then_inc(wm, 1)
            for b in range(B):
                pe.wait_ge(normed, b + 1)
                if b >= 2:
                    pe.wait_ge(nT_sb, b - 1)
                for t in range(TB):
                    mm = nc.tensor.transpose(ps_x[0:D, b % 2, t * P:(t + 1) * P], xn[:, b % 2, t, :], ident[:])
                mm.then_inc(nT, 1)


def lattice(nc, ident, hres, xT_dram, wvo, Wq, bq, Wk, bk):
    RING = 8
    with ExitStack() as ctx:
        def sb(name, shape, dt=F32):
            return ctx.enter_context(nc.sbuf_tensor(name, shape, dt))

        def sem(name):
            return ctx.enter_context(nc.semaphore(name))

        xq = sb("xq", [D + 1, S])
        xv = sb("xv", [D + 1, S])
        wqk = sb("wqk", [D + 1, P])
        qT = sb("qT", [P, 2, S])
        kT = sb("kT", [P, 2, S])
        vo = sb("vo", [P, TB, D])
        mag = sb("mag2", [P, 4, 512])
        wgt = sb("wgt", [P, 4, 512])
        att = sb("att", [P, 2, TB, S])
        nturn = sb("nturn", [P, TB, S], BF16)
        ag = sb("ag", [P, 2 * TB, 512])
        work = sb("work", [P, RING, 512])
        sinb = sb("sinb", [P, RING, 512])
        mx = sb("mx", [P, 2, 2 * TB])
        nb = sb("nb", [P, 2, TB])
        ssum = sb("ssum", [P, TB])
        rs = sb("rs", [P, TB])
        negI = sb("negI", [P, P], BF16)
        halfpi = sb("halfpi", [P, 1])

        banks = ctx.enter_context(nc.psum_tensor("banks", [P, 7, 512], F32))
        outp = ctx.enter_context(nc.psum_tensor("outp", [P, 512], F32))

        names = ("consts loadq loadv projd qk_sb vald v_sb qk mags halved rounded rest factor filtered bias expd "
                 "recip weights weights2 turned xpose squared gauss agd cosd acd nned sined tmul summed av outd").split()
        (consts, loadq, loadv, projd, qk_sb, vald, v_sb, qk, mags, halved, rounded, rest, factor, filtered, bias,
         expd, recip, weights, weights2, turned, xpose, squared, gauss, agd, cosd, acd, nned, sined, tmul, summed,
         av, outd) = (sem("l_" + n) for n in names)

        NTILE = 2 * TB
        NX = 2 * NTILE
        STEPS = 44
        SCORE = [5, 7, 9, 11] + list(range(12, 24))
        ABS, HALF, RND, REST, FILT = (1, 1, 2, 2, 3)
        PROJ, VAL = 16, 24 + STEPS
        EXP = STEPS + 3
        GAUSS = STEPS + 12
        SINE = STEPS + 28
        AV = [SINE + 6 + 8 * k // 5 for k in range(NTILE)]
        OUT = AV[-1] + 1
        EV = 2
        PACE = 2
        TURNS = EXP + 3
        DVE_ROWS = (TB // 2 - 1, TB - 1)

        block = ctx.enter_context(nc.Block())

        def over_heads(eng, iteration):
            iteration(0, 0)
            iteration(1, 1)
            with eng.Fori(1, NHEADS // 2 - 1) as i:
                iteration(2 * i, 0)
                iteration(2 * i + 1, 1)
            for t in range(NHEADS - 2, NHEADS + 2):
                iteration(t, t % 2)

        def stages(t, par, s):
            for stage in (2, 1, 0):
                g = t - stage
                if not isinstance(g, int) or 0 <= g < NHEADS:
                    yield g, (par - stage) % 2, s + STEPS * stage

        def score_bank(n):
            return banks[:, n % 4]

        def gauss_bank(d):
            return banks[:, 4 + d % 3]

        def sine_bank(k):
            return banks[:, 3 + k % 4]

        @block.sync
        def _(sp):
            def tokens(t):
                return xT_dram[:, bass.ds((t // H) * S, S)]

            def load_q(t):
                wait(sp, projd, 2 * t)
                h = t % H
                sp.dma_start(xq[0:D, :], tokens(t)).then_inc(loadq, 16)
                sp.dma_start(wqk[0:D, 0:D], Wq[:, bass.ds(h * D, D)]).then_inc(loadq, 16)
                sp.dma_start(wqk[0:D, D:P], Wk[:, bass.ds(h * D, D)]).then_inc(loadq, 16)
                sp.dma_start(wqk[D:D + 1, 0:D], bq.rearrange("(a n) -> a n", a=1)[:, bass.ds(h * D, D)]).then_inc(loadq, 16)
                sp.dma_start(wqk[D:D + 1, D:P], bk.rearrange("(a n) -> a n", a=1)[:, bass.ds(h * D, D)]).then_inc(loadq, 16)

            def load_v(t):
                wait(sp, vald, t)
                sp.dma_start(xv[0:D, :], tokens(t)).then_inc(loadv, 16)

            load_q(0)
            load_q(1)
            load_v(0)
            with sp.Fori(2, NHEADS) as t:
                load_q(t)
                load_v(t - 1)
            load_v(NHEADS - 1)

        @block.gpsimd
        def _(pool):
            nc.gpsimd.memset(xq[D:D + 1, :], 1.0).then_inc(consts, 1)
            pool.wait_ge(consts, 1)
            nc.gpsimd.memset(xv[D:D + 1, :], 1.0).then_inc(consts, 1)
            pool.wait_ge(consts, 2)
            nc.gpsimd.memset(negI[:], 0.0).then_inc(consts, 1)
            pool.wait_ge(consts, 3)
            nc.gpsimd.affine_select(out=negI[:], in_=negI[:], compare_op=ALU.not_equal, fill=-1.0,
                                    base=0, pattern=[[-1, P]], channel_multiplier=1).then_inc(consts, 1)
            nc.gpsimd.memset(halfpi[:], math.pi / 2).then_inc(consts, 1)
            pool.wait_ge(consts, 5)
            nc.gpsimd.memset(qT[D:P], 0.0).then_inc(consts, 1)
            pool.wait_ge(consts, 6)
            nc.gpsimd.memset(kT[D:P], 0.0).then_inc(consts, 1)

            def iteration(t, par):
                for s in range(STEPS):
                    for g, p, a in stages(t, par, s):
                        k = a - SINE - 5
                        if 0 <= k < NTILE:
                            wait(pool, tmul, NTILE * g + k + 1)
                            nc.gpsimd.tensor_tensor(sinb[:, k % RING], sinb[:, k % RING], work[:, k % RING],
                                                    ALU.add).then_inc(summed, 1)
                        j = a - EXP - 1
                        if 0 <= j < TB and j not in DVE_ROWS:
                            held(pool, recip, TB * g + j + 1)
                            nc.gpsimd.tensor_scalar(att[:, p, j], att[:, p, j], rs[:, j:j + 1], TURN,
                                                    ALU.mult, ALU.mult).then_inc(weights, 1)
                        if a - HALF in SCORE:
                            n = SCORE.index(a - HALF)
                            held(pool, mags, NTILE * g + n + 1)
                            nc.gpsimd.tensor_scalar(mag[:, n % 4], mag[:, n % 4], 1.0, -0.5,
                                                    ALU.mult, ALU.add).then_inc(halved, 1)
                        if a - REST in SCORE:
                            n = SCORE.index(a - REST)
                            wait(pool, rounded, NTILE * g + n + 1)
                            nc.gpsimd.tensor_tensor(wgt[:, n % 4], mag[:, n % 4], wgt[:, n % 4],
                                                    ALU.subtract).then_inc(rest, 1)

            over_heads(pool, iteration)

        @block.scalar
        def _(act):
            act.wait_ge(consts, 7)

            def projections(g, p, c):
                wait(act, projd, 2 * g + c + 1)
                if c == 0:
                    wait(act, qk, NTILE * (g - 1))
                cols = slice(c * 512, (c + 1) * 512)
                nc.scalar.activation(qT[0:D, p, cols], outp[0:D], ACT.Copy, scale=QSCALE).then_inc(qk_sb, 1)
                nc.scalar.activation(kT[0:D, p, cols], outp[D:P], ACT.Copy).then_inc(qk_sb, 1)

            projections(0, 0, 0)
            projections(0, 0, 1)

            def iteration(t, par):
                for s in range(STEPS):
                    for c in range(2):
                        if s == PROJ + EV + 2 * c and (not isinstance(t, int) or t + 1 < NHEADS):
                            projections(t + 1, 1 - par, c)
                    for g, p, a in stages(t, par, s):
                        if a == VAL + EV:
                            wait(act, vald, g + 1)
                            wait(act, av, NTILE * g)
                            nc.scalar.activation(vo[:], outp[:].rearrange("p (t d) -> p t d", d=D),
                                                 ACT.Copy, scale=1.0 / TURN).then_inc(v_sb, 1)
                        j = a - EXP
                        if 0 <= j < TB:
                            wait(act, bias, TB * g + j + 1)
                            nc.scalar.activation(att[:, p, j], att[:, p, j], ACT.Exp,
                                                 bias=nb[:, p, j:j + 1], scale=EXPSCALE,
                                                 accum_out=ssum[:, j:j + 1]).then_inc(expd, 1)
                        k = a - SINE - 1
                        if 0 <= k < NTILE:
                            wait(act, xpose, NX * g + NTILE + k + 1)
                            if k < RING:
                                wait(act, agd, NTILE * (g + 1) - RING + k + 1)
                            else:
                                wait(act, summed, NTILE * g + k - RING + 1)
                            nc.scalar.activation(work[:, k % RING], sine_bank(k), ACT.Sin,
                                                 bias=halfpi[:, 0:1], scale=-C2 / TURN).then_inc(cosd, 1)
                        k = a - SINE - 3
                        if 0 <= k < NTILE:
                            wait(act, nned, NTILE * g + k + 1)
                            wait(act, av, NTILE * g + k - RING + 1)
                            nc.scalar.activation(sinb[:, k % RING], sine_bank(k), ACT.Sin,
                                                 scale=2.0 * math.pi * (1.0 - 2.0 ** -22)).then_inc(sined, 1)
                    for g, p, a in stages(t, par, s):
                        d = a - GAUSS - 1
                        if 0 <= d < NTILE:
                            wait(act, xpose, NX * g + d + 1)
                            if d < RING:
                                wait(act, summed, NTILE * g - RING + d + 1)
                            else:
                                wait(act, agd, NTILE * g + d - RING + 1)
                            nc.scalar.activation(work[:, d % RING], gauss_bank(d), ACT.Square,
                                                 scale=1.0 / TURN).then_inc(squared, 1)
                    for g, p, a in stages(t, par, s):
                        if a - ABS in SCORE:
                            n = SCORE.index(a - ABS)
                            wait(act, qk, NTILE * g + n + 1)
                            wait(act, rest, NTILE * g + n - 3)
                            nc.scalar.activation(mag[:, n % 4], score_bank(n), ACT.Abs).then_inc(mags, 1)
                    for g, p, a in stages(t, par, s):
                        d = a - GAUSS - 1
                        if 0 <= d < NTILE:
                            wait(act, squared, NTILE * g + d + 1)
                            nc.scalar.activation(work[:, d % RING], work[:, d % RING], ACT.Exp,
                                                 scale=-1.0 / PHI).then_inc(gauss, 1)

            over_heads(act, iteration)

        @block.vector
        def _(dve):
            def iteration(t, par):
                for s in range(STEPS):
                    for g, p, a in stages(t, par, s):
                        k = a - SINE - 2
                        if 0 <= k < NTILE:
                            wait(dve, cosd, NTILE * g + k + 1)
                            nc.vector.tensor_tensor(work[:, k % RING], sine_bank(k), work[:, k % RING],
                                                    ALU.mult).then_inc(acd, 1)
                        k = a - SINE - 4
                        if 0 <= k < NTILE:
                            wait(dve, sined, NTILE * g + k + 1)
                            nc.vector.tensor_tensor(sinb[:, k % RING], sinb[:, k % RING], ag[:, k],
                                                    ALU.mult).then_inc(tmul, 1)
                        if a == OUT:
                            wait(dve, av, NTILE * (g + 1))
                            hv = hres[:, bass.ds((g // H) * TB, TB), :]
                            nc.vector.tensor_tensor(hv, outp[:].rearrange("p (t d) -> p t d", d=D), hv,
                                                    ALU.add).then_inc(outd, 1)
                        j = a - EXP - 1
                        if 0 <= j < TB:
                            wait(dve, expd, TB * g + j + 1)
                            nc.vector.reciprocal(rs[:, j:j + 1], ssum[:, j:j + 1]).then_inc(recip, 1)
                        if a - RND in SCORE:
                            n = SCORE.index(a - RND)
                            wait(dve, halved, NTILE * g + n + 1)
                            nc.vector.tensor_scalar(wgt[:, n % 4], mag[:, n % 4], ROUND, -ROUND,
                                                    ALU.add, ALU.add).then_inc(rounded, 1)
                        if a - FILT in SCORE:
                            n = SCORE.index(a - FILT)
                            wait(dve, rest, NTILE * g + n + 1)
                            nc.vector.tensor_scalar(wgt[:, n % 4], wgt[:, n % 4], 1.0 / 3.0 - 0.5, PHI,
                                                    ALU.is_ge, ALU.add).then_inc(factor, 1)
                    for g, p, a in stages(t, par, s):
                        d = a - GAUSS - 2
                        if 0 <= d < NTILE:
                            wait(dve, gauss, NTILE * g + d + 1)
                            nc.vector.tensor_tensor(ag[:, d], gauss_bank(d), work[:, d % RING],
                                                    ALU.mult).then_inc(agd, 1)
                        j = a - EXP - 1
                        if j in DVE_ROWS:
                            wait(dve, recip, TB * g + j + 1)
                            nc.vector.tensor_scalar(att[:, p, j], att[:, p, j], rs[:, j:j + 1], TURN,
                                                    ALU.mult, ALU.mult).then_inc(weights2, 1)
                        j = a - TURNS
                        if 0 <= j < TB:
                            if j in DVE_ROWS:
                                wait(dve, weights2, 2 * g + j // 4 + 1)
                            else:
                                wait(dve, weights, (TB - 2) * g + j + 1 - j // 4)
                            wait(dve, nned, NTILE * g)
                            nc.vector.tensor_scalar(nturn[:, j], att[:, p, j], ROUND, -ROUND,
                                                    ALU.add, ALU.add).then_inc(turned, 1)
                    for g, p, a in stages(t, par, s):
                        if a - FILT in SCORE:
                            n = SCORE.index(a - FILT)
                            u, c = n // 2, n % 2
                            wait(dve, factor, NTILE * g + n + 1)
                            wait(dve, filtered, NTILE * g + n)
                            wait(dve, xpose, NX * (g - 1))
                            dve.nop(nofuse=True)
                            nc.vector.tensor_tensor_reduce(
                                att[:, p, u, c * 512:(c + 1) * 512], wgt[:, n % 4], score_bank(n), 1.0,
                                mx[:, p, n - 1:n] if c else -3.0e38, ALU.mult, ALU.max,
                                mx[:, p, n:n + 1]).then_inc(filtered, 1)
                        if a - FILT - 1 in SCORE and SCORE.index(a - FILT - 1) % 2 == 1:
                            n = SCORE.index(a - FILT - 1)
                            u = n // 2
                            wait(dve, filtered, NTILE * g + n + 1)
                            nc.vector.tensor_scalar(nb[:, p, u:u + 1], mx[:, p, n:n + 1], -EXPSCALE, None,
                                                    ALU.mult).then_inc(bias, 1)

            over_heads(dve, iteration)

        @block.tensor
        def _(pe):
            pe.wait_ge(consts, 7)

            def project(g, c):
                wait(pe, loadq, 80 * (g + 1))
                if c == 0:
                    wait(pe, outd, g - 2)
                else:
                    wait(pe, qk_sb, 4 * g + 2)
                nc.tensor.matmul(outp[:], wqk[:], xq[:, c * 512:(c + 1) * 512], start=True, stop=True).then_inc(projd, 1)

            project(0, 0)
            project(0, 1)

            def fill(g, p, bank, kt, half):
                wait(pe, weights, (TB - 2) * g + (TB // 2 - 1) * (half + 1))
                wait(pe, weights2, 2 * g + half + 1)
                for i in range(4):
                    mm = nc.tensor.matmul(bank[:, i * P:(i + 1) * P],
                                          att[:, p, 4 * half + i, kt * P:(kt + 1) * P], ident[:],
                                          is_transpose=True, start=(i == 0), stop=(i == 3), skip_group_check=True)
                mm.then_inc(xpose, 1)

            def iteration(t, par):
                for s in range(STEPS):
                    for g, p, a in stages(t, par, s):
                        k = a - SINE - 3
                        if 0 <= k < NTILE:
                            wait(pe, acd, NTILE * g + k + 1)
                            wait(pe, turned, TB * (g + 1))
                            kt, half = k // 2, k % 2
                            for i in range(4):
                                mm = nc.tensor.matmul(sine_bank(k)[:, i * P:(i + 1) * P],
                                                      nturn[:, 4 * half + i, kt * P:(kt + 1) * P], negI[:],
                                                      start=False, stop=True, skip_group_check=True)
                            mm.then_inc(nned, 1)
                        if a in SCORE:
                            n = SCORE.index(a)
                            if n < 2:
                                wait(pe, qk_sb, 4 * (g + 1))
                            wait(pe, filtered, NTILE * g + n - 3)
                            if n == 3:
                                wait(pe, sined, NTILE * (g - 2) + 13)
                            nc.tensor.matmul(score_bank(n), qT[:, p, (n // 2) * P:(n // 2 + 1) * P],
                                             kT[:, p, (n % 2) * 512:(n % 2 + 1) * 512],
                                             start=True, stop=True).then_inc(qk, 1)
                        j = a - EXP - PACE
                        if 0 <= j < TB:
                            wait(pe, expd, TB * g + j + 1)
                        d = a - GAUSS
                        if 0 <= d < NTILE:
                            if d < 3:
                                wait(pe, sined, NTILE * (g - 1) + 14 + d)
                            else:
                                wait(pe, agd, NTILE * g + d - 2)
                            fill(g, p, gauss_bank(d), d // 2, d % 2)
                        k = a - SINE
                        if 0 <= k < NTILE:
                            if k == 0:
                                last = isinstance(g, int) and g == NHEADS - 1
                                wait(pe, filtered, NTILE * (g + 1 if last else g + 2))
                            elif k < 4:
                                wait(pe, agd, NTILE * g + (16, 14, 15)[k - 1])
                            else:
                                wait(pe, sined, NTILE * g + k - 3)
                            fill(g, p, sine_bank(k), k // 2, k % 2)
                        if a in AV:
                            k = AV.index(a)
                            wait(pe, summed, NTILE * g + k + 1)
                            if k == 0:
                                wait(pe, v_sb, g + 1)
                            kt, half = k // 2, k % 2
                            for i in range(4):
                                o = (4 * half + i) * D
                                mm = nc.tensor.matmul(outp[:, o:o + D], sinb[:, k % RING, i * P:(i + 1) * P],
                                                      vo[:, kt, :], start=(k == 0 and i == 0),
                                                      stop=(k >= NTILE - 2), skip_group_check=True)
                            mm.then_inc(av, 1)
                        if a == VAL:
                            wait(pe, loadv, 16 * (g + 1))
                            last = isinstance(g, int) and g + 2 >= NHEADS
                            wait(pe, qk_sb, 4 * NHEADS if last else 4 * (g + 3))
                            wait(pe, outd, g)
                            for j in range(TB):
                                mm = nc.tensor.matmul(outp[:, j * D:(j + 1) * D], xv[:, j * P:(j + 1) * P],
                                                      wvo[:, bass.ds((g % H) * D, D)], start=True, stop=True)
                            mm.then_inc(vald, 1)
                    for c in range(2):
                        if s == PROJ + 2 * c and (not isinstance(t, int) or t + 1 < NHEADS):
                            project(t + 1, c)

            over_heads(pe, iteration)


NH, NKV, HD = 4, 2, 16
NE, HID = 8, 170
HC = HID // 2
EPS_RMS = 1e-6


def over_batches(eng, body):
    body(0)
    with eng.Fori(1, B) as b:
        body(b)


def causal(nc, ident, hres, x2, wqk4, wvT, woT, ln1, cosT, sinT):
    with ExitStack() as ctx:
        def sb(name, shape, dt=F32):
            return ctx.enter_context(nc.sbuf_tensor(name, shape, dt))

        sq = sb("c_sq", [P, NT, D])
        s1, mean, s2, var, std, rstd = (sb("c_" + n, [P, NT]) for n in ("s1", "mean", "s2", "var", "std", "rstd"))
        ms, rms, rinv = (sb("c_" + n, [P, NT]) for n in ("ms", "rms", "rinv"))
        lnw = sb("lnw1", [D, 1])
        wqk = sb("c_wqk", [D, 4, P])
        wv = sb("c_wv", [D, NKV * HD])
        wo = sb("c_wo", [D, D])
        cs = sb("c_cs", [P, S])
        sn = sb("c_sn", [P, S])
        mask = sb("c_mask", [P, P])
        xs = sb("c_xs", [P, TB, D])
        xsT = sb("c_xsT", [D, S])
        q_r = sb("c_q", [P, S])
        k_r = sb("c_k", [P, S])
        q_s = sb("c_qs", [P, S])
        k_s = sb("c_ks", [P, S])
        v = sb("c_v", [P, TB, NKV * HD])
        pr = sb("c_pr", [P, 2, S])
        prT = sb("c_prT", [P, 2, S])
        m = sb("c_m", [P, 4 * TB])
        nm = sb("c_nm", [P, 4 * TB])
        sm = sb("c_sm", [P, 4 * TB])
        rs = sb("c_rs", [P, 4 * TB])
        y = sb("c_y", [P, TB, D])
        yT = sb("c_yT", [D, S])

        sc = ctx.enter_context(nc.psum_tensor("c_sc", [P, 2, S], F32))
        pt = ctx.enter_context(nc.psum_tensor("c_pt", [P, 3, 512], F32))
        yp = ctx.enter_context(nc.psum_tensor("c_yp", [P, 512], F32))

        names = ("w_in consts wmul ln sqd rooted scaled xT xT_sb proj cosd sind roped pt_done pt_sb sc_done "
                 "masked maxed negd expd yd recip ynorm wo_add").split()
        (w_in, consts, wmul, ln, sqd, rooted, scaled, xT, xT_sb, proj, cosd, sind, roped, pt_done, pt_sb, sc_done,
         masked, maxed, negd, expd, yd, recip, ynorm, wo_add) = (ctx.enter_context(nc.semaphore("c_" + n)) for n in names)

        UNITS = [(qt, h) for qt in range(TB) for h in range(NH)]
        NU = len(UNITS)
        GROUPS = [(n, g) for n, (qt, h) in enumerate(UNITS) for g in range(qt // 4 + 1)]
        USE_V, USE_G, USE_YT, USE_WO = 0, 1, 1 + len(GROUPS), 3 + len(GROUPS)
        NSB = 3 + len(GROUPS)
        FIRST = {n: GROUPS.index((n, 0)) for n in range(NU)}
        LAST = {n: FIRST[n] + UNITS[n][0] // 4 for n in range(NU)}

        block = ctx.enter_context(nc.Block())

        @block.sync
        def _(sp):
            for dst, src in ((wqk[:], wqk4), (wv[:], wvT), (wo[:], woT), (cs[:], cosT), (sn[:], sinT),
                             (lnw[:], ln1.rearrange("(p a) -> p a", a=1))):
                sp.dma_start(dst, src).then_inc(w_in, 16)
            sp.wait_ge(w_in, 96)

        @block.gpsimd
        def _(pool):
            nc.gpsimd.memset(mask[:], 0.0).then_inc(consts, 1)
            pool.wait_ge(consts, 1)
            nc.gpsimd.affine_select(out=mask[:], in_=mask[:], compare_op=ALU.is_ge, fill=-1e30,
                                    base=0, pattern=[[-1, P]], channel_multiplier=1).then_inc(consts, 1)

            def body(b):
                wait(pool, sind, 2 * b + 1)
                nc.gpsimd.tensor_tensor(q_r[:], q_r[:], q_s[:], ALU.add).then_inc(roped, 1)
                wait(pool, sind, 2 * b + 2)
                nc.gpsimd.tensor_tensor(k_r[:], k_r[:], k_s[:], ALU.add).then_inc(roped, 1)
            over_batches(pool, body)

        @block.scalar
        def _(act):
            act.wait_ge(ln, 3)
            nc.scalar.activation(sq[:], x2[:], ACT.Square).then_inc(sqd, 1)
            act.wait_ge(ln, 5)
            nc.scalar.activation(std[:], var[:], ACT.Sqrt).then_inc(rooted, 1)
            act.wait_ge(ln, 7)
            nc.scalar.activation(sq[:], x2[:], ACT.Square).then_inc(sqd, 1)
            act.wait_ge(ln, 9)
            nc.scalar.activation(rms[:], ms[:], ACT.Sqrt).then_inc(rooted, 1)

            def body(b):
                wait(act, xT, b + 1)
                wait(act, proj, 5 * b)
                nc.scalar.activation(xsT[:], sc[0:D, 0], ACT.Copy).then_inc(xT_sb, 1)
                wait(act, pt_done, 52 * b + USE_V + 1)
                nc.scalar.activation(v[:], pt[:, 0, 0:TB * NKV * HD].rearrange("p (t d) -> p t d", t=TB),
                                     ACT.Copy).then_inc(pt_sb, 1)

                def expo(n):
                    qt = UNITS[n][0]
                    wait(act, negd, NU * b + n + 1)
                    wait(act, pt_done, 52 * b + (USE_G + LAST[n - 2] + 1 if n >= 2 else 0))
                    nc.scalar.activation(pr[:, n % 2, 0:(qt + 1) * P], sc[:, n % 2, 0:(qt + 1) * P], ACT.Exp,
                                         bias=nm[:, n:n + 1], scale=1.0 / math.sqrt(HD),
                                         accum_out=sm[:, n:n + 1]).then_inc(expd, 1)

                expo(0)
                for n in range(NU):
                    if n + 1 < NU:
                        expo(n + 1)
                    qt = UNITS[n][0]
                    for g in range(qt // 4 + 1):
                        use = USE_G + FIRST[n] + g
                        wid = (min(qt, 4 * g + 3) - 4 * g + 1) * P
                        wait(act, pt_done, 52 * b + use + 1)
                        wait(act, yd, NU * b + n - 1)
                        nc.scalar.activation(prT[:, n % 2, g * 512:g * 512 + wid], pt[:, use % 3, 0:wid],
                                             ACT.Copy).then_inc(pt_sb, 1)
                for i in range(2):
                    use = USE_YT + i
                    wait(act, pt_done, 52 * b + use + 1)
                    nc.scalar.activation(yT[:, i * 512:(i + 1) * 512], pt[0:D, use % 3], ACT.Copy).then_inc(pt_sb, 1)
            over_batches(act, body)

        @block.vector
        def _(dve):
            dve.wait_ge(w_in, 96)
            nc.vector.tensor_scalar(wqk[:], wqk[:], lnw[:, 0:1], None, ALU.mult).then_inc(wmul, 1)
            nc.vector.tensor_scalar(wv[:], wv[:], lnw[:, 0:1], None, ALU.mult).then_inc(wmul, 1)
            nc.vector.tensor_reduce(s1[:], hres[:], AX, ALU.add).then_inc(ln, 1)
            dve.wait_ge(ln, 1)
            nc.vector.tensor_scalar(mean[:], s1[:], 1.0 / D, None, ALU.mult).then_inc(ln, 1)
            dve.wait_ge(ln, 2)
            nc.vector.tensor_tensor(x2[:], hres[:], mean[:].unsqueeze(2).to_broadcast([P, NT, D]),
                                    ALU.subtract).then_inc(ln, 1)
            dve.wait_ge(sqd, 1)
            nc.vector.tensor_reduce(s2[:], sq[:], AX, ALU.add).then_inc(ln, 1)
            dve.wait_ge(ln, 4)
            nc.vector.tensor_scalar(var[:], s2[:], 1.0 / D, EPS, ALU.mult, ALU.add).then_inc(ln, 1)
            dve.wait_ge(rooted, 1)
            nc.vector.reciprocal(rstd[:], std[:]).then_inc(ln, 1)
            dve.wait_ge(ln, 6)
            nc.vector.tensor_tensor(x2[:], x2[:], rstd[:].unsqueeze(2).to_broadcast([P, NT, D]),
                                    ALU.mult).then_inc(ln, 1)
            dve.wait_ge(sqd, 2)
            nc.vector.tensor_reduce(s2[:], sq[:], AX, ALU.add).then_inc(ln, 1)
            dve.wait_ge(ln, 8)
            nc.vector.tensor_scalar(ms[:], s2[:], 1.0 / D, EPS_RMS, ALU.mult, ALU.add).then_inc(ln, 1)
            dve.wait_ge(rooted, 2)
            nc.vector.reciprocal(rinv[:], rms[:]).then_inc(ln, 1)
            dve.wait_ge(ln, 10)
            dve.wait_ge(consts, 2)

            def body(b):
                wait(dve, xT, b)
                nc.vector.tensor_tensor(xs[:], x2[:, bass.ds(b * TB, TB), :],
                                        rinv[:, bass.ds(b * TB, TB)].unsqueeze(2).to_broadcast([P, TB, D]),
                                        ALU.mult).then_inc(scaled, 1)
                for i, (dst, tab, done) in enumerate(((q_r, cs, cosd), (q_s, sn, sind), (k_r, cs, cosd), (k_s, sn, sind))):
                    wait(dve, proj, 5 * b + i + 1)
                    wait(dve, sc_done, NU * b)
                    wait(dve, roped, 2 * b)
                    nc.vector.tensor_tensor(dst[:], sc[:, (i + 1) % 2], tab[:], ALU.mult).then_inc(done, 1)

                def top(n):
                    qt = UNITS[n][0]
                    wait(dve, sc_done, NU * b + n + 1)
                    dg = sc[:, n % 2, qt * P:(qt + 1) * P]
                    nc.vector.tensor_tensor(dg, dg, mask[:], ALU.add).then_inc(masked, 1)
                    wait(dve, masked, NU * b + n + 1)
                    nc.vector.tensor_reduce(m[:, n:n + 1], sc[:, n % 2, 0:(qt + 1) * P], AX, ALU.max).then_inc(maxed, 1)
                    wait(dve, maxed, NU * b + n + 1)
                    wait(dve, expd, NU * b)
                    nc.vector.tensor_scalar(nm[:, n:n + 1], m[:, n:n + 1], -1.0 / math.sqrt(HD), None,
                                            ALU.mult).then_inc(negd, 1)

                def norm(n):
                    qt, h = UNITS[n]
                    wait(dve, expd, NU * b + n + 1)
                    nc.vector.reciprocal(rs[:, n:n + 1], sm[:, n:n + 1]).then_inc(recip, 1)
                    wait(dve, recip, NU * b + n + 1)
                    wait(dve, yd, NU * b + n + 1)
                    wait(dve, pt_done, 52 * b)
                    nc.vector.tensor_scalar(y[:, qt, h * HD:(h + 1) * HD], yp[:, 0:HD], rs[:, n:n + 1], None,
                                            ALU.mult).then_inc(ynorm, 1)

                for n in range(NU + 2):
                    if n < NU:
                        top(n)
                    if n >= 2:
                        norm(n - 2)
                wait(dve, pt_done, 52 * (b + 1))
                xv = x2[:, bass.ds(b * TB, TB), :]
                hv = hres[:, bass.ds(b * TB, TB), :]
                nc.vector.tensor_tensor(xv, pt[:, USE_WO % 3].rearrange("p (t d) -> p t d", d=D), xv,
                                        ALU.add).then_inc(wo_add, 1)
                wait(dve, wo_add, 2 * b + 1)
                nc.vector.tensor_tensor(hv, hv, xv, ALU.add).then_inc(wo_add, 1)
            over_batches(dve, body)

        @block.tensor
        def _(pe):
            pe.wait_ge(wmul, 2)

            def body(b):
                wait(pe, expd, NU * b)
                wait(pe, scaled, b + 1)
                pe.nop(nofuse=True)
                for t in range(TB):
                    mm = nc.tensor.transpose(sc[0:D, 0, t * P:(t + 1) * P], xs[:, t, :], ident[:])
                mm.then_inc(xT, 1)
                wait(pe, xT_sb, b + 1)
                for i in range(4):
                    if i >= 2:
                        wait(pe, (cosd, sind)[i - 2], 2 * b + 1)
                    for c in range(2):
                        mm = nc.tensor.matmul(sc[:, (i + 1) % 2, c * 512:(c + 1) * 512], wqk[:, i],
                                              xsT[:, c * 512:(c + 1) * 512], start=True, stop=True)
                    mm.then_inc(proj, 1)
                wait(pe, wo_add, 2 * b)
                for t in range(TB):
                    mm = nc.tensor.matmul(pt[:, 0, t * NKV * HD:(t + 1) * NKV * HD], xsT[:, t * P:(t + 1) * P],
                                          wv[:], start=True, stop=True)
                mm.then_inc(pt_done, 1)
                mm = nc.tensor.matmul(pt[:, 1, 0:NKV * HD], xsT[:, 0:P], wv[:], start=True, stop=True)
                mm.then_inc(proj, 1)
                wait(pe, roped, 2 * b + 2)
                wait(pe, cosd, 2 * b + 2)
                wait(pe, pt_sb, NSB * b + 1)

                def score(n):
                    qt, h = UNITS[n]
                    if n >= 2:
                        wait(pe, expd, NU * b + n - 1)
                    pe.nop(nofuse=True)
                    r = slice(32 * h, 32 * h + HD)
                    for c in range(0, (qt + 1) * P, 512):
                        e = min(c + 512, (qt + 1) * P)
                        mm = nc.tensor.matmul(sc[:, n % 2, c:e], q_r[r, qt * P:(qt + 1) * P], k_r[r, c:e],
                                              start=True, stop=True)
                    mm.then_inc(sc_done, 1)

                def turn(n):
                    qt = UNITS[n][0]
                    wait(pe, expd, NU * b + n + 1)
                    for g in range(qt // 4 + 1):
                        use = USE_G + FIRST[n] + g
                        wait(pe, pt_sb, NSB * b + max(use - 2, 1))
                        for kt in range(4 * g, min(qt, 4 * g + 3) + 1):
                            mm = nc.tensor.transpose(pt[:, use % 3, (kt - 4 * g) * P:(kt - 4 * g + 1) * P],
                                                     pr[:, n % 2, kt * P:(kt + 1) * P], ident[:])
                        mm.then_inc(pt_done, 1)

                def apply(n):
                    qt, h = UNITS[n]
                    wait(pe, pt_sb, NSB * b + USE_G + LAST[n] + 1)
                    wait(pe, ynorm, NU * b + n)
                    pe.nop(nofuse=True)
                    kv = h // (NH // NKV) * HD
                    for kt in range(qt + 1):
                        mm = nc.tensor.matmul(yp[:, 0:HD], prT[:, n % 2, kt * P:(kt + 1) * P],
                                              v[:, kt, kv:kv + HD], start=(kt == 0), stop=(kt == qt))
                    mm.then_inc(yd, 1)

                for n in range(NU + 2):
                    if n < NU:
                        score(n)
                    if 1 <= n <= NU:
                        turn(n - 1)
                    if n >= 2:
                        apply(n - 2)
                wait(pe, ynorm, NU * (b + 1))
                for i in range(2):
                    use = USE_YT + i
                    wait(pe, pt_sb, NSB * b + use - 2)
                    pe.nop(nofuse=True)
                    for t in range(4):
                        mm = nc.tensor.transpose(pt[0:D, use % 3, t * P:(t + 1) * P], y[:, 4 * i + t, :], ident[:])
                    mm.then_inc(pt_done, 1)
                wait(pe, pt_sb, NSB * (b + 1))
                pe.nop(nofuse=True)
                for t in range(TB):
                    mm = nc.tensor.matmul(pt[:, USE_WO % 3, t * D:(t + 1) * D], yT[:, t * P:(t + 1) * P], wo[:],
                                          start=True, stop=True)
                mm.then_inc(pt_done, 1)
            assert USE_WO + 1 == 52 and NSB == 51
            over_batches(pe, body)


def experts(nc, ident, hres, x3, router, w1T, w3T, w2T, ln2, out):
    with ExitStack() as ctx:
        def sb(name, shape, dt=F32):
            return ctx.enter_context(nc.sbuf_tensor(name, shape, dt))

        sq = sb("e_sq", [P, NT, D])
        s2, ms, rms, rinv = (sb("e_" + n, [P, NT]) for n in ("s2", "ms", "rms", "rinv"))
        lnw = sb("lnw2", [D, 1])
        rt = sb("e_rt", [D, NE])
        w1 = sb("e_w1", [D, NE, 2, HC])
        w3 = sb("e_w3", [D, NE, 2, HC])
        w2 = sb("e_w2", [HC, NE, 2, D])
        rank = sb("e_rank", [P, TB, NE])
        rank_i = sb("e_ranki", [P, TB, NE], I32)
        xs = sb("e_xs", [P, TB, D])
        xT = sb("e_xT", [D, S])
        prob = sb("e_prob", [P, TB, NE])
        hot1 = sb("e_hot1", [P, TB, NE])
        hot2 = sb("e_hot2", [P, TB, NE])
        tmp = sb("e_tmp", [P, TB, NE])
        wts = sb("e_wts", [P, TB, NE])
        c1, c2, c3, m1, m2 = (sb("e_" + n, [P, TB]) for n in ("c1", "c2", "c3", "m1", "m2"))
        sl = sb("e_sl", [HC, 3, 512])
        hh = sb("e_hh", [HC, 2, 2, S])
        wout = sb("e_wout", [P, 2, TB, D])

        hp = ctx.enter_context(nc.psum_tensor("e_hp", [P, 3, 2, 512], F32))
        op = ctx.enter_context(nc.psum_tensor("e_op", [P, 2, 512], F32))

        names = ("w_in ranked wmul rm sqd rooted scaled xTd xT_sb logit routed lexp hpd silud hhd opd woutd added out_dma").split()
        (w_in, ranked, wmul, rm, sqd, rooted, scaled, xTd, xT_sb, logit, routed, lexp, hpd, silud, hhd, opd, woutd,
         added, out_dma) = (ctx.enter_context(nc.semaphore("e_" + n)) for n in names)

        UNITS = [(e, c, half) for e in range(NE) for c in range(2) for half in range(2)]
        NU = len(UNITS)
        NR = 20

        block = ctx.enter_context(nc.Block())
        out_v = out.rearrange("b (t p) d -> b p t d", p=P)

        @block.sync
        def _(sp):
            for dst, src in ((rt[:], router), (w1[:], w1T), (w3[:], w3T), (w2[:], w2T),
                             (lnw[:], ln2.rearrange("(p a) -> p a", a=1))):
                sp.dma_start(dst, src).then_inc(w_in, 16)
            sp.wait_ge(w_in, 80)

            def body(b):
                wait(sp, added, NE * (b + 1))
                sp.dma_start(out_v[bass.ds(b, 1)].rearrange("a p t d -> (a p) t d"),
                             hres[:, bass.ds(b * TB, TB), :]).then_inc(out_dma, 16)
            over_batches(sp, body)
            sp.wait_ge(out_dma, 16 * B)

        @block.gpsimd
        def _(pool):
            nc.gpsimd.iota(rank_i[:], pattern=[[0, TB], [-1, NE]], base=NE, channel_multiplier=0).then_inc(ranked, 1)

            def body(b):
                for e in range(NE):
                    wait(pool, woutd, NE * b + e + 1)
                    wait(pool, added, NE * b + e)
                    pool.nop(nofuse=True)
                    hv = hres[:, bass.ds(b * TB, TB), :]
                    nc.gpsimd.tensor_tensor(hv, hv, wout[:, e % 2], ALU.add).then_inc(added, 1)
            over_batches(pool, body)

        @block.scalar
        def _(act):
            nc.scalar.activation(sq[:], x3[:], ACT.Square).then_inc(sqd, 1)
            act.wait_ge(rm, 2)
            nc.scalar.activation(rms[:], ms[:], ACT.Sqrt).then_inc(rooted, 1)

            def body(b):
                wait(act, xTd, b + 1)
                wait(act, hpd, NU * b)
                nc.scalar.activation(xT[:], hp[0:D, 0].rearrange("p a n -> p (a n)"), ACT.Copy).then_inc(xT_sb, 1)
                wait(act, routed, NR * b + 2)
                nc.scalar.activation(prob[:], prob[:], ACT.Exp).then_inc(lexp, 1)
                for n in range(NU):
                    wait(act, hpd, NU * b + n + 1)
                    wait(act, hhd, NU * b + n - 2)
                    nc.scalar.activation(sl[:, n % 3], hp[0:HC, n % 3, 0], ACT.Silu).then_inc(silud, 1)
            over_batches(act, body)

        @block.vector
        def _(dve):
            dve.wait_ge(w_in, 80)
            for t in (rt, w1, w3):
                nc.vector.tensor_scalar(t[:], t[:], lnw[:, 0:1], None, ALU.mult).then_inc(wmul, 1)
            dve.wait_ge(ranked, 1)
            nc.vector.tensor_copy(rank[:], rank_i[:]).then_inc(wmul, 1)
            dve.wait_ge(sqd, 1)
            nc.vector.tensor_reduce(s2[:], sq[:], AX, ALU.add).then_inc(rm, 1)
            dve.wait_ge(rm, 1)
            nc.vector.tensor_scalar(ms[:], s2[:], 1.0 / D, EPS_RMS, ALU.mult, ALU.add).then_inc(rm, 1)
            dve.wait_ge(rooted, 1)
            nc.vector.reciprocal(rinv[:], rms[:]).then_inc(rm, 1)
            dve.wait_ge(rm, 3)
            dve.wait_ge(wmul, 4)

            def body(b):
                wait(dve, xTd, b)
                nc.vector.tensor_tensor(xs[:], x3[:, bass.ds(b * TB, TB), :],
                                        rinv[:, bass.ds(b * TB, TB)].unsqueeze(2).to_broadcast([P, TB, D]),
                                        ALU.mult).then_inc(scaled, 1)
                step = [0]

                def did(ins):
                    step[0] += 1
                    ins.then_inc(routed, 1)
                    wait(dve, routed, NR * b + step[0])

                def wide(x):
                    return x[:].unsqueeze(2).to_broadcast([P, TB, NE])

                V = nc.vector
                lg = op[:, 0, 0:TB * NE].rearrange("p (t e) -> p t e", e=NE)
                wait(dve, logit, b + 1)
                did(V.tensor_reduce(c1[:], lg, AX, ALU.max))
                did(V.tensor_tensor(prob[:], lg, wide(c1), ALU.subtract))
                wait(dve, lexp, b + 1)
                did(V.tensor_reduce(c2[:], prob[:], AX, ALU.add))
                did(V.reciprocal(c3[:], c2[:]))
                did(V.tensor_tensor(prob[:], prob[:], wide(c3), ALU.mult))
                for m, hot, c in ((m1, hot1, c1), (m2, hot2, c2)):
                    did(V.tensor_reduce(m[:], prob[:], AX, ALU.max))
                    did(V.tensor_tensor(tmp[:], prob[:], wide(m), ALU.is_equal))
                    did(V.tensor_tensor(tmp[:], tmp[:], rank[:], ALU.mult))
                    did(V.tensor_reduce(c[:], tmp[:], AX, ALU.max))
                    did(V.tensor_tensor(hot[:], tmp[:], wide(c), ALU.is_equal))
                    if m is m1:
                        did(V.scalar_tensor_tensor(out=prob[:], in0=hot[:], scalar=-4.0, in1=prob[:],
                                                   op0=ALU.mult, op1=ALU.add))
                did(V.scalar_tensor_tensor(out=c3[:], in0=m1[:], scalar=1e-9, in1=m2[:], op0=ALU.add, op1=ALU.add))
                did(V.reciprocal(c1[:], c3[:]))
                V.tensor_tensor(m1[:], m1[:], c1[:], ALU.mult)
                did(V.tensor_tensor(m2[:], m2[:], c1[:], ALU.mult))
                did(V.tensor_tensor(hot1[:], hot1[:], wide(m1), ALU.mult))
                assert step[0] == NR, step[0]
                finish_routing(b)

                for n in range(NU):
                    e, c, half = UNITS[n]
                    wait(dve, silud, NU * b + n + 1)
                    if e >= 2:
                        wait(dve, opd, NE * b + e - 1)
                    else:
                        wait(dve, opd, NE * b)
                    nc.vector.tensor_tensor(hh[:, e % 2, c, half * 512:(half + 1) * 512], hp[0:HC, n % 3, 1],
                                            sl[:, n % 3], ALU.mult).then_inc(hhd, 1)
                    if n % 4 == 1 and e >= 1:
                        weigh(b, e - 1)
                weigh(b, NE - 1)

            def finish_routing(b):
                nc.vector.tensor_tensor(hot2[:], hot2[:], m2[:].unsqueeze(2).to_broadcast([P, TB, NE]),
                                        ALU.mult).then_inc(rm, 1)
                wait(dve, rm, 2 * b + 4)
                nc.vector.tensor_tensor(wts[:], hot1[:], hot2[:], ALU.add).then_inc(rm, 1)
                wait(dve, rm, 2 * b + 5)

            def weigh(b, e):
                wait(dve, opd, NE * b + e + 1)
                wait(dve, added, NE * b + e - 1)
                nc.vector.tensor_tensor(wout[:, e % 2], op[:, e % 2].rearrange("p (t d) -> p t d", d=D),
                                        wts[:, :, e:e + 1].to_broadcast([P, TB, D]), ALU.mult).then_inc(woutd, 1)
            over_batches(dve, body)

        @block.tensor
        def _(pe):
            pe.wait_ge(wmul, 3)

            def body(b):
                wait(pe, hhd, NU * b)
                wait(pe, scaled, b + 1)
                pe.nop(nofuse=True)
                tv = hp[0:D, 0].rearrange("p a n -> p (a n)")
                for t in range(TB):
                    mm = nc.tensor.transpose(tv[:, t * P:(t + 1) * P], xs[:, t, :], ident[:])
                mm.then_inc(xTd, 1)
                wait(pe, xT_sb, b + 1)
                wait(pe, woutd, NE * b)
                pe.nop(nofuse=True)
                for t in range(TB):
                    mm = nc.tensor.matmul(op[:, 0, t * NE:(t + 1) * NE], xT[:, t * P:(t + 1) * P], rt[:],
                                          start=True, stop=True)
                mm.then_inc(logit, 1)

                def up(n):
                    e, c, half = UNITS[n]
                    wait(pe, hhd, NU * b + n - 2)
                    pe.nop(nofuse=True)
                    nc.tensor.matmul(hp[0:HC, n % 3, 0], w1[:, e, c], xT[:, half * 512:(half + 1) * 512],
                                     start=True, stop=True)
                    nc.tensor.matmul(hp[0:HC, n % 3, 1], w3[:, e, c], xT[:, half * 512:(half + 1) * 512],
                                     start=True, stop=True).then_inc(hpd, 1)

                def down(e):
                    wait(pe, hhd, NU * b + 4 * (e + 1))
                    if e == 0:
                        wait(pe, routed, NR * b + 2)
                    wait(pe, woutd, NE * b + max(e - 1, 0))
                    pe.nop(nofuse=True)
                    for t in range(TB):
                        for c in range(2):
                            mm = nc.tensor.matmul(op[:, e % 2, t * D:(t + 1) * D], hh[:, e % 2, c, t * P:(t + 1) * P],
                                                  w2[:, e, c], start=(c == 0), stop=(c == 1))
                    mm.then_inc(opd, 1)

                for n in range(NU):
                    up(n)
                    if n % 4 == 3 and n > 4:
                        down(n // 4 - 1)
                down(NE - 1)
            over_batches(pe, body)


def tower(nc, a, out):
    with ExitStack() as ctx:
        ident = ctx.enter_context(nc.sbuf_tensor("ident", [P, P], F32))
        hres = ctx.enter_context(nc.sbuf_tensor("hres", [P, NT, D], F32))
        wvo = ctx.enter_context(nc.sbuf_tensor("wvo", [D + 1, H * D], F32))
        xT_dram = nc.dram_tensor("xT_dram", (D, B * S), F32, kind="Internal").ap()
        made = ctx.enter_context(nc.semaphore("made"))
        with nc.Block() as block:
            @block.gpsimd
            def _(pool):
                nc.gpsimd.memset(ident[:], 0.0).then_inc(made, 1)
                pool.wait_ge(made, 1)
                nc.gpsimd.affine_select(out=ident[:], in_=ident[:], compare_op=ALU.not_equal, fill=1.0,
                                        base=0, pattern=[[-1, P]], channel_multiplier=1).then_inc(made, 1)
                pool.wait_ge(made, 2)
        embed(nc, ident, hres, xT_dram, wvo, a["x"], a["L0_tok_turns"], a["L0_tok_poly_coeffs"],
              a["L0_attn_Wv"], a["L0_attn_bv"], a["L0_attn_Wo"], a["L0_attn_bo"])
        lattice(nc, ident, hres, xT_dram, wvo, a["L0_attn_Wq"], a["L0_attn_bq"], a["L0_attn_Wk"],
                a["L0_attn_bk"])
        x2 = ctx.enter_context(nc.sbuf_tensor("x2", [P, NT, D], F32))
        causal(nc, ident, hres, x2, a["wqk4"], a["wvT"], a["woT"], a["L0_ffn_ln1_w"], a["cosT"], a["sinT"])
        experts(nc, ident, hres, x2, a["routerT"], a["w1T"], a["w3T"], a["w2T"], a["L0_ffn_ln2_w"], out)


_INS = ["x", "L0_tok_turns", "L0_tok_poly_coeffs", "L0_attn_Wq", "L0_attn_bq", "L0_attn_Wk", "L0_attn_bk",
        "L0_attn_Wv", "L0_attn_bv", "L0_attn_Wo", "L0_attn_bo", "L0_ffn_ln1_w", "L0_ffn_ln2_w"]


def _laid_out(inputs):
    import numpy as _np

    def spread(w, heads, swap):
        o = _np.zeros((D, P), w.dtype)
        for h in range(NH):
            r = w[heads[h] * HD:(heads[h] + 1) * HD]
            if swap:
                r = _np.concatenate([r[HD // 2:], r[:HD // 2]])
            o[:, 32 * h:32 * h + HD] = r.T
        return o

    wq, wk = (_np.asarray(inputs["L0_ffn_" + n]) for n in ("wq", "wk"))
    qh, kh = list(range(NH)), [h // (NH // NKV) for h in range(NH)]
    inv_freq = 1.0 / 10000.0 ** (_np.arange(0, HD, 2, dtype=_np.float32) / HD)
    freqs = _np.outer(_np.arange(S, dtype=_np.float32), inv_freq)
    cos, sin = _np.zeros((P, S), _np.float32), _np.zeros((P, S), _np.float32)
    for h in range(NH):
        cos[32 * h:32 * h + HD] = _np.concatenate([_np.cos(freqs), _np.cos(freqs)], axis=-1).T
        sin[32 * h:32 * h + HD] = _np.concatenate([-_np.sin(freqs), _np.sin(freqs)], axis=-1).T
    hid = lambda n: _np.asarray(inputs["L0_ffn_" + n]).transpose(2, 0, 1).reshape(D, NE, 2, HC)
    return {
        "wqk4": _np.stack([spread(wq, qh, False), spread(wq, qh, True), spread(wk, kh, False),
                           spread(wk, kh, True)], axis=1),
        "wvT": _np.asarray(inputs["L0_ffn_wv"]).T, "woT": _np.asarray(inputs["L0_ffn_wo"]).T,
        "routerT": _np.asarray(inputs["L0_ffn_router_w"]).T, "w1T": hid("w1"), "w3T": hid("w3"),
        "w2T": _np.asarray(inputs["L0_ffn_w2"]).reshape(NE, D, 2, HC).transpose(3, 0, 2, 1),
        "cosT": cos, "sinT": sin,
    }


def kernel(**inputs):
    import numpy as _np
    import concourse.bacc as _bacc
    from concourse import mybir as _mybir
    from concourse.bass_utils import run_bass_kernel_spmd as _run

    nc = _bacc.Bacc("TRN2", target_bir_lowering=False, num_devices=1)
    arrays, aps = {}, {}
    given = {name: inputs[name] for name in _INS} | _laid_out(inputs)
    for name, a in given.items():
        a = _np.ascontiguousarray(a)
        arrays[f"in_{name}"] = a
        aps[name] = nc.dram_tensor(f"in_{name}", a.shape, _mybir.dt.from_np(a.dtype), kind="ExternalInput").ap()
    out = nc.dram_tensor("out", (B, S, D), _mybir.dt.float32, kind="ExternalOutput").ap()
    tower(nc, aps, out)
    r = _run(nc, [arrays], core_ids=[0])
    return r.results[0]["out"]
```

```python
import math
from contextlib import ExitStack

import concourse.bass as bass
from concourse import mybir

ALU = mybir.AluOpType
ACT = mybir.ActivationFunctionType
AX = mybir.AxisListType.X
F32 = mybir.dt.float32
BF16 = mybir.dt.bfloat16
I32 = mybir.dt.int32

P = 128
B, S, D = 8, 1024, 64
NT = B * S // P
TB = S // P
VOCAB, TURNS, DEGS = 50257, 4, 5
H = 8
NHEADS = B * H
PHI = (1.0 + math.sqrt(5.0)) / 2.0
C1 = PHI * math.sqrt(2.0) * 51.85
C2 = math.pi / PHI
ROUND = 1.5 * 2.0 ** 23
QSCALE = 1618.0 / (8.0 * 3.0)
EXPSCALE = 3.0 / (1618.0 * PHI * PHI)
TURN = C1 / (2.0 * math.pi)
EPS = 1e-5


def wait(eng, s, v):
    if not isinstance(v, int) or v > 0:
        eng.wait_ge(s, v)


def held(eng, s, v):
    if not isinstance(v, int) or v > 0:
        eng.wait_ge(s, v)
        eng.nop(nofuse=True)


def embed(nc, ident, hres, xT_dram, wvo, ids, turns, coeffs, Wv, bv, Wo, bo):
    with ExitStack() as ctx:
        def sb(name, shape, dt=F32):
            return ctx.enter_context(nc.sbuf_tensor(name, shape, dt))

        def sem(name):
            return ctx.enter_context(nc.semaphore(name))

        ids_i = sb("ids_i", [NT, P], I32)
        ids_f = sb("ids_f", [NT, P])
        idx = sb("idx", [P, NT], I32)
        base = sb("base", [P, NT, TURNS])
        mag = sb("mag", [P, NT, TURNS])
        sgn = sb("sgn", [P, NT, TURNS])
        rnd = sb("rnd", [P, NT, TURNS])
        over = sb("over", [P, NT, TURNS])
        pw = sb("pw", [P, NT, 32])
        pwT = sb("pwT", [P, 2, P])
        coef4 = sb("coef4", [P, 4 * D])
        wv1 = sb("wv1", [D + 1, H * D])
        wvT = sb("wvT", [D, H, D + 1])
        wo_h = sb("wo_h", [D, H, D])
        bo_all = sb("bo_all", [P, D])
        cen = sb("cen", [P, NT, D])
        sq = sb("sq", [P, NT, D])
        s1 = sb("s1", [P, NT])
        mean = sb("mean", [P, NT])
        s2 = sb("s2", [P, NT])
        var = sb("var", [P, NT])
        std = sb("std", [P, NT])
        rstd = sb("rstd", [P, NT])
        xn = sb("xn", [P, 2, TB, D])
        xT = sb("xT", [D, 2, S])

        ps_a = ctx.enter_context(nc.psum_tensor("ps_a", [P, 2, 512], F32))
        ps_e = ctx.enter_context(nc.psum_tensor("ps_e", [P, 2, 512], F32))
        ps_x = ctx.enter_context(nc.psum_tensor("ps_x", [P, 2, 1024], F32))

        ids_in, w_in, coef_in = sem("ids_in"), sem("w_in"), sem("coef_in")
        zeroed = sem("zeroed")
        idf, idT, idx_ok, got = sem("idf"), sem("idT"), sem("idx_ok"), sem("got")
        magn, trunc, pows = sem("magn"), sem("trunc"), sem("pows")
        pT, pT_sb, emb, emb_sb = sem("pT"), sem("pT_sb"), sem("emb"), sem("emb_sb")
        wT, wT_sb, wm, wm_sb = sem("wT"), sem("wT_sb"), sem("wm"), sem("wm_sb")
        ln, sqd, rooted, normed, nT, nT_sb = (sem(n) for n in
            ("ln", "sqd", "rooted", "normed", "nT", "nT_sb"))
        nT_out = [sem("nT_out0"), sem("nT_out1")]

        block = ctx.enter_context(nc.Block())

        @block.sync
        def _(sp):
            sp.dma_start(ids_i[:], ids.rearrange("b (t p) -> (b t) p", p=P)).then_inc(ids_in, 16)
            sp.dma_start(wv1[0:D, :], Wv).then_inc(w_in, 16)
            sp.dma_start(wv1[D:D + 1, :], bv.rearrange("(a n) -> a n", a=1)).then_inc(w_in, 16)
            sp.dma_start(wo_h[:], Wo.rearrange("(h d) o -> d h o", d=D)).then_inc(w_in, 16)
            sp.dma_start(bo_all[:], bo.partition_broadcast(P)).then_inc(w_in, 16)
            sp.wait_ge(zeroed, 2)
            for j in range(4):
                sp.dma_start(coef4[32 * j:32 * j + TURNS * DEGS, j * D:(j + 1) * D],
                             coeffs.rearrange("t d o -> (t d) o")).then_inc(coef_in, 16)
            for b in range(B):
                sp.wait_ge(nT_sb, b + 1)
                sp.dma_start(xT_dram[:, b * S:(b + 1) * S], xT[:, b % 2, :]).then_inc(nT_out[b % 2], 16)
            for n in nT_out:
                sp.wait_ge(n, 16 * B // 2)

        @block.gpsimd
        def _(pool):
            nc.gpsimd.memset(coef4[:], 0.0).then_inc(zeroed, 1)
            nc.gpsimd.memset(pw[:], 0.0).then_inc(zeroed, 1)
            pool.wait_ge(idx_ok, 1)
            for t in range(NT):
                nc.gpsimd.indirect_dma_start(
                    out=base[:, t, :], out_offset=None, in_=turns[:, :],
                    in_offset=bass.IndirectOffsetOnAxis(ap=idx[:, t:t + 1], axis=0)).then_inc(got, 16)

        @block.scalar
        def _(act):
            act.wait_ge(got, 16 * NT)
            nc.scalar.activation(mag[:], base[:], ACT.Abs).then_inc(magn, 1)
            nc.scalar.activation(sgn[:], base[:], ACT.Sign).then_inc(magn, 1)
            for g in range(NT // 4):
                act.wait_ge(pT, g + 1)
                if g >= 2:
                    act.wait_ge(emb, g - 1)
                nc.scalar.activation(pwT[:, g % 2, :], ps_a[:, g % 2, 0:P], ACT.Copy).then_inc(pT_sb, 1)
            act.wait_ge(wT, 1)
            nc.scalar.activation(wvT[:, 0:4, :], ps_x[0:D, 0, 0:4 * (D + 1)].rearrange("p (h c) -> p h c", h=4),
                                 ACT.Copy).then_inc(wT_sb, 1)
            nc.scalar.activation(wvT[:, 4:8, :], ps_x[0:D, 1, 0:4 * (D + 1)].rearrange("p (h c) -> p h c", h=4),
                                 ACT.Copy).then_inc(wT_sb, 1)
            act.wait_ge(wm, 1)
            nc.scalar.activation(wvo[:], ps_a[0:D + 1, 0, :], ACT.Copy).then_inc(wm_sb, 1)
            act.wait_ge(ln, 3)
            nc.scalar.activation(sq[:], cen[:], ACT.Square).then_inc(sqd, 1)
            act.wait_ge(ln, 5)
            nc.scalar.activation(std[:], var[:], ACT.Sqrt).then_inc(rooted, 1)
            for b in range(B):
                act.wait_ge(nT, b + 1)
                if b >= 2:
                    act.wait_ge(nT_out[b % 2], 16 * (b // 2))
                nc.scalar.activation(xT[:, b % 2, :], ps_x[0:D, b % 2, :], ACT.Copy).then_inc(nT_sb, 1)

        @block.vector
        def _(dve):
            dve.wait_ge(ids_in, 16)
            nc.vector.tensor_copy(ids_f[:], ids_i[:]).then_inc(idf, 1)
            dve.wait_ge(idT, 1)
            nc.vector.tensor_copy(idx[:], ps_a[:, 0, 0:NT]).then_inc(idx_ok, 1)
            dve.wait_ge(magn, 2)
            nc.vector.tensor_scalar(rnd[:], mag[:], ROUND, -ROUND, ALU.add, ALU.add).then_inc(trunc, 1)
            dve.wait_ge(trunc, 1)
            nc.vector.tensor_tensor(over[:], rnd[:], mag[:], ALU.is_gt).then_inc(trunc, 1)
            dve.wait_ge(trunc, 2)
            nc.vector.tensor_tensor(rnd[:], rnd[:], over[:], ALU.subtract).then_inc(trunc, 1)
            dve.wait_ge(trunc, 3)
            dve.wait_ge(zeroed, 2)
            pv = pw[:, :, 0:TURNS * DEGS].rearrange("p n (t d) -> p n t d", d=DEGS)
            nc.vector.memset(pv[:, :, :, 0], 1.0).then_inc(pows, 1)
            nc.vector.tensor_tensor(pv[:, :, :, 1], rnd[:], sgn[:], ALU.mult).then_inc(pows, 1)
            dve.wait_ge(pows, 2)
            for d in range(2, DEGS):
                nc.vector.tensor_tensor(pv[:, :, :, d], pv[:, :, :, d - 1], pv[:, :, :, 1], ALU.mult).then_inc(pows, 1)
                dve.wait_ge(pows, d + 1)
            for e in range(NT // 8):
                dve.wait_ge(emb, 2 * e + 2)
                nc.vector.tensor_copy(hres[:, 8 * e:8 * e + 8, :],
                                      ps_e[:, e % 2, :].rearrange("p (t d) -> p t d", d=D)).then_inc(emb_sb, 1)
            dve.wait_ge(emb_sb, NT // 8)
            nc.vector.tensor_reduce(s1[:], hres[:], AX, ALU.add).then_inc(ln, 1)
            dve.wait_ge(ln, 1)
            nc.vector.tensor_scalar(mean[:], s1[:], 1.0 / D, None, ALU.mult).then_inc(ln, 1)
            dve.wait_ge(ln, 2)
            nc.vector.tensor_tensor(cen[:], hres[:], mean[:].unsqueeze(2).to_broadcast([P, NT, D]),
                                    ALU.subtract).then_inc(ln, 1)
            dve.wait_ge(w_in, 64)
            nc.vector.tensor_tensor(hres[:], hres[:], bo_all[:].unsqueeze(1).to_broadcast([P, NT, D]),
                                    ALU.add)
            dve.wait_ge(sqd, 1)
            nc.vector.tensor_reduce(s2[:], sq[:], AX, ALU.add).then_inc(ln, 1)
            dve.wait_ge(ln, 4)
            nc.vector.tensor_scalar(var[:], s2[:], 1.0 / D, EPS, ALU.mult, ALU.add).then_inc(ln, 1)
            dve.wait_ge(rooted, 1)
            nc.vector.reciprocal(rstd[:], std[:]).then_inc(ln, 1)
            dve.wait_ge(ln, 6)
            for b in range(B):
                if b >= 2:
                    dve.wait_ge(nT, b - 1)
                nc.vector.tensor_tensor(xn[:, b % 2], cen[:, TB * b:TB * b + TB, :],
                                        rstd[:, TB * b:TB * b + TB].unsqueeze(2).to_broadcast([P, TB, D]),
                                        ALU.mult).then_inc(normed, 1)

        @block.tensor
        def _(pe):
            pe.wait_ge(idf, 1)
            nc.tensor.transpose(ps_a[:, 0, 0:NT], ids_f[:], ident[0:NT, 0:NT]).then_inc(idT, 1)
            pe.wait_ge(w_in, 64)
            for h in range(H):
                mm = nc.tensor.transpose(ps_x[0:D, h // 4, (h % 4) * (D + 1):(h % 4 + 1) * (D + 1)],
                                         wv1[:, h * D:(h + 1) * D], ident[0:D + 1, 0:D + 1])
            mm.then_inc(wT, 1)
            pe.wait_ge(coef_in, 64)
            pe.wait_ge(pows, DEGS)
            pe.wait_ge(idx_ok, 1)
            for g in range(NT // 4):
                if g >= 2:
                    pe.wait_ge(pT_sb, g - 1)
                nc.tensor.transpose(ps_a[:, g % 2, 0:P], pw[:, 4 * g:4 * g + 4, :].rearrange("p t c -> p (t c)"),
                                    ident[:]).then_inc(pT, 1)
                pe.wait_ge(pT_sb, g + 1)
                if g >= 4:
                    pe.wait_ge(emb_sb, g // 2 - 1)
                o = (g % 2) * 4 * D
                nc.tensor.matmul(ps_e[:, (g // 2) % 2, o:o + 4 * D], pwT[:, g % 2, :], coef4[:],
                                 start=True, stop=True).then_inc(emb, 1)
            pe.wait_ge(wT_sb, 2)
            for h in range(H):
                mm = nc.tensor.matmul(ps_a[0:D + 1, 0, h * D:(h + 1) * D], wvT[:, h, :], wo_h[:, h, :],
                                      start=True, stop=True)
            mm.then_inc(wm, 1)
            for b in range(B):
                pe.wait_ge(normed, b + 1)
                if b >= 2:
                    pe.wait_ge(nT_sb, b - 1)
                for t in range(TB):
                    mm = nc.tensor.transpose(ps_x[0:D, b % 2, t * P:(t + 1) * P], xn[:, b % 2, t, :], ident[:])
                mm.then_inc(nT, 1)


def lattice(nc, ident, hres, xT_dram, wvo, Wq, bq, Wk, bk):
    RING = 8
    with ExitStack() as ctx:
        def sb(name, shape, dt=F32):
            return ctx.enter_context(nc.sbuf_tensor(name, shape, dt))

        def sem(name):
            return ctx.enter_context(nc.semaphore(name))

        xq = sb("xq", [D + 1, S])
        xv = sb("xv", [D + 1, S])
        wqk = sb("wqk", [D + 1, P])
        qT = sb("qT", [P, 2, S])
        kT = sb("kT", [P, 2, S])
        vo = sb("vo", [P, TB, D])
        mag = sb("mag2", [P, 4, 512])
        wgt = sb("wgt", [P, 4, 512])
        att = sb("att", [P, 2, TB, S])
        nturn = sb("nturn", [P, TB, S], BF16)
        ag = sb("ag", [P, 2 * TB, 512])
        work = sb("work", [P, RING, 512])
        sinb = sb("sinb", [P, RING, 512])
        mx = sb("mx", [P, 2, 2 * TB])
        nb = sb("nb", [P, 2, TB])
        ssum = sb("ssum", [P, TB])
        rs = sb("rs", [P, TB])
        negI = sb("negI", [P, P], BF16)
        halfpi = sb("halfpi", [P, 1])

        banks = ctx.enter_context(nc.psum_tensor("banks", [P, 7, 512], F32))
        outp = ctx.enter_context(nc.psum_tensor("outp", [P, 512], F32))

        names = ("consts loadq loadv projd qk_sb vald v_sb qk mags halved rounded rest factor filtered bias expd "
                 "recip weights weights2 turned xpose squared gauss agd cosd acd nned sined tmul summed av outd").split()
        (consts, loadq, loadv, projd, qk_sb, vald, v_sb, qk, mags, halved, rounded, rest, factor, filtered, bias,
         expd, recip, weights, weights2, turned, xpose, squared, gauss, agd, cosd, acd, nned, sined, tmul, summed,
         av, outd) = (sem("l_" + n) for n in names)

        NTILE = 2 * TB
        NX = 2 * NTILE
        STEPS = 44
        SCORE = [5, 7, 9, 11] + list(range(12, 24))
        ABS, HALF, RND, REST, FILT = (1, 1, 2, 2, 3)
        PROJ, VAL = 18, 25 + STEPS
        EXP = STEPS + 3
        GAUSS = STEPS + 12
        SINE = STEPS + 28
        AV = [SINE + 6 + 8 * k // 5 for k in range(NTILE)]
        OUT = AV[-1] + 1
        EV = 2
        PACE = 2
        TURNS = EXP + 3
        DVE_ROWS = (TB // 2 - 1, TB - 1)

        block = ctx.enter_context(nc.Block())

        def over_heads(eng, iteration):
            iteration(0, 0)
            iteration(1, 1)
            with eng.Fori(1, NHEADS // 2 - 1) as i:
                iteration(2 * i, 0)
                iteration(2 * i + 1, 1)
            for t in range(NHEADS - 2, NHEADS + 2):
                iteration(t, t % 2)

        def stages(t, par, s):
            for stage in (2, 1, 0):
                g = t - stage
                if not isinstance(g, int) or 0 <= g < NHEADS:
                    yield g, (par - stage) % 2, s + STEPS * stage

        def score_bank(n):
            return banks[:, n % 4]

        def gauss_bank(d):
            return banks[:, 4 + d % 3]

        def sine_bank(k):
            return banks[:, 3 + k % 4]

        @block.sync
        def _(sp):
            def tokens(t):
                return xT_dram[:, bass.ds((t // H) * S, S)]

            def load_q(t):
                wait(sp, projd, 2 * t)
                h = t % H
                sp.dma_start(xq[0:D, :], tokens(t)).then_inc(loadq, 16)
                sp.dma_start(wqk[0:D, 0:D], Wq[:, bass.ds(h * D, D)]).then_inc(loadq, 16)
                sp.dma_start(wqk[0:D, D:P], Wk[:, bass.ds(h * D, D)]).then_inc(loadq, 16)
                sp.dma_start(wqk[D:D + 1, 0:D], bq.rearrange("(a n) -> a n", a=1)[:, bass.ds(h * D, D)]).then_inc(loadq, 16)
                sp.dma_start(wqk[D:D + 1, D:P], bk.rearrange("(a n) -> a n", a=1)[:, bass.ds(h * D, D)]).then_inc(loadq, 16)

            def load_v(t):
                wait(sp, vald, t)
                sp.dma_start(xv[0:D, :], tokens(t)).then_inc(loadv, 16)

            load_q(0)
            load_q(1)
            load_v(0)
            with sp.Fori(2, NHEADS) as t:
                load_q(t)
                load_v(t - 1)
            load_v(NHEADS - 1)

        @block.gpsimd
        def _(pool):
            nc.gpsimd.memset(xq[D:D + 1, :], 1.0).then_inc(consts, 1)
            pool.wait_ge(consts, 1)
            nc.gpsimd.memset(xv[D:D + 1, :], 1.0).then_inc(consts, 1)
            pool.wait_ge(consts, 2)
            nc.gpsimd.memset(negI[:], 0.0).then_inc(consts, 1)
            pool.wait_ge(consts, 3)
            nc.gpsimd.affine_select(out=negI[:], in_=negI[:], compare_op=ALU.not_equal, fill=-1.0,
                                    base=0, pattern=[[-1, P]], channel_multiplier=1).then_inc(consts, 1)
            nc.gpsimd.memset(halfpi[:], math.pi / 2).then_inc(consts, 1)
            pool.wait_ge(consts, 5)
            nc.gpsimd.memset(qT[D:P], 0.0).then_inc(consts, 1)
            pool.wait_ge(consts, 6)
            nc.gpsimd.memset(kT[D:P], 0.0).then_inc(consts, 1)

            def iteration(t, par):
                for s in range(STEPS):
                    for g, p, a in stages(t, par, s):
                        k = a - SINE - 5
                        if 0 <= k < NTILE:
                            wait(pool, tmul, NTILE * g + k + 1)
                            nc.gpsimd.tensor_tensor(sinb[:, k % RING], sinb[:, k % RING], work[:, k % RING],
                                                    ALU.add).then_inc(summed, 1)
                        j = a - EXP - 1
                        if 0 <= j < TB and j not in DVE_ROWS:
                            held(pool, recip, TB * g + j + 1)
                            nc.gpsimd.tensor_scalar(att[:, p, j], att[:, p, j], rs[:, j:j + 1], TURN,
                                                    ALU.mult, ALU.mult).then_inc(weights, 1)
                        if a - HALF in SCORE:
                            n = SCORE.index(a - HALF)
                            held(pool, mags, NTILE * g + n + 1)
                            nc.gpsimd.tensor_scalar(mag[:, n % 4], mag[:, n % 4], 1.0, -0.5,
                                                    ALU.mult, ALU.add).then_inc(halved, 1)
                        if a - REST in SCORE:
                            n = SCORE.index(a - REST)
                            wait(pool, rounded, NTILE * g + n + 1)
                            nc.gpsimd.tensor_tensor(wgt[:, n % 4], mag[:, n % 4], wgt[:, n % 4],
                                                    ALU.subtract).then_inc(rest, 1)

            over_heads(pool, iteration)

        @block.scalar
        def _(act):
            act.wait_ge(consts, 7)

            def projections(g, p, c):
                wait(act, projd, 2 * g + c + 1)
                if c == 0:
                    wait(act, qk, NTILE * (g - 1))
                cols = slice(c * 512, (c + 1) * 512)
                nc.scalar.activation(qT[0:D, p, cols], outp[0:D], ACT.Copy, scale=QSCALE).then_inc(qk_sb, 1)
                nc.scalar.activation(kT[0:D, p, cols], outp[D:P], ACT.Copy).then_inc(qk_sb, 1)

            projections(0, 0, 0)
            projections(0, 0, 1)

            def iteration(t, par):
                for s in range(STEPS):
                    for c in range(2):
                        if s == PROJ + EV + 2 * c and (not isinstance(t, int) or t + 1 < NHEADS):
                            projections(t + 1, 1 - par, c)
                    for g, p, a in stages(t, par, s):
                        if a == VAL + EV:
                            wait(act, vald, g + 1)
                            wait(act, av, NTILE * g)
                            nc.scalar.activation(vo[:], outp[:].rearrange("p (t d) -> p t d", d=D),
                                                 ACT.Copy, scale=1.0 / TURN).then_inc(v_sb, 1)
                        j = a - EXP
                        if 0 <= j < TB:
                            wait(act, bias, TB * g + j + 1)
                            nc.scalar.activation(att[:, p, j], att[:, p, j], ACT.Exp,
                                                 bias=nb[:, p, j:j + 1], scale=EXPSCALE,
                                                 accum_out=ssum[:, j:j + 1]).then_inc(expd, 1)
                        k = a - SINE - 1
                        if 0 <= k < NTILE:
                            wait(act, xpose, NX * g + NTILE + k + 1)
                            if k < RING:
                                wait(act, agd, NTILE * (g + 1) - RING + k + 1)
                            else:
                                wait(act, summed, NTILE * g + k - RING + 1)
                            nc.scalar.activation(work[:, k % RING], sine_bank(k), ACT.Sin,
                                                 bias=halfpi[:, 0:1], scale=-C2 / TURN).then_inc(cosd, 1)
                        k = a - SINE - 3
                        if 0 <= k < NTILE:
                            wait(act, nned, NTILE * g + k + 1)
                            wait(act, av, NTILE * g + k - RING + 1)
                            nc.scalar.activation(sinb[:, k % RING], sine_bank(k), ACT.Sin,
                                                 scale=2.0 * math.pi * (1.0 - 2.0 ** -22)).then_inc(sined, 1)
                    for g, p, a in stages(t, par, s):
                        d = a - GAUSS - 1
                        if 0 <= d < NTILE:
                            wait(act, xpose, NX * g + d + 1)
                            if d < RING:
                                wait(act, summed, NTILE * g - RING + d + 1)
                            else:
                                wait(act, agd, NTILE * g + d - RING + 1)
                            nc.scalar.activation(work[:, d % RING], gauss_bank(d), ACT.Square,
                                                 scale=1.0 / TURN).then_inc(squared, 1)
                    for g, p, a in stages(t, par, s):
                        if a - ABS in SCORE:
                            n = SCORE.index(a - ABS)
                            wait(act, qk, NTILE * g + n + 1)
                            wait(act, rest, NTILE * g + n - 3)
                            nc.scalar.activation(mag[:, n % 4], score_bank(n), ACT.Abs).then_inc(mags, 1)
                    for g, p, a in stages(t, par, s):
                        d = a - GAUSS - 1
                        if 0 <= d < NTILE:
                            wait(act, squared, NTILE * g + d + 1)
                            nc.scalar.activation(work[:, d % RING], work[:, d % RING], ACT.Exp,
                                                 scale=-1.0 / PHI).then_inc(gauss, 1)

            over_heads(act, iteration)

        @block.vector
        def _(dve):
            def iteration(t, par):
                for s in range(STEPS):
                    for g, p, a in stages(t, par, s):
                        k = a - SINE - 2
                        if 0 <= k < NTILE:
                            wait(dve, cosd, NTILE * g + k + 1)
                            nc.vector.tensor_tensor(work[:, k % RING], sine_bank(k), work[:, k % RING],
                                                    ALU.mult).then_inc(acd, 1)
                        k = a - SINE - 4
                        if 0 <= k < NTILE:
                            wait(dve, sined, NTILE * g + k + 1)
                            nc.vector.tensor_tensor(sinb[:, k % RING], sinb[:, k % RING], ag[:, k],
                                                    ALU.mult).then_inc(tmul, 1)
                        if a == OUT:
                            wait(dve, av, NTILE * (g + 1))
                            hv = hres[:, bass.ds((g // H) * TB, TB), :]
                            nc.vector.tensor_tensor(hv, outp[:].rearrange("p (t d) -> p t d", d=D), hv,
                                                    ALU.add).then_inc(outd, 1)
                        j = a - EXP - 1
                        if 0 <= j < TB:
                            wait(dve, expd, TB * g + j + 1)
                            nc.vector.reciprocal(rs[:, j:j + 1], ssum[:, j:j + 1]).then_inc(recip, 1)
                        if a - RND in SCORE:
                            n = SCORE.index(a - RND)
                            wait(dve, halved, NTILE * g + n + 1)
                            nc.vector.tensor_scalar(wgt[:, n % 4], mag[:, n % 4], ROUND, -ROUND,
                                                    ALU.add, ALU.add).then_inc(rounded, 1)
                        if a - FILT in SCORE:
                            n = SCORE.index(a - FILT)
                            wait(dve, rest, NTILE * g + n + 1)
                            nc.vector.tensor_scalar(wgt[:, n % 4], wgt[:, n % 4], 1.0 / 3.0 - 0.5, PHI,
                                                    ALU.is_ge, ALU.add).then_inc(factor, 1)
                    for g, p, a in stages(t, par, s):
                        d = a - GAUSS - 2
                        if 0 <= d < NTILE:
                            wait(dve, gauss, NTILE * g + d + 1)
                            nc.vector.tensor_tensor(ag[:, d], gauss_bank(d), work[:, d % RING],
                                                    ALU.mult).then_inc(agd, 1)
                        j = a - EXP - 1
                        if j in DVE_ROWS:
                            wait(dve, recip, TB * g + j + 1)
                            nc.vector.tensor_scalar(att[:, p, j], att[:, p, j], rs[:, j:j + 1], TURN,
                                                    ALU.mult, ALU.mult).then_inc(weights2, 1)
                        j = a - TURNS
                        if 0 <= j < TB:
                            if j in DVE_ROWS:
                                wait(dve, weights2, 2 * g + j // 4 + 1)
                            else:
                                wait(dve, weights, (TB - 2) * g + j + 1 - j // 4)
                            wait(dve, nned, NTILE * g)
                            nc.vector.tensor_scalar(nturn[:, j], att[:, p, j], ROUND, -ROUND,
                                                    ALU.add, ALU.add).then_inc(turned, 1)
                    for g, p, a in stages(t, par, s):
                        if a - FILT in SCORE:
                            n = SCORE.index(a - FILT)
                            u, c = n // 2, n % 2
                            wait(dve, factor, NTILE * g + n + 1)
                            wait(dve, filtered, NTILE * g + n)
                            wait(dve, xpose, NX * (g - 1))
                            dve.nop(nofuse=True)
                            nc.vector.tensor_tensor_reduce(
                                att[:, p, u, c * 512:(c + 1) * 512], wgt[:, n % 4], score_bank(n), 1.0,
                                mx[:, p, n - 1:n] if c else -3.0e38, ALU.mult, ALU.max,
                                mx[:, p, n:n + 1]).then_inc(filtered, 1)
                        if a - FILT - 1 in SCORE and SCORE.index(a - FILT - 1) % 2 == 1:
                            n = SCORE.index(a - FILT - 1)
                            u = n // 2
                            wait(dve, filtered, NTILE * g + n + 1)
                            nc.vector.tensor_scalar(nb[:, p, u:u + 1], mx[:, p, n:n + 1], -EXPSCALE, None,
                                                    ALU.mult).then_inc(bias, 1)

            over_heads(dve, iteration)

        @block.tensor
        def _(pe):
            pe.wait_ge(consts, 7)

            def project(g, c):
                wait(pe, loadq, 80 * (g + 1))
                if c == 0:
                    wait(pe, outd, g - 2)
                else:
                    wait(pe, qk_sb, 4 * g + 2)
                nc.tensor.matmul(outp[:], wqk[:], xq[:, c * 512:(c + 1) * 512], start=True, stop=True).then_inc(projd, 1)

            project(0, 0)
            project(0, 1)

            def fill(g, p, bank, kt, half):
                wait(pe, weights, (TB - 2) * g + (TB // 2 - 1) * (half + 1))
                wait(pe, weights2, 2 * g + half + 1)
                for i in range(4):
                    mm = nc.tensor.matmul(bank[:, i * P:(i + 1) * P],
                                          att[:, p, 4 * half + i, kt * P:(kt + 1) * P], ident[:],
                                          is_transpose=True, start=(i == 0), stop=(i == 3), skip_group_check=True)
                mm.then_inc(xpose, 1)

            def iteration(t, par):
                for s in range(STEPS):
                    for g, p, a in stages(t, par, s):
                        k = a - SINE - 3
                        if 0 <= k < NTILE:
                            wait(pe, acd, NTILE * g + k + 1)
                            wait(pe, turned, TB * (g + 1))
                            kt, half = k // 2, k % 2
                            for i in range(4):
                                mm = nc.tensor.matmul(sine_bank(k)[:, i * P:(i + 1) * P],
                                                      nturn[:, 4 * half + i, kt * P:(kt + 1) * P], negI[:],
                                                      start=False, stop=True, skip_group_check=True)
                            mm.then_inc(nned, 1)
                        if a in SCORE:
                            n = SCORE.index(a)
                            if n < 2:
                                wait(pe, qk_sb, 4 * (g + 1))
                            wait(pe, filtered, NTILE * g + n - 3)
                            if n == 3:
                                wait(pe, sined, NTILE * (g - 2) + 13)
                            nc.tensor.matmul(score_bank(n), qT[:, p, (n // 2) * P:(n // 2 + 1) * P],
                                             kT[:, p, (n % 2) * 512:(n % 2 + 1) * 512],
                                             start=True, stop=True).then_inc(qk, 1)
                        j = a - EXP - PACE
                        if 0 <= j < TB:
                            wait(pe, expd, TB * g + j + 1)
                        d = a - GAUSS
                        if 0 <= d < NTILE:
                            if d < 3:
                                wait(pe, sined, NTILE * (g - 1) + 14 + d)
                            else:
                                wait(pe, agd, NTILE * g + d - 2)
                            fill(g, p, gauss_bank(d), d // 2, d % 2)
                        k = a - SINE
                        if 0 <= k < NTILE:
                            if k == 0:
                                last = isinstance(g, int) and g == NHEADS - 1
                                wait(pe, filtered, NTILE * (g + 1 if last else g + 2))
                            elif k < 4:
                                wait(pe, agd, NTILE * g + (16, 14, 15)[k - 1])
                            else:
                                wait(pe, sined, NTILE * g + k - 3)
                            fill(g, p, sine_bank(k), k // 2, k % 2)
                        if a in AV:
                            k = AV.index(a)
                            wait(pe, summed, NTILE * g + k + 1)
                            if k == 0:
                                wait(pe, v_sb, g + 1)
                            kt, half = k // 2, k % 2
                            for i in range(4):
                                o = (4 * half + i) * D
                                mm = nc.tensor.matmul(outp[:, o:o + D], sinb[:, k % RING, i * P:(i + 1) * P],
                                                      vo[:, kt, :], start=(k == 0 and i == 0),
                                                      stop=(k >= NTILE - 2), skip_group_check=True)
                            mm.then_inc(av, 1)
                        if a == VAL:
                            wait(pe, loadv, 16 * (g + 1))
                            last = isinstance(g, int) and g + 2 >= NHEADS
                            wait(pe, qk_sb, 4 * NHEADS if last else 4 * (g + 3))
                            wait(pe, outd, g)
                            for j in range(TB):
                                mm = nc.tensor.matmul(outp[:, j * D:(j + 1) * D], xv[:, j * P:(j + 1) * P],
                                                      wvo[:, bass.ds((g % H) * D, D)], start=True, stop=True)
                            mm.then_inc(vald, 1)
                    for c in range(2):
                        if s == PROJ + 2 * c and (not isinstance(t, int) or t + 1 < NHEADS):
                            project(t + 1, c)

            over_heads(pe, iteration)


NH, NKV, HD = 4, 2, 16
NE, HID = 8, 170
NC = -(-NE * HID // P)
PAIRS = [(e, j) for e in range(NE) for j in range(HID * e // P, (HID * (e + 1) - 1) // P + 1)]
LAG = 2
EPS_RMS = 1e-6


def causal(nc, ident, hres, x2, wqk4, wvT, woT, ln1, cosT, sinT):
    with ExitStack() as ctx:
        def sb(name, shape, dt=F32):
            return ctx.enter_context(nc.sbuf_tensor(name, shape, dt))

        UNITS = [(qt, h) for qt in range(TB) for h in range(NH)]
        NU = len(UNITS)

        sq = sb("c_sq", [P, NT, D])
        s1, mean, s2, var, std, rstd = (sb("c_" + n, [P, NT]) for n in ("s1", "mean", "s2", "var", "std", "rstd"))
        ms, rms, rinv = (sb("c_" + n, [P, NT]) for n in ("ms", "rms", "rinv"))
        lnw = sb("lnw1", [D, 1])
        wqk = sb("c_wqk", [D, 4, P])
        wv = sb("c_wv", [D, NKV * HD])
        wo = sb("c_wo", [D, D])
        cs = sb("c_cs", [P, S])
        sn = sb("c_sn", [P, S])
        mask = sb("c_mask", [P, P], BF16)
        one = sb("c_one", [P, P], BF16)
        xs = sb("c_xs", [P, TB, D])
        xsT = sb("c_xsT", [D, S])
        q_r = sb("c_q", [P, S])
        q_h = sb("c_qh", [P, 2, NH, S])
        k_r = sb("c_k", [P, 2, S])
        own = sb("c_own", [P, NH])
        q_s = sb("c_qs", [P, S])
        k_s = sb("c_ks", [P, S])
        v = sb("c_v", [P, 2, TB * NKV * HD])
        pr = sb("c_pr", [P, 4, S])
        prT = sb("c_prT", [P, 4, S])
        nm = sb("c_nm", [P, 2, NU])
        sm = sb("c_sm", [P, 2, NU])
        rs = sb("c_rs", [P, NU])
        y = sb("c_y", [P, TB, D])
        yT = sb("c_yT", [D, S])

        sc = ctx.enter_context(nc.psum_tensor("c_sc", [P, 2, S], F32))
        pt = ctx.enter_context(nc.psum_tensor("c_pt", [P, 3, 512], F32))
        yp = ctx.enter_context(nc.psum_tensor("c_yp", [P, 512], F32))

        names = ("w_in consts wmul ln sqd rooted scaled xT xT_sb proj cosd sind roped pt_done pt_sb sc_done vd v_sb "
                 "maxed expd yd summed spread recip ynorm wo_add").split()
        (w_in, consts, wmul, ln, sqd, rooted, scaled, xT, xT_sb, proj, cosd, sind, roped, pt_done, pt_sb, sc_done,
         vd, v_sb, maxed, expd, yd, summed, spread, recip, ynorm, wo_add) = (ctx.enter_context(nc.semaphore("c_" + n)) for n in names)

        TURN_AT, APPLY_AT = 2, 3
        NORM_AT = APPLY_AT
        YT_AT, WO_AT = APPLY_AT + 2, APPLY_AT + 4
        PIECES = {9: "x", 13: "p0", 15: "p1", 17: "p2", 19: "p3", 21: "v"}

        SEQUENCE = [x for n in range(NU) for x in [n] + ([PIECES[n]] if n in PIECES else [])]
        SLOT = {kind: i % 2 for i, kind in enumerate(PIECES.values())}
        assert all(SEQUENCE.index(kind) % 2 == s for kind, s in SLOT.items()) and len(SEQUENCE) % 2 == 0

        def score_slot(n):
            return SEQUENCE.index(n) % 2

        def parts(n):
            return UNITS[n][0] // 4 + 1

        def uses(first, last):
            o = []
            for n in range(NU if not last else APPLY_AT + 5):
                m = n - TURN_AT
                if (m >= 0 and not last) or (m < 0 and not first):
                    o += [("g", m, g) for g in range(parts(m % NU))]
                if n == YT_AT and not first:
                    o += [("y", 0), ("y", 1)]
                if n == WO_AT and not first:
                    o += [("w",)]
            return o

        RING = uses(False, False)
        FIRST, LAST = uses(True, False), uses(False, True)
        NR = len(RING)
        SHORT = NR - len(FIRST)
        assert NR % 3 == 0

        def use(b, what):
            if isinstance(b, int):
                return FIRST.index(what) + 1 if b == 0 else NR * b - SHORT + (LAST if b == B else RING).index(what) + 1
            return NR * b - SHORT + RING.index(what) + 1

        def bank(b, what):
            k = use(b, what) if isinstance(b, int) else RING.index(what) + 1 - SHORT
            return pt[:, k % 3]

        def turned(b, n, g=None):
            g = parts(n) - 1 if g is None else g
            over = n + TURN_AT >= NU
            return (b + 1, ("g", n - NU, g)) if over else (b, ("g", n, g))

        def at(b, n, lag):
            return (b, n - lag) if n >= lag else (b - 1, n - lag + NU)

        def steps(b):
            return APPLY_AT + 5 if isinstance(b, int) and b == B else NU

        def pieces(b):
            return not isinstance(b, int) or b + 1 < B

        def exists(b):
            return not isinstance(b, int) or 0 <= b < B

        def over_batches(eng, body):
            body(0, 0)
            with eng.Fori(1, B // 2) as i:
                body(2 * i - 1, 1)
                body(2 * i, 0)
            body(B - 1, (B - 1) % 2)
            body(B, B % 2)

        block = ctx.enter_context(nc.Block())

        @block.sync
        def _(sp):
            for dst, src in ((wqk[:], wqk4), (wv[:], wvT), (wo[:], woT), (cs[:], cosT), (sn[:], sinT),
                             (lnw[:], ln1.rearrange("(p a) -> p a", a=1))):
                sp.dma_start(dst, src).then_inc(w_in, 16)
            sp.wait_ge(w_in, 96)

        @block.gpsimd
        def _(pool):
            for tile, fill, n in ((mask, -1e30, 0), (one, 1.0, 2)):
                nc.gpsimd.memset(tile[:], 0.0).then_inc(consts, 1)
                pool.wait_ge(consts, n + 1)
                nc.gpsimd.affine_select(out=tile[:], in_=tile[:],
                                        compare_op=ALU.is_ge if tile is mask else ALU.not_equal, fill=fill,
                                        base=0, pattern=[[-1, P]], channel_multiplier=1).then_inc(consts, 1)

            nc.gpsimd.memset(own[:], 1.0).then_inc(consts, 1)
            for n, (base, sign) in enumerate(((0, 1), (31, -1))):
                pool.wait_ge(consts, 5 + n)
                nc.gpsimd.affine_select(out=own[:], in_=own[:], compare_op=ALU.is_ge, fill=0.0, base=base,
                                        pattern=[[-32 * sign, NH]], channel_multiplier=sign).then_inc(consts, 1)
            pool.wait_ge(consts, 7)

            def rope(b, par):
                held(pool, sind, 2 * b + 1)
                nc.gpsimd.tensor_tensor(q_r[:], q_r[:], q_s[:], ALU.add).then_inc(summed, 1)
                held(pool, summed, b + 1)
                for h in range(NH):
                    nc.gpsimd.tensor_scalar(q_h[:, par, h], q_r[:], own[:, h:h + 1], 1.0,
                                            ALU.mult, ALU.mult).then_inc(spread, 1)
                held(pool, sind, 2 * b + 2)
                nc.gpsimd.tensor_tensor(k_r[:, par], k_r[:, par], k_s[:], ALU.add).then_inc(roped, 1)

            rope(0, 0)

            def body(b, par):
                if exists(b - 1):
                    held(pool, pt_sb, use(b, ("w",)))
                    xv = x2[:, bass.ds((b - 1) * TB, TB), :]
                    hv = hres[:, bass.ds((b - 1) * TB, TB), :]
                    nc.gpsimd.tensor_tensor(hv, hv, xv, ALU.add).then_inc(wo_add, 1)
                if pieces(b):
                    rope(b + 1, 1 - par)
            over_batches(pool, body)

        @block.scalar
        def _(act):
            act.wait_ge(ln, 3)
            nc.scalar.activation(sq[:], x2[:], ACT.Square).then_inc(sqd, 1)
            act.wait_ge(ln, 5)
            nc.scalar.activation(std[:], var[:], ACT.Sqrt).then_inc(rooted, 1)
            act.wait_ge(ln, 7)
            nc.scalar.activation(sq[:], x2[:], ACT.Square).then_inc(sqd, 1)
            act.wait_ge(ln, 9)
            nc.scalar.activation(rms[:], ms[:], ACT.Sqrt).then_inc(rooted, 1)

            def tokens_out(b):
                wait(act, xT, b + 1)
                wait(act, proj, 4 * b)
                wait(act, vd, b)
                nc.scalar.activation(xsT[:], sc[0:D, SLOT["x"]], ACT.Copy).then_inc(xT_sb, 1)

            def values_out(b, par):
                wait(act, vd, b + 1)
                nc.scalar.activation(v[:, par], sc[:, SLOT["v"], 0:TB * NKV * HD], ACT.Copy).then_inc(v_sb, 1)

            tokens_out(0)
            values_out(0, 0)

            def body(b, par):
                for n in range(steps(b)):
                    if exists(b):
                        wait(act, maxed, NU * b + n + 1)
                        if n >= 4 or exists(b - 1):
                            wait(act, pt_done, use(*turned(*at(b, n, 4))))
                        w = (UNITS[n][0] + 1) * P
                        nc.scalar.activation(pr[:, n % 4, 0:w], sc[:, score_slot(n), 0:w], ACT.Exp,
                                             bias=nm[:, par, n:n + 1], scale=1.0,
                                             accum_out=sm[:, par, n:n + 1]).then_inc(expd, 1)
                    if pieces(b) and PIECES.get(n) == "x":
                        tokens_out(b + 1)
                    if pieces(b) and PIECES.get(n) == "v":
                        values_out(b + 1, 1 - par)
            over_batches(act, body)

        @block.vector
        def _(dve):
            dve.wait_ge(w_in, 96)
            nc.vector.tensor_scalar(wqk[:, 0:2], wqk[:, 0:2], lnw[:, 0:1], 1.0 / math.sqrt(HD),
                                    ALU.mult, ALU.mult).then_inc(wmul, 1)
            nc.vector.tensor_scalar(wqk[:, 2:4], wqk[:, 2:4], lnw[:, 0:1], None, ALU.mult).then_inc(wmul, 1)
            nc.vector.tensor_scalar(wv[:], wv[:], lnw[:, 0:1], None, ALU.mult).then_inc(wmul, 1)
            nc.vector.tensor_reduce(s1[:], hres[:], AX, ALU.add).then_inc(ln, 1)
            dve.wait_ge(ln, 1)
            nc.vector.tensor_scalar(mean[:], s1[:], 1.0 / D, None, ALU.mult).then_inc(ln, 1)
            dve.wait_ge(ln, 2)
            nc.vector.tensor_tensor(x2[:], hres[:], mean[:].unsqueeze(2).to_broadcast([P, NT, D]),
                                    ALU.subtract).then_inc(ln, 1)
            dve.wait_ge(sqd, 1)
            nc.vector.tensor_reduce(s2[:], sq[:], AX, ALU.add).then_inc(ln, 1)
            dve.wait_ge(ln, 4)
            nc.vector.tensor_scalar(var[:], s2[:], 1.0 / D, EPS, ALU.mult, ALU.add).then_inc(ln, 1)
            dve.wait_ge(rooted, 1)
            nc.vector.reciprocal(rstd[:], std[:]).then_inc(ln, 1)
            dve.wait_ge(ln, 6)
            nc.vector.tensor_tensor(x2[:], x2[:], rstd[:].unsqueeze(2).to_broadcast([P, NT, D]),
                                    ALU.mult).then_inc(ln, 1)
            dve.wait_ge(sqd, 2)
            nc.vector.tensor_reduce(s2[:], sq[:], AX, ALU.add).then_inc(ln, 1)
            dve.wait_ge(ln, 8)
            nc.vector.tensor_scalar(ms[:], s2[:], 1.0 / D, EPS_RMS, ALU.mult, ALU.add).then_inc(ln, 1)
            dve.wait_ge(rooted, 2)
            nc.vector.reciprocal(rinv[:], rms[:]).then_inc(ln, 1)
            dve.wait_ge(ln, 10)

            def scale_tokens(b):
                wait(dve, xT, b)
                nc.vector.tensor_tensor(xs[:], x2[:, bass.ds(b * TB, TB), :],
                                        rinv[:, bass.ds(b * TB, TB)].unsqueeze(2).to_broadcast([P, TB, D]),
                                        ALU.mult).then_inc(scaled, 1)

            def table(b, par, i):
                dst, tab, done = ((q_r[:], cs, cosd), (q_s[:], sn, sind), (k_r[:, par], cs, cosd),
                                  (k_s[:], sn, sind))[i]
                wait(dve, proj, 4 * b + i + 1)
                wait(dve, roped, b)
                nc.vector.tensor_tensor(dst, sc[:, SLOT["p%d" % i]], tab[:], ALU.mult).then_inc(done, 1)

            scale_tokens(0)
            for i in range(4):
                table(0, 0, i)

            def body(b, par):
                for n in range(steps(b)):
                    if exists(b):
                        wait(dve, sc_done, NU * b + n + 1)
                        nc.vector.tensor_reduce(nm[:, par, n:n + 1], sc[:, score_slot(n), 0:(UNITS[n][0] + 1) * P],
                                                AX, ALU.max, negate=True).then_inc(maxed, 1)
                    if pieces(b) and n + 1 in PIECES and PIECES[n + 1] == "x":
                        scale_tokens(b + 1)
                    if pieces(b) and PIECES.get(n, "")[:1] == "p":
                        table(b + 1, 1 - par, int(PIECES[n][1]))
                    tb, tn = at(b, n, TURN_AT)
                    if exists(tb):
                        for g in range(parts(tn)):
                            what = turned(tb, tn, g)
                            wid = min(UNITS[tn][0] + 1 - 4 * g, 4) * P
                            wait(dve, pt_done, use(*what))
                            wait(dve, yd, NU * tb + tn - 3)
                            nc.vector.tensor_copy(prT[:, tn % 4, g * 512:g * 512 + wid],
                                                  bank(*what)[:, 0:wid]).then_inc(pt_sb, 1)
                    if n == NORM_AT and exists(b - 1):
                        wait(dve, expd, NU * b)
                        nc.vector.reciprocal(rs[:], sm[:, 1 - par]).then_inc(recip, 1)
                        wait(dve, recip, b)
                        wait(dve, yd, NU * b)
                        nc.vector.tensor_tensor(y[:].rearrange("p t (h d) -> p (t h) d", d=HD),
                                                yp[:].rearrange("p (n d) -> p n d", d=HD),
                                                rs[:].unsqueeze(2).to_broadcast([P, NU, HD]),
                                                ALU.mult).then_inc(ynorm, 1)
                    if n == YT_AT and exists(b - 1):
                        for i in range(2):
                            wait(dve, pt_done, use(b, ("y", i)))
                            nc.vector.tensor_copy(yT[:, i * 512:(i + 1) * 512],
                                                  bank(b, ("y", i))[0:D]).then_inc(pt_sb, 1)
                    if n == WO_AT and exists(b - 1):
                        wait(dve, pt_done, use(b, ("w",)))
                        xv = x2[:, bass.ds((b - 1) * TB, TB), :]
                        nc.vector.tensor_tensor(xv, bank(b, ("w",)).rearrange("p (t d) -> p t d", d=D), xv,
                                                ALU.add).then_inc(pt_sb, 1)
            over_batches(dve, body)

        @block.tensor
        def _(pe):
            pe.wait_ge(wmul, 3)

            pe.wait_ge(consts, 7)

            def freed(b, item):
                if isinstance(item, int):
                    wait(pe, expd, NU * b + item + 1)
                else:
                    s, count = {"x": (xT_sb, b + 1), "p0": (cosd, 2 * b + 1), "p1": (sind, 2 * b + 1),
                                "p2": (cosd, 2 * b + 2), "p3": (sind, 2 * b + 2), "v": (v_sb, b + 1)}[item]
                    wait(pe, s, count)

            def piece(b, kind):
                if kind == "x":
                    wait(pe, scaled, b + 1)
                    pe.nop(nofuse=True)
                    for t in range(TB):
                        mm = nc.tensor.transpose(sc[0:D, SLOT["x"], t * P:(t + 1) * P], xs[:, t, :], ident[:])
                    mm.then_inc(xT, 1)
                elif kind == "v":
                    for t in range(TB):
                        mm = nc.tensor.matmul(sc[:, SLOT["v"], t * NKV * HD:(t + 1) * NKV * HD],
                                              xsT[:, t * P:(t + 1) * P], wv[:], start=True, stop=True)
                    mm.then_inc(vd, 1)
                else:
                    if kind == "p0":
                        wait(pe, xT_sb, b + 1)
                        pe.nop(nofuse=True)
                    for c in range(2):
                        mm = nc.tensor.matmul(sc[:, SLOT[kind], c * 512:(c + 1) * 512], wqk[:, int(kind[1])],
                                              xsT[:, c * 512:(c + 1) * 512], start=True, stop=True)
                    mm.then_inc(proj, 1)

            PREPARE = list(PIECES.values())
            for u, kind in enumerate(PREPARE):
                if u >= 2:
                    freed(0, PREPARE[u - 2])
                piece(0, kind)

            def body(b, par):
                last = {score_slot(n): (b - 1, n) for n in (NU - 2, NU - 1)}
                if isinstance(b, int) and b == 0:
                    last = {SLOT[kind]: (0, kind) for kind in ("p3", "v")}
                for n in range(steps(b)):
                    if exists(b):
                        if n == 0:
                            wait(pe, spread, NH * (b + 1))
                            wait(pe, roped, b + 1)
                        freed(*last[score_slot(n)])
                        pe.nop(nofuse=True)
                        qt, h = UNITS[n]
                        s = sc[:, score_slot(n)]
                        for c in range(0, (qt + 1) * P, 512):
                            e = min(c + 512, (qt + 1) * P)
                            nc.tensor.matmul(s[:, c:e], q_h[:, par, h, qt * P:(qt + 1) * P], k_r[:, par, c:e],
                                             start=True, stop=True, skip_group_check=True)
                        nc.tensor.matmul(s[:, qt * P:(qt + 1) * P], one[:], mask[:], start=False, stop=True,
                                         skip_group_check=True).then_inc(sc_done, 1)
                        last[score_slot(n)] = (b, n)
                    if n in PIECES and pieces(b):
                        freed(*last[SLOT[PIECES[n]]])
                        pe.nop(nofuse=True)
                        piece(b + 1, PIECES[n])
                        last[SLOT[PIECES[n]]] = (b + 1, PIECES[n])
                    tb, tn = at(b, n, TURN_AT)
                    if exists(tb):
                        wait(pe, expd, NU * tb + tn + 1)
                        for g in range(parts(tn)):
                            what = turned(tb, tn, g)
                            wait(pe, pt_sb, use(*what) - 3)
                            pe.nop(nofuse=True)
                            for i in range(min(UNITS[tn][0] + 1 - 4 * g, 4)):
                                mm = nc.tensor.transpose(bank(*what)[:, i * P:(i + 1) * P],
                                                         pr[:, tn % 4, (4 * g + i) * P:(4 * g + i + 1) * P], ident[:])
                            mm.then_inc(pt_done, 1)
                    if n == YT_AT and exists(b - 1):
                        for i in range(2):
                            wait(pe, pt_sb, use(b, ("y", i)) - 3)
                            wait(pe, ynorm, b)
                            pe.nop(nofuse=True)
                            for t in range(4):
                                mm = nc.tensor.transpose(bank(b, ("y", i))[0:D, t * P:(t + 1) * P],
                                                         y[:, 4 * i + t, :], ident[:])
                            mm.then_inc(pt_done, 1)
                    if n == WO_AT and exists(b - 1):
                        wait(pe, pt_sb, use(b, ("y", 1)))
                        pe.nop(nofuse=True)
                        for t in range(TB):
                            mm = nc.tensor.matmul(bank(b, ("w",))[:, t * D:(t + 1) * D], yT[:, t * P:(t + 1) * P],
                                                  wo[:], start=True, stop=True)
                        mm.then_inc(pt_done, 1)
                    ab, an = at(b, n, APPLY_AT)
                    if exists(ab):
                        wait(pe, pt_sb, use(*turned(ab, an)))
                        if an == 0:
                            wait(pe, v_sb, ab + 1)
                            wait(pe, ynorm, ab)
                        pe.nop(nofuse=True)
                        qt, h = UNITS[an]
                        vpar = par if n >= APPLY_AT else 1 - par
                        for kt in range(qt + 1):
                            col = kt * NKV * HD + h // (NH // NKV) * HD
                            mm = nc.tensor.matmul(yp[:, an * HD:(an + 1) * HD], prT[:, an % 4, kt * P:(kt + 1) * P],
                                                  v[:, vpar, col:col + HD], start=(kt == 0), stop=(kt == qt),
                                                  skip_group_check=True)
                        mm.then_inc(yd, 1)

            assert RING.index(("y", 1)) >= RING.index(("w",)) - 3
            over_batches(pe, body)


def experts(nc, ident, hres, x3, router, w1T, w3T, w2T, ln2, out):
    with ExitStack() as ctx:
        def sb(name, shape, dt=F32):
            return ctx.enter_context(nc.sbuf_tensor(name, shape, dt))

        sq = sb("e_sq", [P, NT, D])
        s2, ms, rms, rinv = (sb("e_" + n, [P, NT]) for n in ("s2", "ms", "rms", "rinv"))
        lnw = sb("lnw2", [P, 1])
        rt = sb("e_rt", [D, NE])
        w1 = sb("e_w1", [P, NC * P])
        w3 = sb("e_w3", [P, NC * P])
        wp = sb("e_wp", [P, 2, 3, NC * P], BF16)
        xp = sb("e_xp", [P, 2, 2, S], BF16)
        xparts = sb("e_xparts", [P, 2, S], BF16)
        xrest = sb("e_xrest", [P, S])
        w2 = sb("e_w2", [P, len(PAIRS), D])
        rank = sb("e_rank", [P, TB, NE])
        rank_i = sb("e_ranki", [P, TB, NE], I32)
        xs = sb("e_xs", [P, TB, 2, D])
        xT = sb("e_xT", [P, S])
        prob = sb("e_prob", [P, TB, NE])
        hot1 = sb("e_hot1", [P, TB, NE])
        hot2 = sb("e_hot2", [P, TB, NE])
        tmp = sb("e_tmp", [P, TB, NE])
        wts = sb("e_wts", [P, 2, TB, NE])
        c1, c2, c3, m1, m2 = (sb("e_" + n, [P, TB]) for n in ("c1", "c2", "c3", "m1", "m2"))
        sl = sb("e_sl", [P, 2, 512])
        hh = sb("e_hh", [P, NC, S])
        wout = sb("e_wout", [P, 2, TB, D])

        hp = ctx.enter_context(nc.psum_tensor("e_hp", [P, 3, 2, 512], F32))
        op = ctx.enter_context(nc.psum_tensor("e_op", [P, 2, 512], F32))

        names = ("w_in ranked wmul rm sqd rooted scaled xTd xT_sb logit routed lexp hpd silud hhd opd woutd added "
                 "out_dma wsplit xsplit").split()
        (w_in, ranked, wmul, rm, sqd, rooted, scaled, xTd, xT_sb, logit, routed, lexp, hpd, silud, hhd, opd, woutd,
         added, out_dma, wsplit, xsplit) = (ctx.enter_context(nc.semaphore("e_" + n)) for n in names)

        NU = 2 * NC
        NR = 22
        DOWN = [2 * ((HID * (e + 1) - 1) // P) + 1 + LAG for e in range(NE)]
        WEIGH = [n + 1 for n in DOWN]
        PIECES = {4: "x", 8: "l"}
        SEQUENCE = [x for n in range(NU) for x in [n] + ([PIECES[n]] if n in PIECES else [])]
        SLOT = {x: i % 3 for i, x in enumerate(SEQUENCE)}
        assert len(SEQUENCE) % 3 == 0

        def at(b, n, table):
            for e, m in enumerate(table):
                if m % NU == n:
                    yield (b - m // NU, e)

        def exists(b):
            return not isinstance(b, int) or 0 <= b < B

        def steps(b):
            return max(WEIGH) % NU + 1 if isinstance(b, int) and b == B else NU

        def pieces(b):
            return not isinstance(b, int) or b + 1 < B

        def over_batches(eng, body):
            body(0, 0)
            with eng.Fori(1, B // 2) as i:
                body(2 * i - 1, 1)
                body(2 * i, 0)
            body(B - 1, (B - 1) % 2)
            body(B, B % 2)

        block = ctx.enter_context(nc.Block())
        out_v = out.rearrange("b (t p) d -> b p t d", p=P)

        @block.sync
        def _(sp):
            for dst, src in ((rt[:], router), (w1[0:D], w1T), (w1[D:P], w1T), (w3[0:D], w3T), (w3[D:P], w3T), (w2[:], w2T),
                             (lnw[0:D], ln2.rearrange("(p a) -> p a", a=1)), (lnw[D:P], ln2.rearrange("(p a) -> p a", a=1))):
                sp.dma_start(dst, src).then_inc(w_in, 16)
            sp.wait_ge(w_in, 128)

            def store(b):
                wait(sp, added, NE * (b + 1))
                sp.dma_start(out_v[bass.ds(b, 1)].rearrange("a p t d -> (a p) t d"),
                             hres[:, bass.ds(b * TB, TB), :]).then_inc(out_dma, 16)
            store(0)
            with sp.Fori(1, B) as b:
                store(b)
            sp.wait_ge(out_dma, 16 * B)

        @block.gpsimd
        def _(pool):
            nc.gpsimd.iota(rank_i[:], pattern=[[0, TB], [-1, NE]], base=NE, channel_multiplier=0).then_inc(ranked, 1)

            def add(b):
                for e in range(NE):
                    held(pool, woutd, NE * b + e + 1)
                    held(pool, added, NE * b + e)
                    hv = hres[:, bass.ds(b * TB, TB), :]
                    nc.gpsimd.tensor_tensor(hv, hv, wout[:, e % 2], ALU.add).then_inc(added, 1)
            add(0)
            with pool.Fori(1, B) as b:
                add(b)

        @block.scalar
        def _(act):
            nc.scalar.activation(sq[:], x3[:], ACT.Square).then_inc(sqd, 1)
            act.wait_ge(rm, 2)
            nc.scalar.activation(rms[:], ms[:], ACT.Sqrt).then_inc(rooted, 1)

            def tokens_out(b, par):
                wait(act, xTd, b + 1)
                wait(act, logit, b)
                wait(act, xsplit, 5 * b)
                nc.scalar.activation(xT[:], hp[:, SLOT["x"]].rearrange("p a n -> p (a n)"),
                                     ACT.Copy).then_inc(xT_sb, 1)

            def exponentials(b):
                wait(act, routed, NR * b + 2)
                nc.scalar.activation(prob[:], prob[:], ACT.Exp).then_inc(lexp, 1)

            tokens_out(0, 0)
            exponentials(0)

            def body(b, par):
                for n in range(steps(b)):
                    if exists(b):
                        wait(act, hpd, NU * b + n + 1)
                        wait(act, hhd, NU * b + n - 1)
                        nc.scalar.activation(sl[:, n % 2], hp[:, SLOT[n], 0], ACT.Silu).then_inc(silud, 1)
                    if pieces(b) and PIECES.get(n) == "x":
                        tokens_out(b + 1, 1 - par)
                    if pieces(b) and PIECES.get(n - 2) == "l":
                        exponentials(b + 1)
            over_batches(act, body)

        @block.vector
        def _(dve):
            dve.wait_ge(w_in, 128)
            nc.vector.tensor_scalar(rt[:], rt[:], lnw[0:D, 0:1], None, ALU.mult).then_inc(wmul, 1)
            for t in (w1, w3):
                nc.vector.tensor_scalar(t[:], t[:], lnw[:, 0:1], None, ALU.mult).then_inc(wmul, 1)
            dve.wait_ge(wmul, 3)
            up, low = slice(0, D), slice(D, P)
            for i, w in enumerate((w1, w3)):
                nc.vector.tensor_copy(wp[:, i, 0], w[:]).then_inc(wsplit, 1)
                dve.wait_ge(wsplit, 6 * i + 1)
                nc.vector.tensor_tensor(w[:], w[:], wp[:, i, 0], ALU.subtract).then_inc(wsplit, 1)
                dve.wait_ge(wsplit, 6 * i + 2)
                nc.vector.tensor_copy(wp[:, i, 1], w[:]).then_inc(wsplit, 1)
                dve.wait_ge(wsplit, 6 * i + 3)
                nc.vector.tensor_tensor(w[:], w[:], wp[:, i, 1], ALU.subtract).then_inc(wsplit, 1)
                dve.wait_ge(wsplit, 6 * i + 4)
                nc.vector.tensor_copy(wp[low, i, 2], w[low]).then_inc(wsplit, 1)
                nc.vector.tensor_copy(wp[up, i, 2], wp[up, i, 0]).then_inc(wsplit, 1)
            dve.wait_ge(ranked, 1)
            nc.vector.tensor_copy(rank[:], rank_i[:]).then_inc(wmul, 1)
            dve.wait_ge(sqd, 1)
            nc.vector.tensor_reduce(s2[:], sq[:], AX, ALU.add).then_inc(rm, 1)
            dve.wait_ge(rm, 1)
            nc.vector.tensor_scalar(ms[:], s2[:], 1.0 / D, EPS_RMS, ALU.mult, ALU.add).then_inc(rm, 1)
            dve.wait_ge(rooted, 1)
            nc.vector.reciprocal(rinv[:], rms[:]).then_inc(rm, 1)
            dve.wait_ge(rm, 3)
            dve.wait_ge(wmul, 4)

            def scale_tokens(b):
                wait(dve, xTd, b)
                for twice in range(2):
                    nc.vector.tensor_tensor(xs[:, :, twice], x3[:, bass.ds(b * TB, TB), :],
                                            rinv[:, bass.ds(b * TB, TB)].unsqueeze(2).to_broadcast([P, TB, D]),
                                            ALU.mult).then_inc(scaled, 1)

            def split_tokens(b, par):
                def part(n, ins):
                    ins.then_inc(xsplit, 1)
                    wait(dve, xsplit, 5 * b + n)

                wait(dve, xT_sb, b + 1)
                part(1, nc.vector.tensor_copy(xparts[:, 0], xT[:]))
                part(2, nc.vector.tensor_tensor(xrest[:], xT[:], xparts[:, 0], ALU.subtract))
                part(3, nc.vector.tensor_copy(xparts[:, 1], xrest[:]))
                nc.vector.tensor_copy(xp[up, par, 0], xparts[up, 0])
                nc.vector.tensor_copy(xp[low, par, 0], xparts[low, 1])
                nc.vector.tensor_copy(xp[low, par, 1], xparts[low, 0]).then_inc(xsplit, 1)
                part(5, nc.vector.tensor_tensor(xp[up, par, 1], xrest[up], xparts[up, 1], ALU.subtract))

            V = nc.vector

            def wide(x):
                return x[:].unsqueeze(2).to_broadcast([P, TB, NE])

            def did(b, step, ins):
                ins.then_inc(routed, 1)
                wait(dve, routed, NR * b + step)

            def logits_in(b):
                lg = hp[:, SLOT["l"], 0, 0:TB * NE].rearrange("p (t e) -> p t e", e=NE)
                wait(dve, logit, b + 1)
                did(b, 1, V.tensor_reduce(c1[:], lg, AX, ALU.max))
                did(b, 2, V.tensor_tensor(prob[:], lg, wide(c1), ALU.subtract))

            def normalize(b):
                wait(dve, lexp, b + 1)
                did(b, 3, V.tensor_reduce(c2[:], prob[:], AX, ALU.add))
                did(b, 4, V.reciprocal(c3[:], c2[:]))
                did(b, 5, V.tensor_tensor(prob[:], prob[:], wide(c3), ALU.mult))

            def choose(b, first, m, hot, c):
                did(b, first, V.tensor_reduce(m[:], prob[:], AX, ALU.max))
                did(b, first + 1, V.tensor_tensor(tmp[:], prob[:], wide(m), ALU.is_equal))
                did(b, first + 2, V.tensor_tensor(tmp[:], tmp[:], rank[:], ALU.mult))
                did(b, first + 3, V.tensor_reduce(c[:], tmp[:], AX, ALU.max))
                did(b, first + 4, V.tensor_tensor(hot[:], tmp[:], wide(c), ALU.is_equal))

            def choose_first(b):
                choose(b, 6, m1, hot1, c1)
                did(b, 11, V.scalar_tensor_tensor(out=prob[:], in0=hot1[:], scalar=-4.0, in1=prob[:],
                                                  op0=ALU.mult, op1=ALU.add))

            def choose_second(b):
                choose(b, 12, m2, hot2, c2)

            def weights_of(b, par):
                did(b, 17, V.scalar_tensor_tensor(out=c3[:], in0=m1[:], scalar=1e-9, in1=m2[:], op0=ALU.add,
                                                  op1=ALU.add))
                did(b, 18, V.reciprocal(c1[:], c3[:]))
                V.tensor_tensor(m1[:], m1[:], c1[:], ALU.mult)
                did(b, 19, V.tensor_tensor(m2[:], m2[:], c1[:], ALU.mult))
                did(b, 20, V.tensor_tensor(hot1[:], hot1[:], wide(m1), ALU.mult))
                did(b, 21, V.tensor_tensor(hot2[:], hot2[:], wide(m2), ALU.mult))
                did(b, 22, V.tensor_tensor(wts[:, par], hot1[:], hot2[:], ALU.add))

            scale_tokens(0)
            split_tokens(0, 0)
            logits_in(0)
            normalize(0)
            choose_first(0)
            choose_second(0)
            weights_of(0, 0)

            def body(b, par):
                for n in range(steps(b)):
                    if exists(b):
                        wait(dve, silud, NU * b + n + 1)
                        wait(dve, opd, NE * (b - 1) + min((n // 2 * P + P - 1) // HID + 1, NE))
                        nc.vector.tensor_tensor(hh[:, n // 2, n % 2 * 512:(n % 2 + 1) * 512], hp[:, SLOT[n], 1],
                                                sl[:, n % 2], ALU.mult).then_inc(hhd, 1)
                    if pieces(b):
                        if n == 1:
                            scale_tokens(b + 1)
                        elif n == 6:
                            split_tokens(b + 1, 1 - par)
                        elif n == 9:
                            logits_in(b + 1)
                        elif n == 12:
                            normalize(b + 1)
                        elif n == 14:
                            choose_first(b + 1)
                        elif n == 16:
                            choose_second(b + 1)
                        elif n == 18:
                            weights_of(b + 1, 1 - par)
                    for eb, e in at(b, n, WEIGH):
                        if exists(eb):
                            wpar = par if WEIGH[e] < NU else 1 - par
                            wait(dve, opd, NE * eb + e + 1)
                            wait(dve, added, NE * eb + e - 1)
                            nc.vector.tensor_tensor(wout[:, e % 2], op[:, e % 2].rearrange("p (t d) -> p t d", d=D),
                                                    wts[:, wpar, :, e:e + 1].to_broadcast([P, TB, D]),
                                                    ALU.mult).then_inc(woutd, 1)
            over_batches(dve, body)

        @block.tensor
        def _(pe):
            pe.wait_ge(wmul, 3)
            pe.wait_ge(wsplit, 12)

            def freed(b, item):
                if item == "x":
                    wait(pe, xT_sb, b + 1)
                elif item == "l":
                    wait(pe, routed, NR * b + 2)
                else:
                    wait(pe, hhd, NU * b + item + 1)

            def piece(b, par, kind):
                if kind == "x":
                    wait(pe, scaled, 2 * (b + 1))
                    pe.nop(nofuse=True)
                    tv = hp[:, SLOT["x"]].rearrange("p a n -> p (a n)")
                    for t in range(TB):
                        mm = nc.tensor.transpose(tv[:, t * P:(t + 1) * P], xs[:, t].rearrange("p a d -> p (a d)"),
                                                 ident[:])
                    mm.then_inc(xTd, 1)
                else:
                    wait(pe, xT_sb, b + 1)
                    pe.nop(nofuse=True)
                    for t in range(TB):
                        mm = nc.tensor.matmul(hp[:, SLOT["l"], 0, t * NE:(t + 1) * NE],
                                              xT[0:D, t * P:(t + 1) * P], rt[:], start=True, stop=True)
                    mm.then_inc(logit, 1)

            piece(0, 0, "x")
            piece(0, 0, "l")

            def body(b, par):
                if isinstance(b, int) and b == 0:
                    last = {SLOT[kind]: (0, kind) for kind in PIECES.values()}
                else:
                    last = {SLOT[n]: (b - 1, n) for n in range(NU - 3, NU)}
                if exists(b):
                    wait(pe, xsplit, 5 * (b + 1))
                for n in range(steps(b)):
                    if exists(b):
                        if SLOT[n] in last:
                            freed(*last[SLOT[n]])
                        pe.nop(nofuse=True)
                        cols = slice(n % 2 * 512, (n % 2 + 1) * 512)
                        rows = slice(n // 2 * P, (n // 2 + 1) * P)
                        for w in range(2):
                            for i, j in ((0, 0), (1, 0), (2, 1)):
                                mm = nc.tensor.matmul(hp[:, SLOT[n], w], wp[:, w, i, rows], xp[:, par, j, cols],
                                                      start=(i == 0), stop=(i == 2))
                        mm.then_inc(hpd, 1)
                        last[SLOT[n]] = (b, n)
                    if n in PIECES and pieces(b):
                        freed(*last[SLOT[PIECES[n]]])
                        piece(b + 1, 1 - par, PIECES[n])
                        last[SLOT[PIECES[n]]] = (b + 1, PIECES[n])
                    for eb, e in at(b, n, DOWN):
                        if exists(eb):
                            wait(pe, hhd, NU * eb + DOWN[e] - LAG + 1)
                            wait(pe, woutd, NE * eb + e - 1)
                            pe.nop(nofuse=True)
                            mine = [(i, j) for i, (x, j) in enumerate(PAIRS) if x == e]
                            for t in range(TB):
                                for i, j in mine:
                                    mm = nc.tensor.matmul(op[:, e % 2, t * D:(t + 1) * D],
                                                          hh[:, j, t * P:(t + 1) * P], w2[:, i],
                                                          start=(i == mine[0][0]), stop=(i == mine[-1][0]))
                            mm.then_inc(opd, 1)
            over_batches(pe, body)


def tower(nc, a, out):
    with ExitStack() as ctx:
        ident = ctx.enter_context(nc.sbuf_tensor("ident", [P, P], F32))
        hres = ctx.enter_context(nc.sbuf_tensor("hres", [P, NT, D], F32))
        wvo = ctx.enter_context(nc.sbuf_tensor("wvo", [D + 1, H * D], F32))
        xT_dram = nc.dram_tensor("xT_dram", (D, B * S), F32, kind="Internal").ap()
        made = ctx.enter_context(nc.semaphore("made"))
        with nc.Block() as block:
            @block.gpsimd
            def _(pool):
                nc.gpsimd.memset(ident[:], 0.0).then_inc(made, 1)
                pool.wait_ge(made, 1)
                nc.gpsimd.affine_select(out=ident[:], in_=ident[:], compare_op=ALU.not_equal, fill=1.0,
                                        base=0, pattern=[[-1, P]], channel_multiplier=1).then_inc(made, 1)
                pool.wait_ge(made, 2)
        embed(nc, ident, hres, xT_dram, wvo, a["x"], a["L0_tok_turns"], a["L0_tok_poly_coeffs"],
              a["L0_attn_Wv"], a["L0_attn_bv"], a["L0_attn_Wo"], a["L0_attn_bo"])
        lattice(nc, ident, hres, xT_dram, wvo, a["L0_attn_Wq"], a["L0_attn_bq"], a["L0_attn_Wk"],
                a["L0_attn_bk"])
        x2 = ctx.enter_context(nc.sbuf_tensor("x2", [P, NT, D], F32))
        causal(nc, ident, hres, x2, a["wqk4"], a["wvT"], a["woT"], a["L0_ffn_ln1_w"], a["cosT"], a["sinT"])
        experts(nc, ident, hres, x2, a["routerT"], a["w1T"], a["w3T"], a["w2T"], a["L0_ffn_ln2_w"], out)


_INS = ["x", "L0_tok_turns", "L0_tok_poly_coeffs", "L0_attn_Wq", "L0_attn_bq", "L0_attn_Wk", "L0_attn_bk",
        "L0_attn_Wv", "L0_attn_bv", "L0_attn_Wo", "L0_attn_bo", "L0_ffn_ln1_w", "L0_ffn_ln2_w"]


def _laid_out(inputs):
    import numpy as _np

    def spread(w, heads, swap):
        o = _np.zeros((D, P), w.dtype)
        for h in range(NH):
            r = w[heads[h] * HD:(heads[h] + 1) * HD]
            if swap:
                r = _np.concatenate([r[HD // 2:], r[:HD // 2]])
            o[:, 32 * h:32 * h + HD] = r.T
        return o

    wq, wk = (_np.asarray(inputs["L0_ffn_" + n]) for n in ("wq", "wk"))
    qh, kh = list(range(NH)), [h // (NH // NKV) for h in range(NH)]
    inv_freq = 1.0 / 10000.0 ** (_np.arange(0, HD, 2, dtype=_np.float32) / HD)
    freqs = _np.outer(_np.arange(S, dtype=_np.float32), inv_freq)
    cos, sin = _np.zeros((P, S), _np.float32), _np.zeros((P, S), _np.float32)
    for h in range(NH):
        cos[32 * h:32 * h + HD] = _np.concatenate([_np.cos(freqs), _np.cos(freqs)], axis=-1).T
        sin[32 * h:32 * h + HD] = _np.concatenate([-_np.sin(freqs), _np.sin(freqs)], axis=-1).T

    def hid(n):
        w = _np.asarray(inputs["L0_ffn_" + n])
        o = _np.zeros((D, NC * P), w.dtype)
        o[:, :NE * HID] = w.transpose(2, 0, 1).reshape(D, NE * HID)
        return o

    w2 = _np.asarray(inputs["L0_ffn_w2"])
    w2T = _np.zeros((P, len(PAIRS), D), w2.dtype)
    for i, (e, j) in enumerate(PAIRS):
        lo, hi = max(HID * e, P * j), min(HID * (e + 1), P * (j + 1))
        w2T[lo - P * j:hi - P * j, i] = w2[e][:, lo - HID * e:hi - HID * e].T

    return {
        "wqk4": _np.stack([spread(wq, qh, False), spread(wq, qh, True), spread(wk, kh, False),
                           spread(wk, kh, True)], axis=1),
        "wvT": _np.asarray(inputs["L0_ffn_wv"]).T, "woT": _np.asarray(inputs["L0_ffn_wo"]).T,
        "routerT": _np.asarray(inputs["L0_ffn_router_w"]).T, "w1T": hid("w1"), "w3T": hid("w3"),
        "w2T": w2T,
        "cosT": cos, "sinT": sin,
    }


def kernel(**inputs):
    import numpy as _np
    import concourse.bacc as _bacc
    from concourse import mybir as _mybir
    from concourse.bass_utils import run_bass_kernel_spmd as _run

    nc = _bacc.Bacc("TRN2", target_bir_lowering=False, num_devices=1)
    arrays, aps = {}, {}
    given = {name: inputs[name] for name in _INS} | _laid_out(inputs)
    for name, a in given.items():
        a = _np.ascontiguousarray(a)
        arrays[f"in_{name}"] = a
        aps[name] = nc.dram_tensor(f"in_{name}", a.shape, _mybir.dt.from_np(a.dtype), kind="ExternalInput").ap()
    out = nc.dram_tensor("out", (B, S, D), _mybir.dt.float32, kind="ExternalOutput").ap()
    tower(nc, aps, out)
    r = _run(nc, [arrays], core_ids=[0])
    return r.results[0]["out"]
```
